# Optimizing a Trainium2 kernel written in Bass

```python
import numpy as np
import jax
import jax.numpy as jnp

def _softmax(x, axis=-1):
    return jax.nn.softmax(x, axis=axis)
def _gelu(x):
    return jax.nn.gelu(x, approximate=True)
def _silu(x):
    return jax.nn.silu(x)
def _sigmoid(x):
    return jax.nn.sigmoid(x)
def _layernorm(x, axis=-1, eps=1e-5):
    m = jnp.mean(x, axis=axis, keepdims=True)
    v = jnp.var(x, axis=axis, keepdims=True)
    return (x - m) / jnp.sqrt(v + eps)
def _scatter_add(tgt, idx, src, axis=0):
    return tgt.at[idx].add(src)
def _segment_sum(src, seg, n):
    return jax.ops.segment_sum(src, seg, n)

kernel_name = 'mk_dlrm_tower_d1_rec_dc6f37'

def setup_inputs(seed: int = 0):
    np.random.seed(seed)
    _w = jnp.asarray
    def _rec_inputs():
        import jax
        import jax.numpy as jnp
        _tk = jax.random.key(seed)
        ids = jnp.stack([jax.random.randint(jax.random.fold_in(_tk, 200 + f), (1024,), 0, v, jnp.int32) for f, v in enumerate([1000, 1000, 10000, 1000])], axis=1)
        tbl_0 = 0.05 * jax.random.normal(jax.random.fold_in(_tk, 500 + 0), (1000, 4), jnp.float32)
        tbl_1 = 0.05 * jax.random.normal(jax.random.fold_in(_tk, 500 + 1), (1000, 4), jnp.float32)
        tbl_2 = 0.05 * jax.random.normal(jax.random.fold_in(_tk, 500 + 2), (10000, 4), jnp.float32)
        tbl_3 = 0.05 * jax.random.normal(jax.random.fold_in(_tk, 500 + 3), (1000, 4), jnp.float32)
        _rk = jax.random.fold_in(_tk, 7)
        r_x = 7.22013e-05 + 1.00017 * jax.random.normal(jax.random.fold_in(_rk, 101), (1024, 2048), jnp.float32)
        W_top1 = 0.0197642 * jax.random.normal(jax.random.fold_in(_tk, 801), (2560, 512), jnp.float32)
        W_top2 = 0.0441942 * jax.random.normal(jax.random.fold_in(_tk, 802), (512, 256), jnp.float32)
        W_top3 = 0.0625 * jax.random.normal(jax.random.fold_in(_tk, 803), (256, 1), jnp.float32)
        b_top1 = jnp.zeros((512,), jnp.float32)
        b_top2 = jnp.zeros((256,), jnp.float32)
        return r_x, ids, tbl_0, tbl_1, tbl_2, tbl_3, W_top1, b_top1, W_top2, b_top2, W_top3
    r_x, ids, tbl_0, tbl_1, tbl_2, tbl_3, W_top1, b_top1, W_top2, b_top2, W_top3 = _rec_inputs()
    def _L0_rec_setup():
        import jax, jax.numpy as jnp
        import numpy as np
        B, IN, HID, D, N, OUT = (4096, 2048, 2048, 512, 4, 512)
        H = 8
        HD = D // H

        def _ln(x, g, b):
            m = x.mean(-1, keepdims=True)
            v = ((x - m) ** 2).mean(-1, keepdims=True)
            return (x - m) / jnp.sqrt(v + 1e-05) * g + b
        key = jax.random.key(seed)
        ks = jax.random.split(key, 32)

        def nrm(k, shape, scale=0.02):
            return jax.random.normal(k, shape, jnp.float32) * scale
        inp = {}
        inp['x'] = jax.random.normal(ks[0], (B, IN), jnp.float32)
        inp['strength'] = jax.random.uniform(ks[1], (B, N, N), jnp.float32)
        for t, i in (('er', 2), ('ei', 4)):
            inp[t + '_W1'] = nrm(ks[i], (HID, IN))
            inp[t + '_b1'] = jnp.zeros((HID,), jnp.float32)
            inp[t + '_g1'] = jnp.ones((HID,), jnp.float32)
            inp[t + '_be1'] = jnp.zeros((HID,), jnp.float32)
            inp[t + '_W2'] = nrm(ks[i + 1], (N * D, HID))
            inp[t + '_b2'] = jnp.zeros((N * D,), jnp.float32)
        names = ['Wq_r', 'Wq_i', 'Wk_r', 'Wk_i', 'Wv_r', 'Wv_i', 'Wo_r', 'Wo_i']
        for j, nm in enumerate(names):
            inp[nm] = nrm(ks[6 + j], (D, D))
            inp['b' + nm[1:]] = jnp.zeros((D,), jnp.float32)
        inp['int_Wr'] = jnp.tile(jnp.eye(D, dtype=jnp.float32)[None], (N, 1, 1))
        inp['int_Wi'] = jnp.zeros((N, D, D), jnp.float32)
        inp['meas_Mr'] = nrm(ks[20], (OUT, D), 1.0 / np.sqrt(D))
        inp['meas_Mi'] = nrm(ks[21], (OUT, D), 1.0 / np.sqrt(D))
        inp['post_W'] = nrm(ks[22], (OUT, OUT))
        inp['post_b'] = jnp.zeros((OUT,), jnp.float32)
        inp['post_g'] = jnp.ones((OUT,), jnp.float32)
        inp['post_be'] = jnp.zeros((OUT,), jnp.float32)
        return inp
    _L0_rec_all = _L0_rec_setup()
    _L0_rec_in = {k: v for k, v in _L0_rec_all.items() if k in ('er_W1', 'er_b1', 'er_g1', 'er_be1', 'er_W2', 'er_b2', 'ei_W1', 'ei_b1', 'ei_g1', 'ei_be1', 'ei_W2', 'ei_b2', 'Wq_r', 'bq_r', 'Wq_i', 'bq_i', 'Wk_r', 'bk_r', 'Wk_i', 'bk_i', 'Wv_r', 'bv_r', 'Wv_i', 'bv_i', 'Wo_r', 'bo_r', 'Wo_i', 'bo_i', 'int_Wr', 'int_Wi', 'meas_Mr', 'meas_Mi', 'post_W', 'post_b', 'post_g', 'post_be', )}
    del _L0_rec_all

    return {
        "r_x": r_x,
        "ids": ids,
        "tbl_0": tbl_0,
        "tbl_1": tbl_1,
        "tbl_2": tbl_2,
        "tbl_3": tbl_3,
        "W_top1": W_top1,
        "b_top1": b_top1,
        "W_top2": W_top2,
        "b_top2": b_top2,
        "W_top3": W_top3,
        "L0_rec_er_W1": _L0_rec_in["er_W1"],
        "L0_rec_er_b1": _L0_rec_in["er_b1"],
        "L0_rec_er_g1": _L0_rec_in["er_g1"],
        "L0_rec_er_be1": _L0_rec_in["er_be1"],
        "L0_rec_er_W2": _L0_rec_in["er_W2"],
        "L0_rec_er_b2": _L0_rec_in["er_b2"],
        "L0_rec_ei_W1": _L0_rec_in["ei_W1"],
        "L0_rec_ei_b1": _L0_rec_in["ei_b1"],
        "L0_rec_ei_g1": _L0_rec_in["ei_g1"],
        "L0_rec_ei_be1": _L0_rec_in["ei_be1"],
        "L0_rec_ei_W2": _L0_rec_in["ei_W2"],
        "L0_rec_ei_b2": _L0_rec_in["ei_b2"],
        "L0_rec_Wq_r": _L0_rec_in["Wq_r"],
        "L0_rec_bq_r": _L0_rec_in["bq_r"],
        "L0_rec_Wq_i": _L0_rec_in["Wq_i"],
        "L0_rec_bq_i": _L0_rec_in["bq_i"],
        "L0_rec_Wk_r": _L0_rec_in["Wk_r"],
        "L0_rec_bk_r": _L0_rec_in["bk_r"],
        "L0_rec_Wk_i": _L0_rec_in["Wk_i"],
        "L0_rec_bk_i": _L0_rec_in["bk_i"],
        "L0_rec_Wv_r": _L0_rec_in["Wv_r"],
        "L0_rec_bv_r": _L0_rec_in["bv_r"],
        "L0_rec_Wv_i": _L0_rec_in["Wv_i"],
        "L0_rec_bv_i": _L0_rec_in["bv_i"],
        "L0_rec_Wo_r": _L0_rec_in["Wo_r"],
        "L0_rec_bo_r": _L0_rec_in["bo_r"],
        "L0_rec_Wo_i": _L0_rec_in["Wo_i"],
        "L0_rec_bo_i": _L0_rec_in["bo_i"],
        "L0_rec_int_Wr": _L0_rec_in["int_Wr"],
        "L0_rec_int_Wi": _L0_rec_in["int_Wi"],
        "L0_rec_meas_Mr": _L0_rec_in["meas_Mr"],
        "L0_rec_meas_Mi": _L0_rec_in["meas_Mi"],
        "L0_rec_post_W": _L0_rec_in["post_W"],
        "L0_rec_post_b": _L0_rec_in["post_b"],
        "L0_rec_post_g": _L0_rec_in["post_g"],
        "L0_rec_post_be": _L0_rec_in["post_be"],
    }

def reference(r_x, ids, tbl_0, tbl_1, tbl_2, tbl_3, W_top1, b_top1, W_top2, b_top2, W_top3, L0_rec_er_W1, L0_rec_er_b1, L0_rec_er_g1, L0_rec_er_be1, L0_rec_er_W2, L0_rec_er_b2, L0_rec_ei_W1, L0_rec_ei_b1, L0_rec_ei_g1, L0_rec_ei_be1, L0_rec_ei_W2, L0_rec_ei_b2, L0_rec_Wq_r, L0_rec_bq_r, L0_rec_Wq_i, L0_rec_bq_i, L0_rec_Wk_r, L0_rec_bk_r, L0_rec_Wk_i, L0_rec_bk_i, L0_rec_Wv_r, L0_rec_bv_r, L0_rec_Wv_i, L0_rec_bv_i, L0_rec_Wo_r, L0_rec_bo_r, L0_rec_Wo_i, L0_rec_bo_i, L0_rec_int_Wr, L0_rec_int_Wi, L0_rec_meas_Mr, L0_rec_meas_Mi, L0_rec_post_W, L0_rec_post_b, L0_rec_post_g, L0_rec_post_be):
    import jax
    import jax.numpy as jnp
    def _L0_rec_ref(x, strength, er_W1, er_b1, er_g1, er_be1, er_W2, er_b2, ei_W1, ei_b1, ei_g1, ei_be1, ei_W2, ei_b2, Wq_r, bq_r, Wq_i, bq_i, Wk_r, bk_r, Wk_i, bk_i, Wv_r, bv_r, Wv_i, bv_i, Wo_r, bo_r, Wo_i, bo_i, int_Wr, int_Wi, meas_Mr, meas_Mi, post_W, post_b, post_g, post_be):
        import jax, jax.numpy as jnp
        import numpy as np
        B, IN, HID, D, N, OUT = (4096, 2048, 2048, 512, 4, 512)
        H = 8
        HD = D // H

        def _ln(x, g, b):
            m = x.mean(-1, keepdims=True)
            v = ((x - m) ** 2).mean(-1, keepdims=True)
            return (x - m) / jnp.sqrt(v + 1e-05) * g + b
        Bsz = x.shape[0]

        def enc(W1, b1, g, be, W2, b2):
            h = jax.nn.gelu(_ln(x @ W1.T + b1, g, be), approximate=False)
            return (h @ W2.T + b2).reshape(Bsz, N, D)
        sr = enc(er_W1, er_b1, er_g1, er_be1, er_W2, er_b2)
        si = enc(ei_W1, ei_b1, ei_g1, ei_be1, ei_W2, ei_b2)

        def heads(t):
            return t.reshape(Bsz, N, H, HD).transpose(0, 2, 1, 3)
        qr = heads(sr @ Wq_r.T + bq_r)
        qi = heads(si @ Wq_i.T + bq_i)
        kr = heads(sr @ Wk_r.T + bk_r)
        ki = heads(si @ Wk_i.T + bk_i)
        vr = heads(sr @ Wv_r.T + bv_r)
        vi = heads(si @ Wv_i.T + bv_i)
        ar = jnp.einsum('bhnd,bhmd->bhnm', qr, kr) + jnp.einsum('bhnd,bhmd->bhnm', qi, ki)
        ai = jnp.einsum('bhnd,bhmd->bhnm', qi, kr) - jnp.einsum('bhnd,bhmd->bhnm', qr, ki)
        mag = jnp.sqrt(ar ** 2 + ai ** 2 + 1e-08) * HD ** (-0.5)
        w = jax.nn.softmax(mag, axis=-1)
        out_r = jnp.einsum('bhnm,bhmd->bhnd', w, vr).transpose(0, 2, 1, 3).reshape(Bsz, N, D)
        out_i = jnp.einsum('bhnm,bhmd->bhnd', w, vi).transpose(0, 2, 1, 3).reshape(Bsz, N, D)
        attn_r = out_r @ Wo_r.T + bo_r
        attn_i = out_i @ Wo_i.T + bo_i
        R = jnp.einsum('bnd,ned->bne', attn_r, int_Wr) - jnp.einsum('bnd,ned->bne', attn_i, int_Wi)
        I = jnp.einsum('bnd,ned->bne', attn_r, int_Wi) + jnp.einsum('bnd,ned->bne', attn_i, int_Wr)
        Ri, Ii = (R[:, :, None, :], I[:, :, None, :])
        Rj, Ij = (R[:, None, :, :], I[:, None, :, :])
        phase = jnp.arctan2(Ii * Rj - Ri * Ij, Ri * Rj + Ii * Ij)
        f = jnp.cos(phase) * strength[..., None]
        sup_r = jnp.einsum('bijd,bjd->bd', f, R)
        sup_i = jnp.einsum('bijd,bjd->bd', f, I)
        norm = jnp.sqrt(jnp.sum(sup_r ** 2 + sup_i ** 2, axis=-1, keepdims=True) + 1e-08)
        sup_r = sup_r / norm
        sup_i = sup_i / norm
        mr = sup_r @ meas_Mr.T - sup_i @ meas_Mi.T
        mi = sup_r @ meas_Mi.T + sup_i @ meas_Mr.T
        amp = jnp.sqrt(mr ** 2 + mi ** 2)
        out = jax.nn.gelu(_ln(amp @ post_W.T + post_b, post_g, post_be), approximate=False)
        return out

    e = jnp.stack([tbl_0[ids[:, 0]], tbl_1[ids[:, 1]], tbl_2[ids[:, 2]], tbl_3[ids[:, 3]]], axis=1)
    z = _L0_rec_ref(r_x, e, L0_rec_er_W1, L0_rec_er_b1, L0_rec_er_g1, L0_rec_er_be1, L0_rec_er_W2, L0_rec_er_b2, L0_rec_ei_W1, L0_rec_ei_b1, L0_rec_ei_g1, L0_rec_ei_be1, L0_rec_ei_W2, L0_rec_ei_b2, L0_rec_Wq_r, L0_rec_bq_r, L0_rec_Wq_i, L0_rec_bq_i, L0_rec_Wk_r, L0_rec_bk_r, L0_rec_Wk_i, L0_rec_bk_i, L0_rec_Wv_r, L0_rec_bv_r, L0_rec_Wv_i, L0_rec_bv_i, L0_rec_Wo_r, L0_rec_bo_r, L0_rec_Wo_i, L0_rec_bo_i, L0_rec_int_Wr, L0_rec_int_Wi, L0_rec_meas_Mr, L0_rec_meas_Mi, L0_rec_post_W, L0_rec_post_b, L0_rec_post_g, L0_rec_post_be)
    z = z.reshape(z.shape[0], -1)
    h = jnp.concatenate([z, r_x], axis=1)
    h = jnp.maximum(h @ W_top1 + b_top1, 0.0)
    h = jnp.maximum(h @ W_top2 + b_top2, 0.0)
    y = h @ W_top3
    return y


_drawn_inputs = setup_inputs


def setup_inputs(seed=0):
    import zlib

    import numpy as np

    out = dict(_drawn_inputs(seed))
    spreads = {'b_top1': (0.0, 0.1),
     'b_top2': (0.0, 0.1),
     'L0_rec_er_b1': (0.0, 0.8),
     'L0_rec_er_g1': (1.0, 0.6),
     'L0_rec_er_be1': (0.0, 0.8),
     'L0_rec_er_b2': (0.0, 0.8),
     'L0_rec_ei_b1': (0.0, 0.8),
     'L0_rec_ei_g1': (1.0, 0.6),
     'L0_rec_ei_be1': (0.0, 0.8),
     'L0_rec_ei_b2': (0.0, 0.8),
     'L0_rec_bq_r': (0.0, 0.8),
     'L0_rec_bq_i': (0.0, 0.8),
     'L0_rec_bk_r': (0.0, 0.8),
     'L0_rec_bk_i': (0.0, 0.8),
     'L0_rec_bv_r': (0.0, 0.1),
     'L0_rec_bv_i': (0.0, 0.1),
     'L0_rec_bo_r': (0.0, 0.1),
     'L0_rec_bo_i': (0.0, 0.1),
     'L0_rec_int_Wi': (0.0, 0.1),
     'L0_rec_post_b': (0.0, 0.1),
     'L0_rec_post_g': (1.0, 0.2),
     'L0_rec_post_be': (0.0, 0.1)}
    factors = {'L0_rec_Wq_r': 8.0, 'L0_rec_Wq_i': 8.0, 'L0_rec_Wk_r': 8.0, 'L0_rec_Wk_i': 8.0}
    for name, (base, spread) in spreads.items():
        noise = np.random.default_rng([zlib.crc32(name.encode()), seed]).standard_normal(out[name].shape)
        drawn = base * np.exp(spread * noise) if base else spread * noise
        out[name] = jnp.asarray(drawn.astype(out[name].dtype))
    for name, factor in factors.items():
        out[name] = (out[name] * factor).astype(out[name].dtype)
    return out
```

```python
from contextlib import ExitStack

import concourse.bass as bass
from concourse import mybir

ALU = mybir.AluOpType
ACT = mybir.ActivationFunctionType
AX = mybir.AxisListType
F32 = mybir.dt.float32
F32R = mybir.dt.float32r
BF16 = mybir.dt.bfloat16
I32 = mybir.dt.int32

P = 128
BATCH = 1024
IN = 2048
HID = 2048
D = 512
N = 4
H = 8
HD = D // H
TOP1 = 512
TOP2 = 256
NT = BATCH // P
HALF = BATCH // 2
HT = HALF // P
KT = IN // P
DT = D // P
UNIT = KT * P
QC = UNIT // 4
EPS_LN = 1e-5
EPS_MAG = 1e-8

PHASES = [
    dict(kind="G1", job=0, ln=None),
    dict(kind="G1", job=1, ln=0),
    dict(kind="TX", half=0, ln=None),
    dict(kind="G2", job=0, ln=None, load_x=1),
    dict(kind="G1", job=2, ln=1),
    dict(kind="G2", job=1, ln=None),
    dict(kind="G1", job=3, ln=2),
    dict(kind="G2", job=2, ln=None),
    dict(kind="TX", half=1, ln=3),
    dict(kind="G2", job=3, ln=None),
]
_unit = _acc = _store = 0
for _p in PHASES:
    _p["units"] = 4 if _p["kind"] == "TX" else KT
    _p["unit"], _p["acc"], _p["store"] = _unit, _acc, _store
    _unit += _p["units"]
    _acc += HT if _p["kind"] == "TX" else KT
    _store += {"G1": 0, "G2": KT, "TX": HT}[_p["kind"]]
UNITS = _unit
STORES = _store


def encode(nc, dram):
    with ExitStack() as ctx:
        def sb(name, shape, dt=F32):
            return ctx.enter_context(nc.sbuf_tensor(name, shape, dt))

        def sem(name):
            return ctx.enter_context(nc.semaphore(name))

        x_hi = sb("x_hi", [P, KT, HALF], F32R)
        x_lo = sb("x_lo", [P, KT, HALF], F32R)
        h_hi = sb("h_hi", [P, KT, HALF], F32R)
        h_lo = sb("h_lo", [P, KT, HALF], F32R)
        raw = sb("raw", [P, KT, HALF])
        w_raw = sb("w_raw", [P, 2, UNIT])
        w_hi = sb("w_hi", [P, 4, QC], F32R)
        w_lo = sb("w_lo", [P, 4, QC], F32R)
        lane_sum = sb("lane_sum", [P, HALF])
        lane_sq = sb("lane_sq", [P, HALF])
        rstd = sb("rstd", [P, HALF])
        dev = sb("dev", [P, HALF])
        stage = sb("stage", [P, 2, HALF])
        x_stage = sb("x_stage", [P, HALF])
        ones = sb("ones", [P, P])
        eps = sb("eps", [P, 1])
        vecs = sb("features", [P, 8, KT])

        bank = [ctx.enter_context(nc.psum_tensor(f"bank{i}", [P, 512], F32)) for i in range(8)]
        mean_bank, gelu_bank, sq_bank = bank[2], bank[3], bank[7]
        tx_banks = [bank[0], bank[1], bank[4], bank[5]]

        w_loaded = [sem(f"w_loaded{i}") for i in range(2)]
        wh_ready = sem("wh_ready")
        wl_ready = sem("wl_ready")
        w_used = sem("w_used")
        x0_loaded = [sem(f"x0_loaded{i}") for i in range(4)]
        x_loaded = sem("x_loaded")
        xh_ready = sem("xh_ready")
        xl_ready = sem("xl_ready")
        consts = sem("consts")
        vecs_loaded = sem("vecs_loaded")
        acc_evacuated = sem("acc_evacuated")
        stored = [sem(f"stored{i}") for i in range(2)]
        dev_ready = sem("dev_ready")
        sq_ready = sem("sq_ready")
        stat_done = sem("stat_done")
        merge = sem("merge")
        lane_mean_ready = sem("lane_mean_ready")
        lane_var_ready = sem("lane_var_ready")
        mean_ready = sem("mean_ready")
        var_ready = sem("var_ready")
        std_ready = sem("std_ready")
        centered = sem("centered")
        ln_scaled = sem("ln_scaled")
        ln_gelu = sem("ln_gelu")
        ln_hi = sem("ln_hi")
        ln_lo = sem("ln_lo")

        B1, G, BE, B2 = range(4)
        last_g2 = {}
        end = 0
        for ph in PHASES:
            if ph["ln"] is not None:
                last_g2[ph["ln"]] = end
            if ph["kind"] == "G2":
                end = ph["unit"] + ph["units"]
        tx0_end = PHASES[2]["unit"] + PHASES[2]["units"]

        def steps(eng, ph, body):
            pairs = ph["units"] // 2
            if ph["kind"] == "TX":
                for i in range(pairs):
                    for e in range(2):
                        body(i, e, i == 0, False)
                return
            final = ph is PHASES[-1]
            for e in range(2):
                body(0, e, True, False)
            with eng.Fori(1, pairs - final) as i:
                for e in range(2):
                    body(i, e, False, False)
            if final:
                for e in range(2):
                    body(pairs - 1, e, False, True)

        def slab(t, i):
            return t[:, i, :] if isinstance(i, int) else t[:, bass.ds(i, 1), :].rearrange("p a c -> p (a c)")

        def col(k, enc, i):
            j = 4 * enc + k
            return vecs[:, j, i:i + 1] if isinstance(i, int) else vecs[:, j, bass.ds(i, 1)]

        block = ctx.enter_context(nc.Block())

        @block.sync
        def _(sp):
            for c in range(4):
                sp.dma_start(raw[:, 4 * c:4 * c + 4, :], dram["x"][0, :, 4 * c:4 * c + 4, :]).then_inc(x0_loaded[c], 16)
                if c < 2:
                    sp.dma_start(w_raw[:, c, :], dram["w1r"][c, :, :]).then_inc(w_loaded[c], 16)
                if c == 2:
                    sp.dma_start(vecs[:, :, :], dram["vecs"]).then_inc(vecs_loaded, 16)
            for ph in PHASES:
                name = "wtx" if ph["kind"] == "TX" else ("w1" if ph["kind"] == "G1" else "w2") + "ri"[ph["job"] % 2]

                def load(i, e, first, last, ph=ph, name=name):
                    if ph is PHASES[0] and first:
                        return
                    sp.wait_ge(wl_ready, 8 * i + (4 * (ph["unit"] + e) - 4))
                    src = dram[name]
                    m = 2 * i + e
                    src = src[m, :, :] if isinstance(m, int) else src[bass.ds(m, 1), :, :].rearrange("a p c -> p (a c)")
                    sp.dma_start(w_raw[:, e, :], src).then_inc(w_loaded[e], 16)
                    if ph.get("load_x"):
                        sp.wait_ge(xl_ready, 2 * i + (KT + e))
                        xs = dram["x"][ph["load_x"]]
                        xs = xs[:, m, :] if isinstance(m, int) else xs[:, bass.ds(m, 1), :].rearrange("p a c -> p (a c)")
                        sp.dma_start(x_stage[:, :], xs).then_inc(x_loaded, 16)
                steps(sp, ph, load)

        @block.gpsimd
        def _(pool):
            pool.memset(ones[:, :], 1.0 / P).then_inc(consts, 1)
            pool.memset(eps[:, :], EPS_LN).then_inc(consts, 1)

        @block.scalar
        def _(act):
            def split_w(u_half, slot, u_base, i, q, first_unit=False):
                if q == 0:
                    act.wait_ge(w_loaded[slot], 16 * i + 16 * (u_base // 2 + 1))
                if not first_unit:
                    act.wait_ge(w_used, 8 * i + (4 * u_base + q - 3))
                act.copy(w_hi[:, q, :], w_raw[:, slot, q * QC:(q + 1) * QC]).then_inc(wh_ready, 1)

            def gelu_tile(ln, t, c):
                act.wait_ge(ln_scaled, c + 1)
                act.wait_ge(ln_lo, c)
                act.activation(gelu_bank[:, :], slab(raw, t), ACT.Gelu, bias=col(BE, ln % 2, t),
                               scale=col(G, ln % 2, t)).then_inc(ln_gelu, 1)

            def hi_tile(t, c):
                act.wait_ge(ln_gelu, c + 1)
                act.copy(slab(h_hi, t), gelu_bank[:, :]).then_inc(ln_hi, 1)

            def std(ln):
                act.wait_ge(var_ready, ln + 1)
                act.activation(rstd[:, :], sq_bank[:, :], ACT.Sqrt, bias=eps[:, :]).then_inc(std_ready, 1)

            act.wait_ge(consts, 2)
            for kt in range(4):
                if kt % 4 == 0:
                    act.wait_ge(x0_loaded[kt // 4], 16)
                act.copy(x_hi[:, kt, :], raw[:, kt, :]).then_inc(xh_ready, 1)
            split_w(0, 0, 0, 0, 0, True)
            for kt in range(4, KT):
                if kt % 4 == 0:
                    act.wait_ge(x0_loaded[kt // 4], 16)
                act.copy(x_hi[:, kt, :], raw[:, kt, :]).then_inc(xh_ready, 1)
                if kt % 4 == 3:
                    split_w(0, 0, 0, 0, kt // 4, True)
            act.wait_ge(vecs_loaded, 16)
            for ph in PHASES:
                ln = ph["ln"]

                def step(i, e, first, last, ph=ph, ln=ln):
                    u, m = ph["unit"] + e, 2 * i + e
                    more = not (last and e == 1)

                    def hi(q):
                        if more:
                            split_w(0, (e + 1) % 2, u + 1, i, q)
                    if ln is not None and first and i == 0 and e == 0:
                        hi(0)
                        std(ln)
                        act.wait_ge(w_used, 4 * last_g2[ln]) if last_g2[ln] else None
                    else:
                        hi(0)
                    if ph["kind"] == "TX":
                        done = []
                        for j in range(4):
                            if ln is not None:
                                t = 4 * m + j
                                gelu_tile(ln, t, KT * ln + t)
                                hi_tile(t, KT * ln + t)
                            if j < 3:
                                hi(j + 1) if j < 2 else None
                        hi(3)
                    else:
                        if ln is not None:
                            gelu_tile(ln, m, m + KT * ln)
                        hi(1)
                        if ln is not None:
                            hi_tile(m, m + KT * ln)
                        hi(2)
                    if ph.get("load_x"):
                        if first and e == 0:
                            act.wait_ge(w_used, 4 * tx0_end)
                        act.wait_ge(x_loaded, 32 * i + 16 * (e + 1))
                        act.copy(slab(x_hi, m), x_stage[:, :]).then_inc(xh_ready, 1)
                    if ph["kind"] == "TX":
                        if m == 3:
                            for bt in range(HT):
                                z = ph["store"] + bt
                                if bt == 0:
                                    act.wait_ge(w_used, 4 * (ph["unit"] + 4))
                                if z >= 2:
                                    act.wait_ge(stored[z % 2], 16 * (z // 2))
                                act.copy(stage[:, z % 2, :], tx_banks[bt][:, :]).then_inc(acc_evacuated, 1)
                                act.wait_ge(acc_evacuated, ph["acc"] + bt + 1)
                                act.dma_start(dram["t1x"][HT * ph["half"] + bt], stage[:, z % 2, :])\
                                   .then_inc(stored[z % 2], 16)
                        return
                    enc, half = ph["job"] % 2, ph["job"] // 2
                    a = ph["acc"] + e
                    act.wait_ge(w_used, 8 * i + (4 * u + 4))
                    if ph["kind"] == "G1":
                        if ph is PHASES[0] and first and e == 0:
                            act.wait_ge(xl_ready, KT)
                        act.activation(slab(raw, m), bank[e][:, :], ACT.Identity,
                                       bias=col(B1, enc, m)).then_inc(acc_evacuated, 1)
                        hi(3)
                        c = KT * ph["job"] + e
                        act.wait_ge(dev_ready, 2 * i + (c + 1))
                        act.wait_ge(stat_done, 2 * i + c)
                        act.activation(sq_bank[:, :], dev[:, :], ACT.Square).then_inc(sq_ready, 1)
                    else:
                        z = ph["store"] + e
                        if not (isinstance(i, int) and z + 2 * i < 2):
                            act.wait_ge(stored[e], 16 * i + 16 * (z // 2))
                        act.activation(stage[:, e, :], bank[e][:, :], ACT.Identity,
                                       bias=col(B2, enc, m)).then_inc(acc_evacuated, 1)
                        hi(3)
                        act.wait_ge(acc_evacuated, 2 * i + (a + 1))
                        dst = dram["s"][HT * half:HT * half + HT, :, enc]
                        dst = dst[:, :, m, :].rearrange("t p c -> p t c") if isinstance(m, int) else \
                            dst[:, :, bass.ds(m, 1), :].rearrange("t p a c -> p t (a c)")
                        act.dma_start(dst, stage[:, e, :].rearrange("p (t c) -> p t c", t=HT)).then_inc(stored[e], 16)
                steps(act, ph, step)
            for z in range(2):
                act.wait_ge(stored[z], 16 * (STORES // 2))

        @block.vector
        def _(dve):
            link_count = [0]

            def link(ins):
                link_count[0] += 1
                ins.then_inc(merge, 1)
                dve.wait_ge(merge, link_count[0])

            def lo_w(slot, u_base, i, q):
                dve.wait_ge(wh_ready, 8 * i + (4 * u_base + q + 1))
                dve.tensor_tensor(w_lo[:, q, :], w_raw[:, slot, q * QC:(q + 1) * QC], w_hi[:, q, :],
                                  ALU.subtract).then_inc(wl_ready, 1)

            def lo_x(i, src, c):
                dve.wait_ge(xh_ready, c + 1)
                dve.tensor_tensor(slab(x_lo, i), src, slab(x_hi, i), ALU.subtract).then_inc(xl_ready, 1)

            def merge_lanes(job):
                dve.wait_ge(stat_done, KT * (job + 1))
                link(dve.tensor_tensor(dev[:, :], lane_sum[:, :], lane_sum[:, :], ALU.mult))
                dve.scalar_tensor_tensor(lane_sum[:, :], lane_sum[:, :], 1.0 / KT, raw[:, 0, :], ALU.mult,
                                         ALU.add).then_inc(lane_mean_ready, 1)
                link(dve.scalar_tensor_tensor(lane_sq[:, :], dev[:, :], -1.0 / KT, lane_sq[:, :], ALU.mult, ALU.add))
                dve.wait_ge(mean_ready, job + 1)
                link(dve.tensor_tensor(dev[:, :], lane_sum[:, :], mean_bank[:, :], ALU.subtract))
                link(dve.tensor_tensor(dev[:, :], dev[:, :], dev[:, :], ALU.mult))
                dve.scalar_tensor_tensor(lane_sq[:, :], lane_sq[:, :], 1.0 / KT, dev[:, :], ALU.mult,
                                         ALU.add).then_inc(lane_var_ready, 1)
                dve.wait_ge(std_ready, job + 1)
                dve.memset(lane_sum[:, :], 0.0)
                dve.memset(lane_sq[:, :], 0.0)
                link(dve.reciprocal(rstd[:, :], rstd[:, :]))

            def normalize(t, c):
                dve.tensor_tensor(slab(raw, t), slab(raw, t), mean_bank[:, :], ALU.subtract).then_inc(centered, 1)
                dve.wait_ge(centered, c + 1)
                dve.tensor_tensor(slab(raw, t), slab(raw, t), rstd[:, :], ALU.mult).then_inc(ln_scaled, 1)

            def lo_tile(t, c):
                dve.wait_ge(ln_hi, c + 1)
                dve.tensor_tensor(slab(h_lo, t), gelu_bank[:, :], slab(h_hi, t), ALU.subtract).then_inc(ln_lo, 1)

            dve.memset(lane_sum[:, :], 0.0)
            link(dve.memset(lane_sq[:, :], 0.0))
            for kt in range(KT):
                lo_x(kt, raw[:, kt, :], kt)
                if kt % 4 == 3:
                    lo_w(0, 0, 0, kt // 4)
            for ph in PHASES:
                ln = ph["ln"]

                def step(i, e, first, last, ph=ph, ln=ln):
                    u, m = ph["unit"] + e, 2 * i + e

                    def lo(q):
                        if not (last and e == 1):
                            lo_w((e + 1) % 2, u + 1, i, q)
                    lo(0)
                    if ln is not None and first and i == 0 and e == 0:
                        merge_lanes(ln)
                    if ph["kind"] == "TX":
                        for j in range(4):
                            if ln is not None:
                                t = 4 * m + j
                                normalize(t, KT * ln + t)
                            if ln is not None:
                                lo_tile(t, KT * ln + t)
                            if j < 2:
                                lo(j + 1)
                        lo(3)
                        return
                    if ln is not None:
                        normalize(m, m + KT * ln)
                    lo(1)
                    if ln is not None:
                        lo_tile(m, m + KT * ln)
                    lo(2)
                    if ph.get("load_x"):
                        lo_x(m, x_stage[:, :], m + KT)
                    lo(3)
                    if ph["kind"] == "G1":
                        c = KT * ph["job"] + e
                        dve.wait_ge(acc_evacuated, 2 * i + (ph["acc"] + e + 1))
                        dve.wait_ge(stat_done, 2 * i + c)
                        dve.tensor_tensor(dev[:, :], slab(raw, m), raw[:, 0, :], ALU.subtract).then_inc(dev_ready, 1)
                        dve.wait_ge(dev_ready, 2 * i + (c + 1))
                        dve.tensor_tensor(lane_sum[:, :], lane_sum[:, :], dev[:, :], ALU.add)
                        dve.wait_ge(sq_ready, 2 * i + (c + 1))
                        dve.tensor_tensor(lane_sq[:, :], lane_sq[:, :], sq_bank[:, :], ALU.add).then_inc(stat_done, 1)
                steps(dve, ph, step)

        @block.tensor
        def _(pe):
            pe.wait_ge(consts, 2)
            for ph in PHASES:
                ln = ph["ln"]

                def step(i, e, first, last, ph=ph, ln=ln):
                    u, m = ph["unit"] + e, 2 * i + e
                    start = first and i == 0 and e == 0
                    if ph["kind"] == "TX":
                        if start:
                            pe.wait_ge(acc_evacuated, ph["acc"])
                    else:
                        half = ph["job"] // 2
                        a = ph["acc"] + e
                        if not (isinstance(i, int) and a + 2 * i < 2):
                            pe.wait_ge(acc_evacuated, 2 * i + (a - 1))
                        hi, lo = (x_hi, x_lo) if ph["kind"] == "G1" else (h_hi, h_lo)
                    for q in range(4):
                        pe.wait_ge(wl_ready, 8 * i + (4 * u + q + 1))
                        if start and ph["kind"] == "G1":
                            pe.wait_ge(xl_ready, KT * half + 4 * q + 4)
                        if start and ph["kind"] == "G2":
                            pe.wait_ge(ln_lo, KT * ph["job"] + 4 * q + 4)
                        for j in range(4):
                            kt = 4 * q + j
                            if ph["kind"] == "TX":
                                kt = 4 * m + q
                                out, rows = tx_banks[j][:, :], slice(j * P, (j + 1) * P)
                                args = ((x_hi[:, kt, rows], w_hi[:, q, :]), (x_lo[:, kt, rows], w_hi[:, q, :]),
                                        (x_hi[:, kt, rows], w_lo[:, q, :]))
                            else:
                                out, cols = bank[e][:, :], slice(j * P, (j + 1) * P)
                                args = ((w_hi[:, q, cols], hi[:, kt, :]), (w_hi[:, q, cols], lo[:, kt, :]),
                                        (w_lo[:, q, cols], hi[:, kt, :]))
                            for k, (a_, b_) in enumerate(args):
                                mm = pe.matmul(out, a_, b_, start=(kt == 0 and k == 0), stop=(kt == KT - 1 and k == 2))
                        mm.then_inc(w_used, 1)
                        if start and ln is not None and q == 0:
                            pe.wait_ge(lane_mean_ready, ln + 1)
                            pe.matmul(mean_bank[:, :], ones[:, :], lane_sum[:, :], start=True, stop=True)\
                              .then_inc(mean_ready, 1)
                        if start and ln is not None and q == 2:
                            pe.wait_ge(lane_var_ready, ln + 1)
                            pe.matmul(sq_bank[:, :], ones[:, :], lane_sq[:, :], start=True, stop=True)\
                              .then_inc(var_ready, 1)
                steps(pe, ph, step)


QKV, WO, INT, MEAS, POST, TOPZ, TOP2W = 0, 6, 8, 16, 18, 19, 20
UNITS2 = 21
TURN = [
    ("att", range(QKV, QKV + 4)),
    ("tail", [MEAS, MEAS + 1]),
    ("inter", [WO, WO + 1]),
    ("tail", [POST]),
    ("inter", range(INT, INT + 4)),
    ("tail", [TOPZ]),
    ("inter", range(INT + 4, INT + 6)),
    ("tail", [TOP2W]),
    ("inter", range(INT + 6, INT + 8)),
    ("att", range(QKV + 4, QKV + 6)),
]
RING = 3


def turn_units(att, inter, tail):
    parts = dict(att=att, inter=inter, tail=tail)
    return [u for part, units in TURN for u in units if parts[part]]


PAIRS = [(0, 3, 1), (3, 2, 2), (5, 1, 3)]
PAIR_AT = {}
for _f, _c, _a in PAIRS:
    for _i in range(_c):
        PAIR_AT[(_i, _i + _a)] = _f + _i
CH = 256
SCORE_STEPS, PV_STEPS, TAIL_STEPS, PHASE_STEPS = 32, 22, 7, 56


def mix(nc, dram):
    with ExitStack() as ctx:
        def sb(name, shape, dt=F32):
            return ctx.enter_context(nc.sbuf_tensor(name, shape, dt))

        def sem(name):
            return ctx.enter_context(nc.semaphore(name))

        s_in = sb("s_in", [P, 2, KT, P])
        q_sb = sb("q_sb", [P, N, 2, D])
        k_sb = sb("k_sb", [P, N, 2, D])
        v_sb = sb("v_sb", [P, N, 2, D])
        work = sb("work", [P, 4096])
        a_t = sb("a_t", [P, 2, DT, D])
        na_t = sb("na_t", [P, DT, D])
        ri_sb = sb("ri_sb", [P, 2, N, D])
        w2 = sb("w2", [P, RING, UNIT])
        pa = sb("pa", [P, N * D])
        pb = sb("pb", [P, 6 * CH])
        zero = sb("zero", [P, N, D], BF16)
        pair_zero = sb("pair_zero", [P, 6, D], BF16)
        rows = sb("rows_sb", [P, 9 * D])
        cols = sb("cols_sb", [P, 4, DT])
        sup = sb("sup", [P, 2, D])
        sup_t = sb("sup_t", [P, 3, DT, P])
        x_t = sb("x_t", [P, DT, P])
        ta = sb("ta", [P, D])
        tb = sb("tb", [P, D])
        x1 = sb("x1", [P, TOP1])
        ident = sb("ident", [P, P])
        ids = sb("ids_sb", [P, NT, N], I32)
        strength = sb("strength", [P, NT, N, N])
        st = sb("st", [P, N * N])
        sc = pb[:, 0:512].rearrange("p (n k m r h) -> p n k m r h", n=N, k=2, m=N, r=2)
        ar, ai, mag = (pb[:, 512 + 128 * j:640 + 128 * j].rearrange("p (n m h) -> p n m h", n=N, m=N)
                       for j in range(3))
        w_att = sb("w_att", [P, N, N, H])
        mx = sb("mx", [P, N, H])
        small = sb("small", [P, 8])
        eps2 = sb("eps2", [P, 1])
        y_all = sb("y_all", [P, NT])
        bank = [ctx.enter_context(nc.psum_tensor(f"bank2_{i}", [P, 512], F32)) for i in range(8)]

        o_sb = a_t[:, :, :, :].rearrange("p r f c -> p (r f c)").rearrange("p (n r d) -> p n r d", n=N, r=2)
        out_t = [na_t[:, :, :], pa[:, :].rearrange("p (f c) -> p f c", f=DT)]
        bq, bk = rows[:, 0:1024], rows[:, 1024:2048]
        post_b, post_g, post_be = (rows[:, 2048 + D * j:2048 + D * (j + 1)] for j in range(3))
        b_top1, b_top2, w3 = rows[:, 3584:4096], rows[:, 4096:4352], rows[:, 4352:4608]

        w2_loaded = [sem(f"w2_loaded{i}") for i in range(RING)]
        s_loaded = [sem(f"s_loaded{i}") for i in range(2)]
        names = """x1_loaded consts2 setup_loaded ids_loaded gathered ident_made
            qkv_done qkv_evacuated biased score scored softmax mag_ready exp_in exp_ready pv out_ready
            out_transposed out_t_ready o_done a_ready na_ready int_done int_evacuated
            squared n2_ready mask_made pair_zero_made ln_ready y_ready ysq_ready phase norm_root norm_sq_ready
            norm_ready sup_ready sup_scaled sup_transposed sup_t_ready meas_done meas_sq amp_sq_ready amp_ready
            amp_transposed amp_t_ready post_done tail mean2_ready var2_ready std2_ready pre_gelu z_ready
            z_transposed z_t_ready topz_done h1_ready h1_transposed h1_t_ready top2_done y_done
            y_stored""".split()
        S = {n: sem("m_" + n) for n in names}

        def turns(eng, body):
            body(0, True, False, False)
            body(1, True, True, False)
            body(2, True, True, True)
            with eng.Fori(3, NT) as i:
                body(i, True, True, True)
            body(NT, False, True, True)
            body(NT + 1, False, False, True)

        def first_unit(i):
            return {0: 0, 1: 6, 2: 22, NT: 22 + UNITS2 * (NT - 2), NT + 1: 22 + UNITS2 * (NT - 2) + 15}[i]

        def place(i, k):
            if isinstance(i, int):
                u = first_unit(i) + k
                return u % RING, 16 * (u // RING + 1)
            k += 22 - 2 * UNITS2
            return k % RING, (16 * UNITS2 // RING) * i + 16 * (k // RING + 1)

        def product(i, unit):
            if unit < WO:
                return S["qkv_done"], 24 * i + 4 * (unit - QKV + 1)
            if unit < INT:
                return S["o_done"], 8 * i + (4 * (unit - WO + 1) - 8)
            if unit < MEAS:
                return S["int_done"], 8 * i + (unit - INT + 1 - 8)
            if unit < POST:
                return S["meas_done"], 2 * i + (unit - MEAS + 1 - 4)
            return S[{POST: "post_done", TOPZ: "topz_done", TOP2W: "top2_done"}[unit]], i - 1

        def units_of(i):
            return turn_units(*((i < NT, 1 <= i <= NT, i >= 2) if isinstance(i, int) else (True, True, True)))

        def qkv_bank(k, n):
            return bank[(4 if k == 5 else 0) + n]

        block = ctx.enter_context(nc.Block())

        @block.sync
        def _(sp):
            sp.dma_start(rows[:, :], dram["rows"]).then_inc(S["setup_loaded"], 16)
            sp.dma_start(cols[:, :, :], dram["cols"]).then_inc(S["setup_loaded"], 16)
            sp.dma_start(ids[:, :, :], dram["ids"]).then_inc(S["ids_loaded"], 16)

            def body(i, att, inter, tail):
                units = units_of(i)
                before = [] if isinstance(i, int) and i == 0 else units_of(i - 1)

                def load_s(t, part):
                    src = dram["s"]
                    src = src[t, :, part] if isinstance(t, int) else \
                        src[bass.ds(t, 1), :, part].rearrange("t p m c -> p (t m) c")
                    sp.dma_start(s_in[:, part, :, :], src).then_inc(s_loaded[part], 16)
                if isinstance(i, int) and i == 0:
                    load_s(0, 0)
                    load_s(0, 1)
                for k, unit in enumerate(units):
                    slot, _ = place(i, k)
                    if k >= RING:
                        sp.wait_ge(*product(i, units[k - RING]))
                    elif before:
                        sp.wait_ge(*product(i - 1, before[k - RING]))
                    if unit in (QKV + 1, QKV + 2) and not (isinstance(i, int) and i == 0):
                        part = unit - QKV - 1
                        sp.wait_ge(S["qkv_done"], 24 * i - (4 if part == 0 else 0))
                        load_s(i, part)
                    size = DT * TOP2 if unit == TOP2W else UNIT
                    sp.dma_start(w2[:, slot, 0:size], dram["ws2"][unit, :, 0:size]).then_inc(w2_loaded[slot], 16)
                    if unit == MEAS:
                        sp.wait_ge(S["tail"], TAIL_STEPS * (i - 2))
                        src = dram["t1x"]
                        src = src[i - 2] if isinstance(i, int) else \
                            src[bass.ds(i - 2, 1)].rearrange("a p c -> p (a c)")
                        sp.dma_start(x1[:, :], src).then_inc(S["x1_loaded"], 16)
            turns(sp, body)
            sp.wait_ge(S["y_done"], NT)
            sp.dma_start(dram["out"], y_all[:, :]).then_inc(S["y_stored"], 16)
            sp.wait_ge(S["y_stored"], 16)

        @block.gpsimd
        def _(pool):
            pool.memset(eps2[:, :], EPS_LN).then_inc(S["consts2"], 1)
            pool.memset(ident[:, :], 0.0).then_inc(S["consts2"], 1)
            pool.wait_ge(S["consts2"], 2)
            pool.affine_select(out=ident[:, :], in_=ident[:, :], compare_op=ALU.not_equal, fill=1.0, base=0,
                               pattern=[[-1, P]], channel_multiplier=1).then_inc(S["ident_made"], 1)
            pool.wait_ge(S["ids_loaded"], 16)
            for t in range(NT):
                for f in range(N):
                    pool.indirect_dma_start(strength[:, t, f, :], None, dram[f"tbl{f}"],
                                            bass.IndirectOffsetOnAxis(ap=ids[:, t, f:f + 1], axis=0))\
                        .then_inc(S["gathered"], 16)

            def body(i, att, inter, tail):
                if not inter:
                    return
                pool.wait_ge(S["mask_made"], i)
                for f, c, apart in PAIRS:
                    last = pool.tensor_tensor(pair_zero[:, f:f + c, :], zero[:, 0:c, :],
                                              zero[:, apart:apart + c, :], ALU.add)
                    last.then_inc(S["pair_zero_made"], 1)
            turns(pool, body)

        @block.scalar
        def _(act):
            act.wait_ge(S["consts2"], 2)
            act.wait_ge(S["setup_loaded"], 32)

            def qkv(t, units):
                for k in units:
                    dst = (q_sb, k_sb, v_sb)[k // 2]
                    if k == 0:
                        act.wait_ge(S["score"], SCORE_STEPS * t)
                    if k == 4:
                        act.wait_ge(S["out_ready"], 2 * t)
                    for n in range(N):
                        act.wait_ge(S["qkv_done"], 24 * t + (4 * k + n + 1))
                        act.copy(dst[:, n, k % 2, :], qkv_bank(k, n)[:, :]).then_inc(S["qkv_evacuated"], 1)

            def interference(t, n):
                act.wait_ge(S["int_done"], 8 * t + (2 * n + 2))
                if n == 0:
                    act.wait_ge(S["norm_ready"], t)
                for part in range(2):
                    act.copy(ri_sb[:, part, n, :], bank[2 * (n % 2) + part][:, :]).then_inc(S["int_evacuated"], 1)

            def sup_transpose(t):
                act.wait_ge(S["sup_transposed"], t + 1)
                act.copy(sup_t[:, 0].rearrange("p k c -> p (k c)"), bank[6][:, :]).then_inc(S["sup_t_ready"], 1)
                act.copy(sup_t[:, 1].rearrange("p k c -> p (k c)"), bank[7][:, :]).then_inc(S["sup_t_ready"], 1)
                act.mul(sup_t[:, 2].rearrange("p k c -> p (k c)"), bank[7][:, :], -1.0).then_inc(S["sup_t_ready"], 1)

            def tail_squares(t):
                act.wait_ge(S["meas_done"], 2 * t + 2)
                act.wait_ge(S["y_done"], t)
                act.activation(ta[:, :], bank[4][:, :], ACT.Square).then_inc(S["meas_sq"], 1)
                act.activation(tb[:, :], bank[5][:, :], ACT.Square).then_inc(S["meas_sq"], 1)

            def tail_amplitude(t):
                act.wait_ge(S["amp_sq_ready"], t + 1)
                act.activation(tb[:, :], ta[:, :], ACT.Sqrt).then_inc(S["amp_ready"], 1)

            def tail_amp_t(t):
                act.wait_ge(S["amp_transposed"], t + 1)
                act.copy(x_t[:, :, :].rearrange("p k c -> p (k c)"), bank[6][:, :]).then_inc(S["amp_t_ready"], 1)

            def tail_post(t):
                act.wait_ge(S["mean2_ready"], t + 1)
                act.activation(tb[:, :], ta[:, :], ACT.Square, bias=small[:, 2:3],
                               accum_out=small[:, 1:2]).then_inc(S["var2_ready"], 1)
                act.wait_ge(S["var2_ready"], t + 1)
                act.activation(small[:, 0:1], small[:, 1:2], ACT.Sqrt, bias=eps2[:, :],
                               scale=1.0 / D).then_inc(S["std2_ready"], 1)
                act.wait_ge(S["pre_gelu"], t + 1)
                act.activation(ta[:, :], tb[:, :], ACT.Gelu).then_inc(S["z_ready"], 1)

            def tail_z_t(t):
                act.wait_ge(S["z_transposed"], t + 1)
                act.copy(x_t[:, :, :].rearrange("p k c -> p (k c)"), bank[7][:, :]).then_inc(S["z_t_ready"], 1)

            def tail_h1_t(t):
                act.wait_ge(S["h1_transposed"], t + 1)
                act.copy(x_t[:, :, :].rearrange("p k c -> p (k c)"), bank[6][:, :]).then_inc(S["h1_t_ready"], 1)

            def softmax(t):
                act.wait_ge(S["scored"], t + 1)
                act.activation(mag[:, :, :, :], ar[:, :, :, :], ACT.Sqrt).then_inc(S["mag_ready"], 1)
                act.wait_ge(S["exp_in"], t + 1)
                act.activation(mag[:, :, :, :], ai[:, :, :, :], ACT.Exp, scale=HD ** -0.5).then_inc(S["exp_ready"], 1)

            def out_transpose(t):
                act.wait_ge(S["int_done"], 8 * t)
                for j in range(8):
                    act.wait_ge(S["out_transposed"], 8 * t + (j + 1))
                    if j == 4:
                        act.wait_ge(S["norm_ready"], t)
                    act.activation(out_t[j // 4][:, j % 4, :], bank[6 + j % 2][:, :], ACT.Identity,
                                   bias=cols[:, j // 4, j % 4:j % 4 + 1]).then_inc(S["out_t_ready"], 1)

            def projection(t, js):
                for j in js:
                    act.wait_ge(S["o_done"], 8 * t + (j + 1))
                    act.activation(a_t[:, j // 4, j % 4, :], bank[j % 4][:, :], ACT.Identity,
                                   bias=cols[:, 2 + j // 4, j % 4:j % 4 + 1]).then_inc(S["a_ready"], 1)
                    if j >= 4:
                        act.wait_ge(S["a_ready"], 8 * t + (j + 1))
                        act.mul(na_t[:, j % 4, :], a_t[:, 1, j % 4, :], -1.0).then_inc(S["na_ready"], 1)

            def unit_vectors(t, att):
                act.wait_ge(S["norm_ready"], t)
                if att:
                    act.wait_ge(S["score"], SCORE_STEPS * t + 2 * SCORE_STEPS)
                else:
                    act.wait_ge(S["out_ready"], 2 * NT)
                act.wait_ge(S["int_evacuated"], 8 * t + 8)
                for part in range(2):
                    act.activation(work[:, part * 2048:(part + 1) * 2048],
                                   ri_sb[:, part, :, :].rearrange("p n d -> p (n d)"), ACT.Square)\
                       .then_inc(S["squared"], 1)
                act.wait_ge(S["n2_ready"], t + 1)
                act.activation(work[:, 2048:4096], work[:, 0:2048], ACT.Ln).then_inc(S["ln_ready"], 1)
                act.wait_ge(S["ln_ready"], t + 1)
                act.activation(work[:, 2048:4096], work[:, 2048:4096], ACT.Exp, scale=-0.5).then_inc(S["y_ready"], 1)
                act.wait_ge(S["y_ready"], t + 1)
                act.activation(pa[:, :], work[:, 2048:4096], ACT.Square).then_inc(S["ysq_ready"], 1)

            def norm_root(t):
                act.wait_ge(S["norm_sq_ready"], t + 1)
                act.activation(small[:, 5:6], small[:, 4:5], ACT.Sqrt).then_inc(S["norm_root"], 1)

            def body(i, att, inter, tail):
                if att:
                    qkv(i, range(0, 2))
                if tail:
                    norm_root(i - 2)
                if att:
                    qkv(i, range(2, 4))
                if tail:
                    act.wait_ge(S["norm_ready"], i - 1)
                    for part in range(2):
                        act.activation(sup[:, part, :], sup[:, part, :], ACT.Copy, scale=small[:, 6:7])\
                           .then_inc(S["sup_scaled"], 1)
                    sup_transpose(i - 2)
                if inter:
                    out_transpose(i - 1)
                if tail:
                    tail_squares(i - 2)
                if inter:
                    projection(i - 1, range(0, 4))
                if tail:
                    tail_amplitude(i - 2)
                if inter:
                    projection(i - 1, range(4, 8))
                if tail:
                    tail_amp_t(i - 2)
                    tail_post(i - 2)
                if inter:
                    interference(i - 1, 0)
                if inter:
                    interference(i - 1, 1)
                if tail:
                    tail_z_t(i - 2)
                if att:
                    softmax(i)
                if inter:
                    interference(i - 1, 2)
                if tail:
                    tail_h1_t(i - 2)
                if inter:
                    interference(i - 1, 3)
                    unit_vectors(i - 1, att)
                if att:
                    qkv(i, range(4, 6))
            turns(act, body)

        @block.vector
        def _(dve):
            class Chain:

                def __init__(self, name, per_tile, t):
                    self.sem, self.per, self.t, self.k = S[name], per_tile, t, 0

                def step(self, ins):
                    self.k += 1
                    ins.then_inc(self.sem, 1)
                    return self.k

                def wait(self, k):
                    dve.wait_ge(self.sem, self.t * self.per + k)

            def bias(t, which):
                buf, row = ((q_sb, bq), (k_sb, bk))[which]
                dve.wait_ge(S["qkv_evacuated"], 24 * t + 8 * (which + 1))
                v = buf[:, :, :, :].rearrange("p n r d -> p n (r d)")
                dve.tensor_tensor(v, v, row.unsqueeze(1).broadcast_to([P, N, 2 * D]), ALU.add)\
                   .then_inc(S["biased"], 1)

            def scores(ch, n):
                if n == 0:
                    dve.wait_ge(S["biased"], 2 * ch.t + 2)
                    dve.wait_ge(S["out_ready"], 2 * ch.t)
                halves = [work[:, 2048 * j:2048 * (j + 1)] for j in range(2)]
                for kind in range(2):
                    made = []
                    for j in range(2):
                        if ch.k >= 2:
                            ch.wait(ch.k - 1)
                        qn = q_sb[:, n, :, :] if kind == 0 else q_sb[:, n, ::-1, :]
                        qn = qn.unsqueeze(1).broadcast_to([P, 2, 2, D])
                        km = k_sb[:, 2 * j:2 * j + 2, :, :]
                        made.append(ch.step(dve.tensor_tensor(halves[j].rearrange("p (m r d) -> p m r d", m=2, r=2),
                                                              qn, km, ALU.mult)))
                    for j in range(2):
                        ch.wait(made[j])
                        ch.step(dve.tensor_reduce(
                            sc[:, n, kind, 2 * j:2 * j + 2].rearrange("p m r h -> p (m r h)"),
                            halves[j].rearrange("p (x d) -> p x d", d=HD), AX.X, ALU.add))

            def softmax(t):
                c = Chain("softmax", 8, t)
                dve.wait_ge(S["score"], SCORE_STEPS * t + SCORE_STEPS)
                c.step(dve.tensor_tensor(ar[:, :, :, :], sc[:, :, 0, :, 0, :], sc[:, :, 0, :, 1, :], ALU.add))
                c.step(dve.tensor_tensor(ai[:, :, :, :], sc[:, :, 1, :, 0, :], sc[:, :, 1, :, 1, :], ALU.subtract))
                c.wait(1)
                c.step(dve.tensor_tensor(ar[:, :, :, :], ar[:, :, :, :], ar[:, :, :, :], ALU.mult))
                c.wait(2)
                c.step(dve.tensor_tensor(ai[:, :, :, :], ai[:, :, :, :], ai[:, :, :, :], ALU.mult))
                c.wait(4)
                dve.scalar_tensor_tensor(ar[:, :, :, :].rearrange("p n m h -> p (n m h)"),
                                         ar[:, :, :, :].rearrange("p n m h -> p (n m h)"), EPS_MAG,
                                         ai[:, :, :, :].rearrange("p n m h -> p (n m h)"), ALU.add,
                                         ALU.add).then_inc(S["scored"], 1)
                dve.wait_ge(S["mag_ready"], t + 1)
                c.step(dve.tensor_reduce(mx[:, :, :], mag[:, :, :, :].rearrange("p n m h -> p n h m"), AX.X, ALU.max))
                c.wait(5)
                dve.tensor_tensor(ai[:, :, :, :], mag[:, :, :, :],
                                  mx[:, :, :].unsqueeze(2).broadcast_to([P, N, N, H]),
                                  ALU.subtract).then_inc(S["exp_in"], 1)
                dve.wait_ge(S["exp_ready"], t + 1)
                c.step(dve.tensor_reduce(mx[:, :, :], mag[:, :, :, :].rearrange("p n m h -> p n h m"), AX.X, ALU.add))
                c.wait(6)
                c.step(dve.reciprocal(mx[:, :, :], mx[:, :, :]))
                c.wait(7)
                c.step(dve.tensor_tensor(w_att[:, :, :, :], mag[:, :, :, :],
                                         mx[:, :, :].unsqueeze(2).broadcast_to([P, N, N, H]), ALU.mult))
                c.wait(8)

            def attend(c, t, part):
                if part == 0:
                    dve.wait_ge(S["qkv_evacuated"], 24 * t + 24)
                    dve.wait_ge(S["int_done"], 8 * t)
                halves = [work[:, 2048 * j:2048 * (j + 1)] for j in range(2)]
                for pair in range(2):
                    a, b = [], []
                    for j in range(2):
                        n = 2 * pair + j
                        if pair:
                            c.wait(c.k - 1)
                        elif part and j:
                            dve.wait_ge(S["out_ready"], 2 * t + 1)
                        elif part:
                            c.wait(c.k)
                        vm = v_sb[:, :, part, :].rearrange("p m (h d) -> p m h d", h=H)
                        w = w_att[:, n, :, :].unsqueeze(3).broadcast_to([P, N, H, HD])
                        a.append(c.step(dve.tensor_tensor(halves[j].rearrange("p (m h d) -> p m h d", m=N, h=H),
                                                          vm, w, ALU.mult)))
                    for j in range(2):
                        c.wait(a[j])
                        b.append(c.step(dve.tensor_tensor(halves[j][:, 0:1024], halves[j][:, 0:1024],
                                                          halves[j][:, 1024:2048], ALU.add)))
                    for j in range(2):
                        c.wait(b[j])
                        ins = dve.tensor_tensor(o_sb[:, 2 * pair + j, part, :], halves[j][:, 0:512],
                                                halves[j][:, 512:1024], ALU.add)
                        if pair == 1 and j == 1:
                            ins.then_inc(S["out_ready"], 1)
                        else:
                            c.step(ins)

            def tail_stage(t, n):
                c = Chain("tail", TAIL_STEPS, t)
                c.k = {0: 0, 1: 1, 2: 5, 3: 6}[n]
                if n == 0:
                    dve.wait_ge(S["meas_sq"], 2 * t + 2)
                    dve.tensor_tensor(ta[:, :], ta[:, :], tb[:, :], ALU.add).then_inc(S["amp_sq_ready"], 1)
                    dve.wait_ge(S["x1_loaded"], 16 * t + 16)
                    c.step(dve.tensor_tensor(x1[:, :], x1[:, :], b_top1, ALU.add))
                if n == 1:
                    dve.wait_ge(S["post_done"], t + 1)
                    c.step(dve.scalar_tensor_tensor(ta[:, :], bank[4][:, :], 1.0, post_b, ALU.mult, ALU.add,
                                                    accum_out=small[:, 7:8]))
                    c.wait(2)
                    dve.tensor_scalar(small[:, 2:3], small[:, 7:8], -1.0 / D, None,
                                      ALU.mult).then_inc(S["mean2_ready"], 1)
                    dve.wait_ge(S["std2_ready"], t + 1)
                    c.step(dve.reciprocal(small[:, 1:2], small[:, 0:1]))
                    c.wait(3)
                    c.step(dve.tensor_scalar(tb[:, :], ta[:, :], small[:, 2:3], small[:, 1:2], ALU.add, ALU.mult))
                    c.wait(4)
                    c.step(dve.tensor_tensor(tb[:, :], tb[:, :], post_g, ALU.mult))
                    c.wait(5)
                    dve.tensor_tensor(tb[:, :], tb[:, :], post_be, ALU.add).then_inc(S["pre_gelu"], 1)
                if n == 2:
                    dve.wait_ge(S["topz_done"], t + 1)
                    c.step(dve.tensor_tensor(tb[:, :], bank[5][:, :], x1[:, :], ALU.add))
                    c.wait(6)
                    dve.tensor_scalar(tb[:, :], tb[:, :], 0.0, None, ALU.max).then_inc(S["h1_ready"], 1)
                if n == 3:
                    dve.wait_ge(S["top2_done"], t + 1)
                    c.step(dve.tensor_tensor(ta[:, 0:TOP2], bank[4][:, 0:TOP2], b_top2, ALU.add))
                    c.wait(7)
                    dve.scalar_tensor_tensor(ta[:, TOP2:2 * TOP2], ta[:, 0:TOP2], 0.0, w3, ALU.max, ALU.mult,
                                             accum_out=y_all[:, t:t + 1] if isinstance(t, int) else y_all[:, bass.ds(t, 1)])\
                       .then_inc(S["y_done"], 1)

            def superposition(t):
                c = Chain("phase", PHASE_STEPS, t)
                t0, t1 = work[:, 0:2048], work[:, 2048:4096]
                dve.wait_ge(S["squared"], 2 * t + 2)
                a = c.step(dve.tensor_tensor(t0, t0, t1, ALU.add))
                dve.wait_ge(S["pair_zero_made"], 3 * t)
                c.wait(a)
                dve.tensor_scalar(zero[:, :, :].rearrange("p n d -> p (n d)"), t0, 0.0, None,
                                  ALU.is_equal).then_inc(S["mask_made"], 1)
                dve.wait_ge(S["mask_made"], t + 1)
                dve.tensor_scalar(t0, t0, 1e-37, None, ALU.max).then_inc(S["n2_ready"], 1)
                c.step(dve.tensor_copy(st[:, :], strength[:, t, :, :].rearrange("p i j -> p (i j)") if isinstance(t, int)
                                       else strength[:, bass.ds(t, 1), :, :].rearrange("p a i j -> p (a i j)")))
                dve.wait_ge(S["ysq_ready"], t + 1)
                a = c.step(dve.tensor_tensor(pa[:, :], pa[:, :], t0, ALU.mult))
                c.wait(a)
                a = c.step(dve.scalar_tensor_tensor(t1, pa[:, :], 3.0, t1, ALU.subtract, ALU.mult))
                c.wait(a)
                ri = [ri_sb[:, part, :, :].rearrange("p n d -> p (n d)") for part in range(2)]
                c.step(dve.scalar_tensor_tensor(t0, ri[0], -0.5, t1, ALU.mult, ALU.mult))
                a = c.step(dve.scalar_tensor_tensor(pa[:, :], ri[1], -0.5, t1, ALU.mult, ALU.mult))
                c.wait(a)
                dve.wait_ge(S["pair_zero_made"], 3 * t + 3)
                cos = t0.rearrange("p (n d) -> p n d", n=N)
                sin = pa[:, :].rearrange("p (n d) -> p n d", n=N)
                xx = t1[:, 0:6 * CH].rearrange("p (j d) -> p j d", j=6)
                yy = pb[:, :].rearrange("p (j d) -> p j d", j=6)
                w = pb[:, 0:N * CH].rearrange("p (j d) -> p j d", j=N)
                prod = t1.rearrange("p (r j d) -> p r j d", r=2, j=N)
                for e in range(0, D, CH):
                    cs = slice(e, e + CH)
                    for f, k, apart in PAIRS:
                        c.step(dve.tensor_tensor(xx[:, f:f + k, :], cos[:, 0:k, cs], cos[:, apart:apart + k, cs], ALU.mult))
                        a = c.step(dve.tensor_tensor(yy[:, f:f + k, :], sin[:, 0:k, cs], sin[:, apart:apart + k, cs],
                                                     ALU.mult))
                    c.wait(a)
                    a = c.step(dve.tensor_tensor(xx, xx, yy, ALU.add))
                    c.wait(a)
                    a = c.step(dve.tensor_tensor(xx, xx, pair_zero[:, :, cs], ALU.add))
                    c.wait(a)
                    last = {}
                    for step in range(3):
                        for j in range(N):
                            i = [i for i in range(N) if i != j][step]
                            f = xx[:, PAIR_AT[(min(i, j), max(i, j))], :]
                            s_ij = st[:, N * i + j:N * i + j + 1]
                            if step == 0:
                                ins = dve.tensor_scalar(w[:, j, :], f, s_ij, st[:, (N + 1) * j:(N + 1) * j + 1],
                                                        ALU.mult, ALU.add)
                            else:
                                c.wait(last[j])
                                ins = dve.scalar_tensor_tensor(w[:, j, :], f, s_ij, w[:, j, :], ALU.mult, ALU.add)
                            last[j] = c.step(ins)
                    c.wait(last[3])
                    for part in range(2):
                        a = c.step(dve.tensor_tensor(prod[:, part, :, :], ri_sb[:, part, :, cs], w, ALU.mult))
                    c.wait(a)
                    a = c.step(dve.tensor_tensor(prod[:, :, 0:2, :], prod[:, :, 0:2, :], prod[:, :, 2:4, :], ALU.add))
                    c.wait(a)
                    if e == 0:
                        dve.wait_ge(S["sup_transposed"], t)
                    a = c.step(dve.tensor_tensor(sup[:, :, cs], prod[:, :, 0, :], prod[:, :, 1, :], ALU.add))
                    c.wait(a)
                for part in range(2):
                    a = c.step(dve.scalar_tensor_tensor(t1[:, part * D:(part + 1) * D], sup[:, part, :], 1.0,
                                                        sup[:, part, :], ALU.mult, ALU.mult,
                                                        accum_out=small[:, 3 + part:4 + part]))
                c.wait(a)
                dve.scalar_tensor_tensor(small[:, 4:5], small[:, 3:4], EPS_MAG, small[:, 4:5], ALU.add,
                                         ALU.add).then_inc(S["norm_sq_ready"], 1)
                assert c.k == PHASE_STEPS, c.k

            def norm(t):
                dve.wait_ge(S["norm_root"], t + 1)
                dve.reciprocal(small[:, 6:7], small[:, 5:6]).then_inc(S["norm_ready"], 1)

            dve.wait_ge(S["setup_loaded"], 32)
            dve.wait_ge(S["gathered"], 16 * NT * N)

            def body(i, att, inter, tail):
                if att:
                    bias(i, 0)
                    bias(i, 1)
                    ch = Chain("score", SCORE_STEPS, i)
                    scores(ch, 0)
                if tail:
                    tail_stage(i - 2, 0)
                if att:
                    scores(ch, 1)
                    scores(ch, 2)
                if tail:
                    tail_stage(i - 2, 1)
                if att:
                    scores(ch, 3)
                    assert ch.k == SCORE_STEPS, ch.k
                if tail:
                    tail_stage(i - 2, 2)
                if att:
                    softmax(i)
                if tail:
                    tail_stage(i - 2, 3)
                if inter:
                    superposition(i - 1)
                if att:
                    c = Chain("pv", PV_STEPS, i)
                    attend(c, i, 0)
                if inter:
                    norm(i - 1)
                if att:
                    attend(c, i, 1)
                    assert c.k == PV_STEPS, c.k
            turns(dve, body)

        @block.tensor
        def _(pe):
            pe.wait_ge(S["ident_made"], 1)

            def body(i, att, inter, tail):
                at = [0]

                def next_unit():
                    slot, loaded = place(i, at[0])
                    at[0] += 1
                    pe.wait_ge(w2_loaded[slot], loaded)
                    return w2[:, slot, :].rearrange("p (k c) -> p k c", k=DT)

                def transposes(out, src, name):
                    for k in range(DT):
                        ins = pe.transpose(out[:, k * P:(k + 1) * P], src[:, k * P:(k + 1) * P], ident[:, :])
                    if name:
                        ins.then_inc(S[name], 1)

                def product_of(out, lhs, rhs, name=None, start=True, stop=True):
                    for kt in range(DT):
                        mm = pe.matmul(out, lhs(kt), rhs(kt), start=start and kt == 0, stop=stop and kt == DT - 1)
                    if name:
                        mm.then_inc(S[name], 1)

                def qkv(t, units):
                    for k in units:
                        w = next_unit()
                        if k < 2:
                            pe.wait_ge(s_loaded[k], 16 * t + 16)
                        if k == 0:
                            if not isinstance(t, int) or t:
                                pe.wait_ge(S["qkv_evacuated"], 24 * t - 4)
                        if k == 4:
                            pe.wait_ge(S["int_evacuated"], 8 * t)
                        if k == 5:
                            pe.wait_ge(S["tail"], TAIL_STEPS * (t - 1) if tail else 0)
                        for n in range(N):
                            if k in (1, 2, 3) or k == 4 and not inter:
                                pe.wait_ge(S["qkv_evacuated"], 24 * t + (4 * (k - 1) + n + 1))
                            product_of(qkv_bank(k, n)[:, :], lambda kt: s_in[:, k % 2, DT * n + kt, :],
                                       lambda kt: w[:, kt, :], "qkv_done")

                def interference(t, n):
                    b_r, b_i = bank[2 * (n % 2)][:, :], bank[2 * (n % 2) + 1][:, :]
                    if n == 0:
                        pe.wait_ge(S["a_ready"], 8 * t + 8)
                        pe.wait_ge(S["na_ready"], 4 * t + 4)
                    if n >= 2:
                        pe.wait_ge(S["int_evacuated"], 8 * t + (2 * (n - 2) + 2))
                    rows_n = slice(n * P, (n + 1) * P)
                    w = next_unit()
                    product_of(b_r, lambda kt: a_t[:, 0, kt, rows_n], lambda kt: w[:, kt, :], None, True, False)
                    product_of(b_i, lambda kt: a_t[:, 1, kt, rows_n], lambda kt: w[:, kt, :], "int_done", True, False)
                    w = next_unit()
                    product_of(b_r, lambda kt: na_t[:, kt, rows_n], lambda kt: w[:, kt, :], None, False, True)
                    product_of(b_i, lambda kt: a_t[:, 0, kt, rows_n], lambda kt: w[:, kt, :], "int_done", False, True)

                def tail_stage(t, n):
                    if n == 0:
                        pe.wait_ge(S["sup_t_ready"], 3 * t + 3)
                        pe.wait_ge(S["tail"], TAIL_STEPS * t)
                        w = next_unit()
                        product_of(bank[4][:, :], lambda kt: sup_t[:, 0, kt, :], lambda kt: w[:, kt, :], None, True, False)
                        product_of(bank[5][:, :], lambda kt: sup_t[:, 1, kt, :], lambda kt: w[:, kt, :], "meas_done",
                                   True, False)
                        w = next_unit()
                        product_of(bank[4][:, :], lambda kt: sup_t[:, 2, kt, :], lambda kt: w[:, kt, :], None, False, True)
                        product_of(bank[5][:, :], lambda kt: sup_t[:, 0, kt, :], lambda kt: w[:, kt, :], "meas_done",
                                   False, True)
                    if n == 1:
                        pe.wait_ge(S["amp_ready"], t + 1)
                        transposes(bank[6], tb, "amp_transposed")
                        pe.wait_ge(S["amp_t_ready"], t + 1)
                        w = next_unit()
                        product_of(bank[4][:, :], lambda kt: x_t[:, kt, :], lambda kt: w[:, kt, :], "post_done")
                    if n == 2:
                        pe.wait_ge(S["z_ready"], t + 1)
                        transposes(bank[7], ta, "z_transposed")
                        pe.wait_ge(S["z_t_ready"], t + 1)
                        w = next_unit()
                        product_of(bank[5][:, :], lambda kt: x_t[:, kt, :], lambda kt: w[:, kt, :], "topz_done")
                    if n == 3:
                        pe.wait_ge(S["h1_ready"], t + 1)
                        transposes(bank[6], tb, "h1_transposed")
                        pe.wait_ge(S["h1_t_ready"], t + 1)
                        next_unit()
                        slot = place(i, at[0] - 1)[0]
                        w2t = w2[:, slot, 0:DT * TOP2].rearrange("p (k c) -> p k c", k=DT)
                        product_of(bank[4][:, 0:TOP2], lambda kt: x_t[:, kt, :], lambda kt: w2t[:, kt, :], "top2_done")

                def out_transpose(t):
                    pe.wait_ge(S["qkv_evacuated"], 24 * t + 24)
                    if tail:
                        pe.wait_ge(S["sup_t_ready"], 3 * t)
                    for j in range(8):
                        r, f = j // 4, j % 4
                        if f == 0:
                            pe.wait_ge(S["out_ready"], 2 * t + (r + 1))
                        if j >= 2:
                            pe.wait_ge(S["out_t_ready"], 8 * t + (j - 1))
                        for n in range(N):
                            ins = pe.transpose(bank[6 + j % 2][:, n * P:(n + 1) * P],
                                               o_sb[:, n, r, f * P:(f + 1) * P], ident[:, :])
                        ins.then_inc(S["out_transposed"], 1)

                def projection(t):
                    if att:
                        pe.wait_ge(S["qkv_evacuated"], 24 * t + 40)
                    for r in range(2):
                        w = next_unit()
                        pe.wait_ge(S["out_t_ready"], 8 * t + (4 * r + 4))
                        for mt in range(DT):
                            j = 4 * r + mt
                            if j >= 4:
                                pe.wait_ge(S["a_ready"], 8 * t + (j - 3))
                            product_of(bank[j % 4][:, :], lambda kt: w[:, kt, mt * P:(mt + 1) * P],
                                       lambda kt: out_t[r][:, kt, :], "o_done")

                if att:
                    qkv(i, range(0, 4))
                if tail:
                    pe.wait_ge(S["sup_scaled"], 2 * i - 2)
                    pe.wait_ge(S["qkv_evacuated"], 24 * i if att else 24 * NT)
                    transposes(bank[6], sup[:, 0, :], None)
                    transposes(bank[7], sup[:, 1, :], "sup_transposed")
                if inter:
                    out_transpose(i - 1)
                if tail:
                    tail_stage(i - 2, 0)
                if inter:
                    projection(i - 1)
                if tail:
                    tail_stage(i - 2, 1)
                if inter:
                    interference(i - 1, 0)
                    interference(i - 1, 1)
                if tail:
                    tail_stage(i - 2, 2)
                if inter:
                    interference(i - 1, 2)
                if tail:
                    tail_stage(i - 2, 3)
                if inter:
                    interference(i - 1, 3)
                if att:
                    qkv(i, range(4, 6))
            turns(pe, body)


def kernel(**inputs):
    import numpy as np
    import concourse.bacc as bacc
    from concourse.bass_utils import run_bass_kernel_spmd

    a = {k: np.asarray(v) for k, v in inputs.items()}

    def rec(name):
        return a["L0_rec_" + name]

    def stationary_units(w):
        o, n = w.shape
        return np.ascontiguousarray(w.reshape(o // P, P, n // P, P).transpose(0, 3, 2, 1)).reshape(o // P, P, n)

    def moving_unit(w):
        n, o = w.shape
        u = np.ascontiguousarray(w.reshape(n // P, P, o).transpose(1, 0, 2)).reshape(P, n // P * o)
        return u if u.shape[1] == UNIT else np.pad(u, ((0, 0), (0, UNIT - u.shape[1])))

    units = [rec(n).T for n in ("Wq_r", "Wq_i", "Wk_r", "Wk_i", "Wv_r", "Wv_i", "Wo_r", "Wo_i")]
    for n in range(N):
        units += [rec("int_Wr")[n].T, rec("int_Wi")[n].T]
    units += [rec("meas_Mr").T, rec("meas_Mi").T, rec("post_W").T, a["W_top1"][0:D], a["W_top2"]]
    rows = np.concatenate([rec(n) for n in ("bq_r", "bq_i", "bk_r", "bk_i", "post_b", "post_g", "post_be")]
                          + [a["b_top1"], a["b_top2"], a["W_top3"][:, 0]])
    cols = np.stack([rec(n) for n in ("bv_r", "bv_i", "bo_r", "bo_i")])
    vecs = np.stack([rec(e + k) for e in ("er_", "ei_") for k in ("b1", "g1", "be1", "b2")])
    arrays = {
        "x": np.ascontiguousarray(a["r_x"].reshape(2, HALF, KT, P).transpose(0, 3, 2, 1)),
        "w1r": stationary_units(rec("er_W1")), "w1i": stationary_units(rec("ei_W1")),
        "w2r": stationary_units(rec("er_W2")), "w2i": stationary_units(rec("ei_W2")),
        "wtx": np.stack([moving_unit(a["W_top1"][D + j * D:D + (j + 1) * D]) for j in range(4)]),
        "vecs": np.ascontiguousarray(vecs.reshape(8, KT, P).transpose(2, 0, 1)),
        "ws2": np.stack([moving_unit(w) for w in units]),
        "rows": np.ascontiguousarray(np.broadcast_to(rows, (P, rows.size))),
        "cols": np.ascontiguousarray(cols.reshape(4, DT, P).transpose(2, 0, 1)),
        "ids": np.ascontiguousarray(a["ids"].reshape(NT, P, N).transpose(1, 0, 2)),
        **{f"tbl{f}": np.ascontiguousarray(a[f"tbl_{f}"]) for f in range(N)},
    }
    nc = bacc.Bacc("TRN2", target_bir_lowering=False, num_devices=1)
    dram = {k: nc.dram_tensor(k, v.shape, mybir.dt.from_np(v.dtype), kind="ExternalInput").ap()
            for k, v in arrays.items()}
    dram["s"] = nc.dram_tensor("s", (NT, P, 2, KT, P), F32, kind="Internal").ap()
    dram["t1x"] = nc.dram_tensor("t1x", (NT, P, TOP1), F32, kind="Internal").ap()
    dram["out"] = nc.dram_tensor("out", (P, NT), F32, kind="ExternalOutput").ap()
    encode(nc, dram)
    mix(nc, dram)
    got = run_bass_kernel_spmd(nc, [arrays], core_ids=[0])
    return np.ascontiguousarray(got.results[0]["out"].T).reshape(BATCH, 1)
```

```python
from contextlib import ExitStack

import concourse.bass as bass
from concourse import mybir

ALU = mybir.AluOpType
ACT = mybir.ActivationFunctionType
AX = mybir.AxisListType
F32 = mybir.dt.float32
F32R = mybir.dt.float32r
BF16 = mybir.dt.bfloat16
I32 = mybir.dt.int32

P = 128
BATCH = 1024
IN = 2048
HID = 2048
D = 512
N = 4
H = 8
HD = D // H
TOP1 = 512
TOP2 = 256
NT = BATCH // P
HALF = BATCH // 2
HT = HALF // P
KT = IN // P
DT = D // P
UNIT = KT * P
QC = UNIT // 4
EPS_LN = 1e-5
EPS_MAG = 1e-8

PHASES = [
    dict(kind="G1", job=0),
    dict(kind="G1", job=1, merge=0, ln=0),
    dict(kind="TX", half=0),
    dict(kind="G2", job=0, merge=1, load_x=1),
    dict(kind="G1", job=2, ln=1),
    dict(kind="G2", job=1, merge=2),
    dict(kind="G1", job=3, ln=2),
    dict(kind="G2", job=2, merge=3, normalize=3),
    dict(kind="TX", half=1, ln=3),
    dict(kind="G2", job=3),
]
_unit = _acc = _store = 0
for _p in PHASES:
    _p["units"] = 4 if _p["kind"] == "TX" else KT
    _p["unit"], _p["acc"], _p["store"] = _unit, _acc, _store
    _unit += _p["units"]
    _acc += HT if _p["kind"] == "TX" else KT
    _store += {"G1": 0, "G2": KT, "TX": HT}[_p["kind"]]
UNITS = _unit
STORES = _store


def early_buffers(nc, stack, tag):
    def sb(name, shape, dt=F32):
        return stack.enter_context(nc.sbuf_tensor(name + tag, shape, dt))

    return dict(
        s_in=sb("s_in", [P, 2, KT, P]),
        w2=sb("w2", [P, RING, UNIT]),
        rows=sb("rows_sb", [P, 9 * D]),
        cols=sb("cols_sb", [P, 4, DT]),
        ids=sb("ids_sb", [P, NT, N], I32),
    )


def encode(nc, dram, early, early_loaded):
    with ExitStack() as ctx:
        def sb(name, shape, dt=F32):
            return ctx.enter_context(nc.sbuf_tensor(name, shape, dt))

        def sem(name):
            return ctx.enter_context(nc.semaphore(name))

        x_hi = sb("x_hi", [P, KT, HALF], F32R)
        x_lo = sb("x_lo", [P, KT, HALF], F32R)
        h_hi = sb("h_hi", [P, KT, HALF], F32R)
        h_lo = sb("h_lo", [P, KT, HALF], F32R)
        raw = sb("raw", [P, KT, HALF])
        w_raw = sb("w_raw", [P, 2, UNIT])
        w_hi = sb("w_hi", [P, 4, QC], F32R)
        w_lo = sb("w_lo", [P, 4, QC], F32R)
        lane_sum = sb("lane_sum", [P, HALF])
        lane_sq = sb("lane_sq", [P, HALF])
        rstd = sb("rstd", [P, HALF])
        dev = sb("dev", [P, HALF])
        stage = sb("stage", [P, 2, HALF])
        x_stage = sb("x_stage", [P, HALF])
        ones = sb("ones", [P, P])
        eps = sb("eps", [P, 1])
        vecs = sb("features", [P, 8, KT])

        bank = [ctx.enter_context(nc.psum_tensor(f"bank{i}", [P, 512], F32)) for i in range(8)]
        mean_bank, gelu_bank, sq_bank = bank[2], [bank[3], bank[6]], bank[7]
        tx_banks = [bank[0], bank[1], bank[4], bank[5]]

        w_loaded = [sem(f"w_loaded{i}") for i in range(2)]
        wh_ready = sem("wh_ready")
        wl_ready = sem("wl_ready")
        w_used = sem("w_used")
        x0_loaded = [sem(f"x0_loaded{i}") for i in range(4)]
        x_loaded = sem("x_loaded")
        xh_ready = sem("xh_ready")
        xl_ready = sem("xl_ready")
        consts = sem("consts")
        vecs_loaded = sem("vecs_loaded")
        acc_evacuated = sem("acc_evacuated")
        stored = [sem(f"stored{i}") for i in range(2)]
        dev_ready = sem("dev_ready")
        sq_ready = sem("sq_ready")
        stat_done = sem("stat_done")
        merge = sem("merge")
        lane_mean_ready = sem("lane_mean_ready")
        lane_var_ready = sem("lane_var_ready")
        mean_ready = sem("mean_ready")
        var_ready = sem("var_ready")
        std_ready = sem("std_ready")
        centered = sem("centered")
        ln_scaled = sem("ln_scaled")
        ln_gelu = sem("ln_gelu")
        ln_hi = sem("ln_hi")
        ln_lo = sem("ln_lo")

        B1, G, BE, B2 = range(4)
        last_g2 = {}
        end = 0
        for ph in PHASES:
            if ph.get("ln") is not None:
                last_g2[ph["ln"]] = end
            if ph["kind"] == "G2":
                end = ph["unit"] + ph["units"]
        tx0_end = PHASES[2]["unit"] + PHASES[2]["units"]

        def steps(eng, ph, body):
            pairs = ph["units"] // 2
            if ph["kind"] == "TX":
                for i in range(pairs):
                    for e in range(2):
                        body(i, e, i == 0, False)
                return
            final = ph is PHASES[-1]
            for e in range(2):
                body(0, e, True, False)
            with eng.Fori(1, pairs - final) as i:
                for e in range(2):
                    body(i, e, False, False)
            if final:
                for e in range(2):
                    body(pairs - 1, e, False, True)

        def slab(t, i):
            return t[:, i, :] if isinstance(i, int) else t[:, bass.ds(i, 1), :].rearrange("p a c -> p (a c)")

        def col(k, enc, i):
            j = 4 * enc + k
            return vecs[:, j, i:i + 1] if isinstance(i, int) else vecs[:, j, bass.ds(i, 1)]

        block = ctx.enter_context(nc.Block())

        @block.sync
        def _(sp):
            for c in range(4):
                sp.dma_start(raw[:, 4 * c:4 * c + 4, :], dram["x"][0, :, 4 * c:4 * c + 4, :]).then_inc(x0_loaded[c], 16)
                if c < 2:
                    sp.dma_start(w_raw[:, c, :], dram["w1r"][c, :, :]).then_inc(w_loaded[c], 16)
                if c == 2:
                    sp.dma_start(vecs[:, :, :], dram["vecs"]).then_inc(vecs_loaded, 16)
            for ph in PHASES:
                name = "wtx" if ph["kind"] == "TX" else ("w1" if ph["kind"] == "G1" else "w2") + "ri"[ph["job"] % 2]

                def load(i, e, first, last, ph=ph, name=name):
                    if ph is PHASES[0] and first:
                        return
                    sp.wait_ge(wl_ready, 8 * i + (4 * (ph["unit"] + e) - 4))
                    src = dram[name]
                    m = 2 * i + e
                    src = src[m, :, :] if isinstance(m, int) else src[bass.ds(m, 1), :, :].rearrange("a p c -> p (a c)")
                    sp.dma_start(w_raw[:, e, :], src).then_inc(w_loaded[e], 16)
                    if last and e == 1:
                        sp.wait_ge(w_used, 4 * ph["unit"])
                        for part in range(2):
                            sp.wait_ge(stored[part], 16 * (PHASES[5]["store"] + KT) // 2)
                        for part in range(2):
                            sp.dma_start(early["s_in"][:, part, :, :], dram["s"][0, :, part])\
                              .then_inc(early_loaded["s"][part], 16)
                            sp.dma_start(early["w2"][:, part, :], dram["ws2"][part, :, :])\
                              .then_inc(early_loaded["w2"][part], 16)
                        sp.dma_start(early["w2"][:, 2, :], dram["ws2"][2, :, :]).then_inc(early_loaded["w2"][2], 16)
                        for name in ("rows", "cols", "ids"):
                            dst = early[name][:, :] if name == "rows" else early[name][:, :, :]
                            sp.dma_start(dst, dram[name]).then_inc(early_loaded[name], 16)
                    if ph.get("load_x"):
                        sp.wait_ge(xl_ready, 2 * i + (KT + e))
                        xs = dram["x"][ph["load_x"]]
                        xs = xs[:, m, :] if isinstance(m, int) else xs[:, bass.ds(m, 1), :].rearrange("p a c -> p (a c)")
                        sp.dma_start(x_stage[:, :], xs).then_inc(x_loaded, 16)
                steps(sp, ph, load)

        @block.gpsimd
        def _(pool):
            pool.memset(ones[:, :], 1.0 / P).then_inc(consts, 1)
            pool.memset(eps[:, :], EPS_LN).then_inc(consts, 1)

        @block.scalar
        def _(act):
            def split_w(u_half, slot, u_base, i, q, first_unit=False):
                if q == 0:
                    act.wait_ge(w_loaded[slot], 16 * i + 16 * (u_base // 2 + 1))
                if not first_unit:
                    act.wait_ge(w_used, 8 * i + (4 * u_base + q - 3))
                act.copy(w_hi[:, q, :], w_raw[:, slot, q * QC:(q + 1) * QC]).then_inc(wh_ready, 1)

            def gelu_tile(ln, t, c, odd):
                act.wait_ge(ln_scaled, c + 1)
                if not (isinstance(c, int) and c < 2):
                    act.wait_ge(ln_lo, c - 1)
                act.activation(gelu_bank[odd][:, :], slab(raw, t), ACT.Gelu, bias=col(BE, ln % 2, t),
                               scale=col(G, ln % 2, t)).then_inc(ln_gelu, 1)

            def hi_tile(t, c, odd):
                act.wait_ge(ln_gelu, c + 1)
                act.copy(slab(h_hi, t), gelu_bank[odd][:, :]).then_inc(ln_hi, 1)

            def std(ln):
                act.wait_ge(var_ready, ln + 1)
                act.activation(rstd[:, :], sq_bank[:, :], ACT.Sqrt, bias=eps[:, :]).then_inc(std_ready, 1)

            act.wait_ge(consts, 2)
            for kt in range(4):
                if kt % 4 == 0:
                    act.wait_ge(x0_loaded[kt // 4], 16)
                act.copy(x_hi[:, kt, :], raw[:, kt, :]).then_inc(xh_ready, 1)
            split_w(0, 0, 0, 0, 0, True)
            for kt in range(4, KT):
                if kt % 4 == 0:
                    act.wait_ge(x0_loaded[kt // 4], 16)
                act.copy(x_hi[:, kt, :], raw[:, kt, :]).then_inc(xh_ready, 1)
                if kt % 4 == 3:
                    split_w(0, 0, 0, 0, kt // 4, True)
            act.wait_ge(vecs_loaded, 16)
            for ph in PHASES:
                ln, merge_of = ph.get("ln"), ph.get("merge")

                def step(i, e, first, last, ph=ph, ln=ln, merge_of=merge_of):
                    u, m = ph["unit"] + e, 2 * i + e
                    more = not (last and e == 1)

                    def hi(q):
                        if more:
                            split_w(0, (e + 1) % 2, u + 1, i, q)
                    hi(0)
                    if ln is not None and first and e == 0:
                        if merge_of is not None:
                            std(merge_of)
                        if last_g2[ln]:
                            act.wait_ge(w_used, 4 * last_g2[ln])
                    if ph["kind"] == "TX":
                        for j in range(4):
                            if ln is not None:
                                t = 4 * m + j
                                gelu_tile(ln, t, KT * ln + t, t % 2)
                                hi_tile(t, KT * ln + t, t % 2)
                            if j < 3:
                                hi(j + 1)
                    else:
                        if ln is not None:
                            gelu_tile(ln, m, m + KT * ln, e)
                        hi(1)
                        if ln is not None:
                            hi_tile(m, m + KT * ln, e)
                        hi(2)
                    if ph.get("load_x"):
                        if first and e == 0:
                            act.wait_ge(w_used, 4 * tx0_end)
                        act.wait_ge(x_loaded, 32 * i + 16 * (e + 1))
                        act.copy(slab(x_hi, m), x_stage[:, :]).then_inc(xh_ready, 1)
                    if ph["kind"] == "TX":
                        if m == 3:
                            for bt in range(HT):
                                z = ph["store"] + bt
                                if bt == 0:
                                    act.wait_ge(w_used, 4 * (ph["unit"] + 4))
                                if z >= 2:
                                    act.wait_ge(stored[z % 2], 16 * (z // 2))
                                act.copy(stage[:, z % 2, :], tx_banks[bt][:, :]).then_inc(acc_evacuated, 1)
                                act.wait_ge(acc_evacuated, ph["acc"] + bt + 1)
                                act.dma_start(dram["t1x"][HT * ph["half"] + bt], stage[:, z % 2, :])\
                                   .then_inc(stored[z % 2], 16)
                        return
                    enc, half = ph["job"] % 2, ph["job"] // 2
                    a = ph["acc"] + e
                    act.wait_ge(w_used, 8 * i + (4 * u + 4))
                    if ph["kind"] == "G1":
                        if ph is PHASES[0] and first and e == 0:
                            act.wait_ge(xl_ready, KT)
                        act.activation(slab(raw, m), bank[e][:, :], ACT.Identity,
                                       bias=col(B1, enc, m)).then_inc(acc_evacuated, 1)
                        hi(3)
                        c = KT * ph["job"] + e
                        act.wait_ge(dev_ready, 2 * i + (c + 1))
                        act.wait_ge(stat_done, 2 * i + c)
                        act.activation(sq_bank[:, :], dev[:, :], ACT.Square).then_inc(sq_ready, 1)
                    else:
                        z = ph["store"] + e
                        if not (isinstance(i, int) and z + 2 * i < 2):
                            act.wait_ge(stored[e], 16 * i + 16 * (z // 2))
                        act.activation(stage[:, e, :], bank[e][:, :], ACT.Identity,
                                       bias=col(B2, enc, m)).then_inc(acc_evacuated, 1)
                        hi(3)
                        act.wait_ge(acc_evacuated, 2 * i + (a + 1))
                        dst = dram["s"][HT * half:HT * half + HT, :, enc]
                        dst = dst[:, :, m, :].rearrange("t p c -> p t c") if isinstance(m, int) else \
                            dst[:, :, bass.ds(m, 1), :].rearrange("t p a c -> p t (a c)")
                        act.dma_start(dst, stage[:, e, :].rearrange("p (t c) -> p t c", t=HT)).then_inc(stored[e], 16)
                        if merge_of is not None and first and e == 1:
                            std(merge_of)
                steps(act, ph, step)
            for z in range(2):
                act.wait_ge(stored[z], 16 * (STORES // 2))

        @block.vector
        def _(dve):
            link_count = [0]

            def link(ins):
                link_count[0] += 1
                ins.then_inc(merge, 1)
                dve.wait_ge(merge, link_count[0])

            def lo_w(slot, u_base, i, q):
                dve.wait_ge(wh_ready, 8 * i + (4 * u_base + q + 1))
                dve.tensor_tensor(w_lo[:, q, :], w_raw[:, slot, q * QC:(q + 1) * QC], w_hi[:, q, :],
                                  ALU.subtract).then_inc(wl_ready, 1)

            def lo_x(i, src, c):
                dve.wait_ge(xh_ready, c + 1)
                dve.tensor_tensor(slab(x_lo, i), src, slab(x_hi, i), ALU.subtract).then_inc(xl_ready, 1)

            def merge_lanes(job, parts=range(4)):
                if 0 in parts:
                    dve.wait_ge(stat_done, KT * (job + 1))
                    link(dve.tensor_tensor(dev[:, :], lane_sum[:, :], lane_sum[:, :], ALU.mult))
                    dve.scalar_tensor_tensor(lane_sum[:, :], lane_sum[:, :], 1.0 / KT, raw[:, 0, :], ALU.mult,
                                             ALU.add).then_inc(lane_mean_ready, 1)
                if 1 in parts:
                    link(dve.scalar_tensor_tensor(lane_sq[:, :], dev[:, :], -1.0 / KT, lane_sq[:, :], ALU.mult,
                                                  ALU.add))
                    dve.wait_ge(mean_ready, job + 1)
                    link(dve.tensor_tensor(dev[:, :], lane_sum[:, :], mean_bank[:, :], ALU.subtract))
                if 2 in parts:
                    link(dve.tensor_tensor(dev[:, :], dev[:, :], dev[:, :], ALU.mult))
                    dve.scalar_tensor_tensor(lane_sq[:, :], lane_sq[:, :], 1.0 / KT, dev[:, :], ALU.mult,
                                             ALU.add).then_inc(lane_var_ready, 1)
                if 3 in parts:
                    dve.wait_ge(std_ready, job + 1)
                    dve.memset(lane_sum[:, :], 0.0)
                    dve.memset(lane_sq[:, :], 0.0)
                    link(dve.reciprocal(rstd[:, :], rstd[:, :]))

            def normalize(t, c):
                dve.tensor_tensor(slab(raw, t), slab(raw, t), mean_bank[:, :], ALU.subtract).then_inc(centered, 1)
                dve.wait_ge(centered, c + 1)
                dve.tensor_tensor(slab(raw, t), slab(raw, t), rstd[:, :], ALU.mult).then_inc(ln_scaled, 1)

            def lo_tile(t, c, odd):
                dve.wait_ge(ln_hi, c + 1)
                dve.tensor_tensor(slab(h_lo, t), gelu_bank[odd][:, :], slab(h_hi, t), ALU.subtract).then_inc(ln_lo, 1)

            dve.memset(lane_sum[:, :], 0.0)
            link(dve.memset(lane_sq[:, :], 0.0))
            for kt in range(KT):
                lo_x(kt, raw[:, kt, :], kt)
                if kt % 4 == 3:
                    lo_w(0, 0, 0, kt // 4)
            for ph in PHASES:
                ln, merge_of = ph.get("ln"), ph.get("merge")

                def step(i, e, first, last, ph=ph, ln=ln, merge_of=merge_of):
                    u, m = ph["unit"] + e, 2 * i + e

                    def lo(q):
                        if not (last and e == 1):
                            lo_w((e + 1) % 2, u + 1, i, q)
                    lo(0)
                    if merge_of is not None and ln is not None and first and e == 0:
                        merge_lanes(merge_of)
                    spread = merge_of is not None and ln is None and first
                    if spread:
                        merge_lanes(merge_of, [0] if e == 0 else [2])
                    behind = ph.get("normalize")
                    if behind is not None and not first:
                        normalize(m - 2, m + (KT * behind - 2))
                    if ph["kind"] == "TX":
                        for j in range(4):
                            if ln is not None:
                                t = 4 * m + j
                                if t < 2:
                                    normalize(KT - 2 + t, KT * (ln + 1) - 2 + t)
                                lo_tile(t, KT * ln + t, t % 2)
                            if j < 3:
                                lo(j + 1)
                        return
                    if ln is not None:
                        normalize(m, m + KT * ln)
                    lo(1)
                    if ln is not None:
                        lo_tile(m, m + KT * ln, e)
                    lo(2)
                    if ph.get("load_x"):
                        lo_x(m, x_stage[:, :], m + KT)
                    lo(3)
                    if spread:
                        merge_lanes(merge_of, [1] if e == 0 else [3])
                    if ph["kind"] == "G1":
                        c = KT * ph["job"] + e
                        dve.wait_ge(acc_evacuated, 2 * i + (ph["acc"] + e + 1))
                        dve.wait_ge(stat_done, 2 * i + c)
                        dve.tensor_tensor(dev[:, :], slab(raw, m), raw[:, 0, :], ALU.subtract).then_inc(dev_ready, 1)
                        dve.wait_ge(dev_ready, 2 * i + (c + 1))
                        dve.tensor_tensor(lane_sum[:, :], lane_sum[:, :], dev[:, :], ALU.add)
                        dve.wait_ge(sq_ready, 2 * i + (c + 1))
                        dve.tensor_tensor(lane_sq[:, :], lane_sq[:, :], sq_bank[:, :], ALU.add).then_inc(stat_done, 1)
                steps(dve, ph, step)

        @block.tensor
        def _(pe):
            pe.wait_ge(consts, 2)
            for ph in PHASES:
                ln, merge_of = ph.get("ln"), ph.get("merge")

                def step(i, e, first, last, ph=ph, ln=ln, merge_of=merge_of):
                    u, m = ph["unit"] + e, 2 * i + e
                    start = first and i == 0 and e == 0
                    if ph["kind"] == "TX":
                        if start:
                            pe.wait_ge(acc_evacuated, ph["acc"])
                    else:
                        half = ph["job"] // 2
                        a = ph["acc"] + e
                        if not (isinstance(i, int) and a + 2 * i < 2):
                            pe.wait_ge(acc_evacuated, 2 * i + (a - 1))
                        hi, lo = (x_hi, x_lo) if ph["kind"] == "G1" else (h_hi, h_lo)
                    for q in range(4):
                        pe.wait_ge(wl_ready, 8 * i + (4 * u + q + 1))
                        if start and ph["kind"] == "G1":
                            pe.wait_ge(xl_ready, KT * half + 4 * q + 4)
                        if start and ph["kind"] == "G2":
                            pe.wait_ge(ln_lo, KT * ph["job"] + 4 * q + 4)
                        for j in range(4):
                            kt = 4 * q + j
                            if ph["kind"] == "TX":
                                kt = 4 * m + q
                                out, rows = tx_banks[j][:, :], slice(j * P, (j + 1) * P)
                                args = ((x_hi[:, kt, rows], w_hi[:, q, :]), (x_lo[:, kt, rows], w_hi[:, q, :]),
                                        (x_hi[:, kt, rows], w_lo[:, q, :]))
                            else:
                                out, cols = bank[e][:, :], slice(j * P, (j + 1) * P)
                                args = ((w_hi[:, q, cols], hi[:, kt, :]), (w_hi[:, q, cols], lo[:, kt, :]),
                                        (w_lo[:, q, cols], hi[:, kt, :]))
                            for k, (a_, b_) in enumerate(args):
                                mm = pe.matmul(out, a_, b_, start=(kt == 0 and k == 0), stop=(kt == KT - 1 and k == 2))
                        mm.then_inc(w_used, 1)
                        at_once = ln is not None
                        if merge_of is not None and first and (e, q) == ((0, 0) if at_once else (0, 2)):
                            pe.wait_ge(lane_mean_ready, merge_of + 1)
                            pe.matmul(mean_bank[:, :], ones[:, :], lane_sum[:, :], start=True, stop=True)\
                              .then_inc(mean_ready, 1)
                        if merge_of is not None and first and (e, q) == ((0, 2) if at_once else (1, 2)):
                            pe.wait_ge(lane_var_ready, merge_of + 1)
                            pe.matmul(sq_bank[:, :], ones[:, :], lane_sq[:, :], start=True, stop=True)\
                              .then_inc(var_ready, 1)
                steps(pe, ph, step)


QKV, WO, INT, MEAS, POST, TOPZ, TOP2W = 0, 6, 8, 16, 18, 19, 20
UNITS2 = 21
TURN = [
    ("att", range(QKV, QKV + 4)),
    ("tail", [MEAS, MEAS + 1]),
    ("inter", [WO, WO + 1]),
    ("tail", [POST]),
    ("inter", range(INT, INT + 4)),
    ("tail", [TOPZ]),
    ("inter", range(INT + 4, INT + 6)),
    ("tail", [TOP2W]),
    ("inter", range(INT + 6, INT + 8)),
    ("att", range(QKV + 4, QKV + 6)),
]
RING = 3


def turn_units(i):
    parts = dict(att=i is None or i < NT, inter=i is None or 1 <= i <= NT, tail=i is None or i >= 2)
    turn = TURN
    if i == NT - 1:
        turn = [TURN[0], TURN[-1]] + TURN[1:5] + TURN[6:9:2] + TURN[5:9:2]
    elif i == NT:
        turn = [p for p in TURN if p[0] != "tail"] + [p for p in TURN if p[0] == "tail"]
    return [u for part, units in turn for u in units if parts[part]]


PAIRS = [(0, 3, 1), (3, 2, 2), (5, 1, 3)]
PAIR_AT = {}
for _f, _c, _a in PAIRS:
    for _i in range(_c):
        PAIR_AT[(_i, _i + _a)] = _f + _i
CH = 256
SCORE_STEPS, PV_STEPS, TAIL_STEPS, PHASE_STEPS = 32, 22, 7, 56


def mix(nc, dram, early, early_loaded):
    with ExitStack() as ctx:
        def sb(name, shape, dt=F32):
            return ctx.enter_context(nc.sbuf_tensor(name, shape, dt))

        def sem(name):
            return ctx.enter_context(nc.semaphore(name))

        early_buffers(nc, ctx, "_place")
        s_in, w2, rows, cols, ids = (early[k] for k in ("s_in", "w2", "rows", "cols", "ids"))
        q_sb = sb("q_sb", [P, N, 2, D])
        k_sb = sb("k_sb", [P, N, 2, D])
        v_sb = sb("v_sb", [P, N, 2, D])
        work = sb("work", [P, 4096])
        a_t = sb("a_t", [P, 2, DT, D])
        na_t = sb("na_t", [P, DT, D])
        ri_sb = sb("ri_sb", [P, 2, N, D])
        pa = sb("pa", [P, N * D])
        pb = sb("pb", [P, 6 * CH])
        zero = sb("zero", [P, N, D], BF16)
        pair_zero = sb("pair_zero", [P, 6, D], BF16)
        sup = sb("sup", [P, 2, D])
        sup_t = sb("sup_t", [P, 3, DT, P])
        x_t = sb("x_t", [P, DT, P])
        ta = sb("ta", [P, D])
        tb = sb("tb", [P, D])
        x1 = sb("x1", [P, TOP1])
        ident = sb("ident", [P, P])
        strength = sb("strength", [P, NT, N, N])
        st = sb("st", [P, N * N])
        sc = pb[:, 0:512].rearrange("p (n k m r h) -> p n k m r h", n=N, k=2, m=N, r=2)
        ar, ai, mag = (pb[:, 512 + 128 * j:640 + 128 * j].rearrange("p (n m h) -> p n m h", n=N, m=N)
                       for j in range(3))
        w_att = sb("w_att", [P, N, N, H])
        mx = sb("mx", [P, N, H])
        small = sb("small", [P, 8])
        eps2 = sb("eps2", [P, 1])
        y_all = sb("y_all", [P, NT])
        bank = [ctx.enter_context(nc.psum_tensor(f"bank2_{i}", [P, 512], F32)) for i in range(8)]

        o_sb = a_t[:, :, :, :].rearrange("p r f c -> p (r f c)").rearrange("p (n r d) -> p n r d", n=N, r=2)
        out_t = [na_t[:, :, :], pa[:, :].rearrange("p (f c) -> p f c", f=DT)]
        bq, bk = rows[:, 0:1024], rows[:, 1024:2048]
        post_b, post_g, post_be = (rows[:, 2048 + D * j:2048 + D * (j + 1)] for j in range(3))
        b_top1, b_top2, w3 = rows[:, 3584:4096], rows[:, 4096:4352], rows[:, 4352:4608]

        w2_loaded, s_loaded = early_loaded["w2"], early_loaded["s"]
        names = """x1_loaded consts2 gathered ident_made
            qkv_done qkv_evacuated biased score scored softmax mag_ready exp_in exp_ready pv out_ready
            out_transposed out_t_ready o_done a_ready na_ready int_done int_evacuated
            squared n2_ready mask_made pair_zero_made ln_ready y_ready ysq_ready phase norm_root norm_sq_ready
            norm_ready sup_ready sup_scaled sup_transposed sup_t_ready meas_done meas_sq amp_sq_ready amp_ready
            amp_transposed amp_t_ready post_done tail mean2_ready var2_ready std2_ready pre_gelu z_ready
            z_transposed z_t_ready topz_done h1_ready h1_transposed h1_t_ready top2_done y_done
            y_stored""".split()
        S = {n: sem("m_" + n) for n in names}

        def turns(eng, body):
            body(0, True, False, False)
            body(1, True, True, False)
            body(2, True, True, True)
            with eng.Fori(3, NT - 1) as i:
                body(i, True, True, True)
            body(NT - 1, True, True, True)
            body(NT, False, True, True)
            body(NT + 1, False, False, True)

        def first_unit(i):
            return {0: 0, 1: 6, 2: 22, NT - 1: 22 + UNITS2 * (NT - 3), NT: 22 + UNITS2 * (NT - 2), NT + 1: 22 + UNITS2 * (NT - 2) + 15}[i]

        def place(i, k):
            if isinstance(i, int):
                u = first_unit(i) + k
                return u % RING, 16 * (u // RING + 1)
            k += 22 - 2 * UNITS2
            return k % RING, (16 * UNITS2 // RING) * i + 16 * (k // RING + 1)

        def product(i, unit):
            if unit < WO:
                return S["qkv_done"], 24 * i + 4 * (unit - QKV + 1)
            if unit < INT:
                return S["o_done"], 8 * i + (4 * (unit - WO + 1) - 8)
            if unit < MEAS:
                return S["int_done"], 8 * i + (unit - INT + 1 - 8)
            if unit < POST:
                return S["meas_done"], 2 * i + (unit - MEAS + 1 - 4)
            return S[{POST: "post_done", TOPZ: "topz_done", TOP2W: "top2_done"}[unit]], i - 1

        def units_of(i):
            return turn_units(i if isinstance(i, int) else None)

        def is_last(i):
            return isinstance(i, int) and i == NT - 1

        def closing(i):
            return isinstance(i, int) and i == NT

        def out_of(t, n, part):
            return (q_sb if is_last(t) else o_sb)[:, n, part, :]

        def out_t_of(t, part):
            if not is_last(t):
                return out_t[part]
            return k_sb[:, 2 * part:2 * part + 2, :, :].rearrange("p n r d -> p (n r) d")

        def ri_of(t):
            return v_sb[:, :, :, :].rearrange("p n r d -> p (n r d)").rearrange("p (r n d) -> p r n d", r=2, n=N) \
                if is_last(t) else ri_sb

        def qkv_bank(k, n):
            return bank[(4 if k == 5 else 0) + n]

        block = ctx.enter_context(nc.Block())

        @block.sync
        def _(sp):
            def body(i, att, inter, tail):
                units = units_of(i)
                before = [] if isinstance(i, int) and i == 0 else units_of(i - 1)

                def load_s(t, part):
                    src = dram["s"]
                    src = src[t, :, part] if isinstance(t, int) else \
                        src[bass.ds(t, 1), :, part].rearrange("t p m c -> p (t m) c")
                    sp.dma_start(s_in[:, part, :, :], src).then_inc(s_loaded[part], 16)
                for k, unit in enumerate(units):
                    if k < RING and not before:
                        continue
                    slot, _ = place(i, k)
                    if k >= RING:
                        sp.wait_ge(*product(i, units[k - RING]))
                    else:
                        sp.wait_ge(*product(i - 1, before[k - RING]))
                    if unit in (QKV + 1, QKV + 2) and not (isinstance(i, int) and i == 0):
                        part = unit - QKV - 1
                        sp.wait_ge(S["qkv_done"], 24 * i - (4 if part == 0 else 0))
                        load_s(i, part)
                    size = DT * TOP2 if unit == TOP2W else UNIT
                    sp.dma_start(w2[:, slot, 0:size], dram["ws2"][unit, :, 0:size]).then_inc(w2_loaded[slot], 16)
                    if unit == MEAS:
                        sp.wait_ge(S["tail"], TAIL_STEPS * (i - 2))
                        src = dram["t1x"]
                        src = src[i - 2] if isinstance(i, int) else \
                            src[bass.ds(i - 2, 1)].rearrange("a p c -> p (a c)")
                        sp.dma_start(x1[:, :], src).then_inc(S["x1_loaded"], 16)
            turns(sp, body)
            sp.wait_ge(S["y_done"], NT)
            sp.dma_start(dram["out"], y_all[:, :]).then_inc(S["y_stored"], 16)
            sp.wait_ge(S["y_stored"], 16)

        @block.gpsimd
        def _(pool):
            pool.memset(eps2[:, :], EPS_LN).then_inc(S["consts2"], 1)
            pool.memset(ident[:, :], 0.0).then_inc(S["consts2"], 1)
            pool.wait_ge(S["consts2"], 2)
            pool.affine_select(out=ident[:, :], in_=ident[:, :], compare_op=ALU.not_equal, fill=1.0, base=0,
                               pattern=[[-1, P]], channel_multiplier=1).then_inc(S["ident_made"], 1)
            pool.wait_ge(early_loaded["ids"], 16)
            for t in range(NT):
                for f in range(N):
                    pool.indirect_dma_start(strength[:, t, f, :], None, dram[f"tbl{f}"],
                                            bass.IndirectOffsetOnAxis(ap=ids[:, t, f:f + 1], axis=0))\
                        .then_inc(S["gathered"], 16)

            def body(i, att, inter, tail):
                if not inter:
                    return
                pool.wait_ge(S["mask_made"], i)
                for f, c, apart in PAIRS:
                    last = pool.tensor_tensor(pair_zero[:, f:f + c, :], zero[:, 0:c, :],
                                              zero[:, apart:apart + c, :], ALU.add)
                    last.then_inc(S["pair_zero_made"], 1)
            turns(pool, body)

        @block.scalar
        def _(act):
            act.wait_ge(S["consts2"], 2)
            act.wait_ge(early_loaded["cols"], 16)

            def qkv(t, units):
                for k in units:
                    dst = (q_sb, k_sb, v_sb)[k // 2]
                    if k == 0:
                        act.wait_ge(S["score"], SCORE_STEPS * t)
                    if k == 4:
                        act.wait_ge(S["out_ready"], 2 * t)
                    for n in range(N):
                        act.wait_ge(S["qkv_done"], 24 * t + (4 * k + n + 1))
                        act.copy(dst[:, n, k % 2, :], qkv_bank(k, n)[:, :]).then_inc(S["qkv_evacuated"], 1)

            def interference(t, n):
                act.wait_ge(S["int_done"], 8 * t + (2 * n + 2))
                if n == 0 and not is_last(t):
                    act.wait_ge(S["norm_ready"], t)
                for part in range(2):
                    act.copy(ri_of(t)[:, part, n, :], bank[2 * (n % 2) + part][:, :]).then_inc(S["int_evacuated"], 1)

            def sup_transpose(t):
                act.wait_ge(S["sup_transposed"], t + 1)
                act.copy(sup_t[:, 0].rearrange("p k c -> p (k c)"), bank[6][:, :]).then_inc(S["sup_t_ready"], 1)
                act.copy(sup_t[:, 1].rearrange("p k c -> p (k c)"), bank[7][:, :]).then_inc(S["sup_t_ready"], 1)
                act.mul(sup_t[:, 2].rearrange("p k c -> p (k c)"), bank[7][:, :], -1.0).then_inc(S["sup_t_ready"], 1)

            def tail_squares(t):
                act.wait_ge(S["meas_done"], 2 * t + 2)
                act.wait_ge(S["y_done"], t)
                act.activation(ta[:, :], bank[4][:, :], ACT.Square).then_inc(S["meas_sq"], 1)
                act.activation(tb[:, :], bank[5][:, :], ACT.Square).then_inc(S["meas_sq"], 1)

            def tail_amplitude(t):
                act.wait_ge(S["amp_sq_ready"], t + 1)
                act.activation(tb[:, :], ta[:, :], ACT.Sqrt).then_inc(S["amp_ready"], 1)

            def tail_amp_t(t):
                act.wait_ge(S["amp_transposed"], t + 1)
                act.copy(x_t[:, :, :].rearrange("p k c -> p (k c)"), bank[6][:, :]).then_inc(S["amp_t_ready"], 1)

            def tail_post(t):
                act.wait_ge(S["mean2_ready"], t + 1)
                act.activation(tb[:, :], ta[:, :], ACT.Square, bias=small[:, 2:3],
                               accum_out=small[:, 1:2]).then_inc(S["var2_ready"], 1)
                act.wait_ge(S["var2_ready"], t + 1)
                act.activation(small[:, 0:1], small[:, 1:2], ACT.Sqrt, bias=eps2[:, :],
                               scale=1.0 / D).then_inc(S["std2_ready"], 1)
                act.wait_ge(S["pre_gelu"], t + 1)
                act.activation(ta[:, :], tb[:, :], ACT.Gelu).then_inc(S["z_ready"], 1)

            def tail_z_t(t):
                act.wait_ge(S["z_transposed"], t + 1)
                act.copy(x_t[:, :, :].rearrange("p k c -> p (k c)"), bank[7][:, :]).then_inc(S["z_t_ready"], 1)

            def tail_h1_t(t):
                act.wait_ge(S["h1_transposed"], t + 1)
                act.copy(x_t[:, :, :].rearrange("p k c -> p (k c)"), bank[6][:, :]).then_inc(S["h1_t_ready"], 1)

            def softmax(t):
                act.wait_ge(S["scored"], t + 1)
                act.activation(mag[:, :, :, :], ar[:, :, :, :], ACT.Sqrt).then_inc(S["mag_ready"], 1)
                act.wait_ge(S["exp_in"], t + 1)
                act.activation(mag[:, :, :, :], ai[:, :, :, :], ACT.Exp, scale=HD ** -0.5).then_inc(S["exp_ready"], 1)

            def out_transpose(t):
                act.wait_ge(S["int_done"], 8 * t)
                for j in range(8):
                    act.wait_ge(S["out_transposed"], 8 * t + (j + 1))
                    if j == 4 and not is_last(t):
                        act.wait_ge(S["norm_ready"], t)
                    act.activation(out_t_of(t, j // 4)[:, j % 4, :], bank[6 + j % 2][:, :], ACT.Identity,
                                   bias=cols[:, j // 4, j % 4:j % 4 + 1]).then_inc(S["out_t_ready"], 1)

            def projection(t, js):
                for j in js:
                    act.wait_ge(S["o_done"], 8 * t + (j + 1))
                    act.activation(a_t[:, j // 4, j % 4, :], bank[j % 4][:, :], ACT.Identity,
                                   bias=cols[:, 2 + j // 4, j % 4:j % 4 + 1]).then_inc(S["a_ready"], 1)
                    if j >= 4:
                        act.wait_ge(S["a_ready"], 8 * t + (j + 1))
                        act.mul(na_t[:, j % 4, :], a_t[:, 1, j % 4, :], -1.0).then_inc(S["na_ready"], 1)

            def squares(t, att):
                act.wait_ge(S["norm_ready"], t)
                if att and not is_last(t + 1):
                    act.wait_ge(S["score"], SCORE_STEPS * t + 2 * SCORE_STEPS)
                else:
                    act.wait_ge(S["out_ready"], 2 * NT)
                act.wait_ge(S["int_evacuated"], 8 * t + 8)
                for part in range(2):
                    act.activation(work[:, part * 2048:(part + 1) * 2048],
                                   ri_of(t)[:, part, :, :].rearrange("p n d -> p (n d)"), ACT.Square)\
                       .then_inc(S["squared"], 1)

            def unit_vectors(t):
                act.wait_ge(S["n2_ready"], t + 1)
                act.activation(work[:, 2048:4096], work[:, 0:2048], ACT.Ln).then_inc(S["ln_ready"], 1)
                act.wait_ge(S["ln_ready"], t + 1)
                act.activation(work[:, 2048:4096], work[:, 2048:4096], ACT.Exp, scale=-0.5).then_inc(S["y_ready"], 1)
                act.wait_ge(S["y_ready"], t + 1)
                act.activation(pa[:, :], work[:, 2048:4096], ACT.Square).then_inc(S["ysq_ready"], 1)

            def norm_root(t):
                act.wait_ge(S["norm_sq_ready"], t + 1)
                act.activation(small[:, 5:6], small[:, 4:5], ACT.Sqrt).then_inc(S["norm_root"], 1)

            def scale_sup(t):
                act.wait_ge(S["norm_ready"], t + 1)
                for part in range(2):
                    act.activation(sup[:, part, :], sup[:, part, :], ACT.Copy, scale=small[:, 6:7])\
                       .then_inc(S["sup_scaled"], 1)

            def body(i, att, inter, tail):
                if closing(i):
                    projection(i - 1, range(8))
                    for n in range(N):
                        interference(i - 1, n)
                    norm_root(i - 2)
                    scale_sup(i - 2)
                    squares(i - 1, False)
                    sup_transpose(i - 2)
                    unit_vectors(i - 1)
                    for part in (tail_squares, tail_amplitude, tail_amp_t, tail_post, tail_z_t, tail_h1_t):
                        part(i - 2)
                    return
                if att:
                    qkv(i, range(0, 2))
                if tail:
                    norm_root(i - 2)
                if att:
                    qkv(i, range(2, 6 if is_last(i) else 4))
                if tail:
                    scale_sup(i - 2)
                    sup_transpose(i - 2)
                if inter:
                    out_transpose(i - 1)
                if tail:
                    tail_squares(i - 2)
                if inter:
                    projection(i - 1, range(0, 4))
                if tail:
                    tail_amplitude(i - 2)
                if inter:
                    projection(i - 1, range(4, 8))
                if tail:
                    tail_amp_t(i - 2)
                    tail_post(i - 2)
                if inter:
                    interference(i - 1, 0)
                if inter:
                    interference(i - 1, 1)
                if tail and not is_last(i):
                    tail_z_t(i - 2)
                if att:
                    softmax(i)
                if inter:
                    interference(i - 1, 2)
                if tail and not is_last(i):
                    tail_h1_t(i - 2)
                if inter:
                    interference(i - 1, 3)
                    if is_last(i):
                        tail_z_t(i - 2)
                        tail_h1_t(i - 2)
                    squares(i - 1, att)
                    if is_last(i):
                        out_transpose(i)
                    unit_vectors(i - 1)
                if att and not is_last(i):
                    qkv(i, range(4, 6))
            turns(act, body)

        @block.vector
        def _(dve):
            class Chain:

                def __init__(self, name, per_tile, t):
                    self.sem, self.per, self.t, self.k = S[name], per_tile, t, 0

                def step(self, ins):
                    self.k += 1
                    ins.then_inc(self.sem, 1)
                    return self.k

                def wait(self, k):
                    dve.wait_ge(self.sem, self.t * self.per + k)

            def bias(t, which):
                buf, row = ((q_sb, bq), (k_sb, bk))[which]
                dve.wait_ge(S["qkv_evacuated"], 24 * t + 8 * (which + 1))
                v = buf[:, :, :, :].rearrange("p n r d -> p n (r d)")
                dve.tensor_tensor(v, v, row.unsqueeze(1).broadcast_to([P, N, 2 * D]), ALU.add)\
                   .then_inc(S["biased"], 1)

            def scores(ch, n):
                if n == 0:
                    dve.wait_ge(S["biased"], 2 * ch.t + 2)
                    dve.wait_ge(S["out_ready"], 2 * ch.t)
                halves = [work[:, 2048 * j:2048 * (j + 1)] for j in range(2)]
                for kind in range(2):
                    made = []
                    for j in range(2):
                        if ch.k >= 2:
                            ch.wait(ch.k - 1)
                        qn = q_sb[:, n, :, :] if kind == 0 else q_sb[:, n, ::-1, :]
                        qn = qn.unsqueeze(1).broadcast_to([P, 2, 2, D])
                        km = k_sb[:, 2 * j:2 * j + 2, :, :]
                        made.append(ch.step(dve.tensor_tensor(halves[j].rearrange("p (m r d) -> p m r d", m=2, r=2),
                                                              qn, km, ALU.mult)))
                    for j in range(2):
                        ch.wait(made[j])
                        ch.step(dve.tensor_reduce(
                            sc[:, n, kind, 2 * j:2 * j + 2].rearrange("p m r h -> p (m r h)"),
                            halves[j].rearrange("p (x d) -> p x d", d=HD), AX.X, ALU.add))

            def softmax(t):
                c = Chain("softmax", 8, t)
                dve.wait_ge(S["score"], SCORE_STEPS * t + SCORE_STEPS)
                c.step(dve.tensor_tensor(ar[:, :, :, :], sc[:, :, 0, :, 0, :], sc[:, :, 0, :, 1, :], ALU.add))
                c.step(dve.tensor_tensor(ai[:, :, :, :], sc[:, :, 1, :, 0, :], sc[:, :, 1, :, 1, :], ALU.subtract))
                c.wait(1)
                c.step(dve.tensor_tensor(ar[:, :, :, :], ar[:, :, :, :], ar[:, :, :, :], ALU.mult))
                c.wait(2)
                c.step(dve.tensor_tensor(ai[:, :, :, :], ai[:, :, :, :], ai[:, :, :, :], ALU.mult))
                c.wait(4)
                dve.scalar_tensor_tensor(ar[:, :, :, :].rearrange("p n m h -> p (n m h)"),
                                         ar[:, :, :, :].rearrange("p n m h -> p (n m h)"), EPS_MAG,
                                         ai[:, :, :, :].rearrange("p n m h -> p (n m h)"), ALU.add,
                                         ALU.add).then_inc(S["scored"], 1)
                dve.wait_ge(S["mag_ready"], t + 1)
                c.step(dve.tensor_reduce(mx[:, :, :], mag[:, :, :, :].rearrange("p n m h -> p n h m"), AX.X, ALU.max))
                c.wait(5)
                dve.tensor_tensor(ai[:, :, :, :], mag[:, :, :, :],
                                  mx[:, :, :].unsqueeze(2).broadcast_to([P, N, N, H]),
                                  ALU.subtract).then_inc(S["exp_in"], 1)
                dve.wait_ge(S["exp_ready"], t + 1)
                c.step(dve.tensor_reduce(mx[:, :, :], mag[:, :, :, :].rearrange("p n m h -> p n h m"), AX.X, ALU.add))
                c.wait(6)
                c.step(dve.reciprocal(mx[:, :, :], mx[:, :, :]))
                c.wait(7)
                c.step(dve.tensor_tensor(w_att[:, :, :, :], mag[:, :, :, :],
                                         mx[:, :, :].unsqueeze(2).broadcast_to([P, N, N, H]), ALU.mult))
                c.wait(8)

            def attend(c, t, part):
                if part == 0:
                    dve.wait_ge(S["qkv_evacuated"], 24 * t + 24)
                    if not is_last(t):
                        dve.wait_ge(S["int_done"], 8 * t)
                halves = [work[:, 2048 * j:2048 * (j + 1)] for j in range(2)]
                for pair in range(2):
                    a, b = [], []
                    for j in range(2):
                        n = 2 * pair + j
                        if pair:
                            c.wait(c.k - 1)
                        elif part and j:
                            dve.wait_ge(S["out_ready"], 2 * t + 1)
                        elif part:
                            c.wait(c.k)
                        vm = v_sb[:, :, part, :].rearrange("p m (h d) -> p m h d", h=H)
                        w = w_att[:, n, :, :].unsqueeze(3).broadcast_to([P, N, H, HD])
                        a.append(c.step(dve.tensor_tensor(halves[j].rearrange("p (m h d) -> p m h d", m=N, h=H),
                                                          vm, w, ALU.mult)))
                    for j in range(2):
                        c.wait(a[j])
                        b.append(c.step(dve.tensor_tensor(halves[j][:, 0:1024], halves[j][:, 0:1024],
                                                          halves[j][:, 1024:2048], ALU.add)))
                    for j in range(2):
                        c.wait(b[j])
                        ins = dve.tensor_tensor(out_of(t, 2 * pair + j, part), halves[j][:, 0:512],
                                                halves[j][:, 512:1024], ALU.add)
                        if pair == 1 and j == 1:
                            ins.then_inc(S["out_ready"], 1)
                        else:
                            c.step(ins)

            def tail_stage(t, n):
                c = Chain("tail", TAIL_STEPS, t)
                c.k = {0: 0, 1: 1, 2: 5, 3: 6}[n]
                if n == 0:
                    dve.wait_ge(S["meas_sq"], 2 * t + 2)
                    dve.tensor_tensor(ta[:, :], ta[:, :], tb[:, :], ALU.add).then_inc(S["amp_sq_ready"], 1)
                    dve.wait_ge(S["x1_loaded"], 16 * t + 16)
                    c.step(dve.tensor_tensor(x1[:, :], x1[:, :], b_top1, ALU.add))
                if n == 1:
                    dve.wait_ge(S["post_done"], t + 1)
                    c.step(dve.scalar_tensor_tensor(ta[:, :], bank[4][:, :], 1.0, post_b, ALU.mult, ALU.add,
                                                    accum_out=small[:, 7:8]))
                    c.wait(2)
                    dve.tensor_scalar(small[:, 2:3], small[:, 7:8], -1.0 / D, None,
                                      ALU.mult).then_inc(S["mean2_ready"], 1)
                    dve.wait_ge(S["std2_ready"], t + 1)
                    c.step(dve.reciprocal(small[:, 1:2], small[:, 0:1]))
                    c.wait(3)
                    c.step(dve.tensor_scalar(tb[:, :], ta[:, :], small[:, 2:3], small[:, 1:2], ALU.add, ALU.mult))
                    c.wait(4)
                    c.step(dve.tensor_tensor(tb[:, :], tb[:, :], post_g, ALU.mult))
                    c.wait(5)
                    dve.tensor_tensor(tb[:, :], tb[:, :], post_be, ALU.add).then_inc(S["pre_gelu"], 1)
                if n == 2:
                    dve.wait_ge(S["topz_done"], t + 1)
                    c.step(dve.tensor_tensor(tb[:, :], bank[5][:, :], x1[:, :], ALU.add))
                    c.wait(6)
                    dve.tensor_scalar(tb[:, :], tb[:, :], 0.0, None, ALU.max).then_inc(S["h1_ready"], 1)
                if n == 3:
                    dve.wait_ge(S["top2_done"], t + 1)
                    c.step(dve.tensor_tensor(ta[:, 0:TOP2], bank[4][:, 0:TOP2], b_top2, ALU.add))
                    c.wait(7)
                    dve.scalar_tensor_tensor(ta[:, TOP2:2 * TOP2], ta[:, 0:TOP2], 0.0, w3, ALU.max, ALU.mult,
                                             accum_out=y_all[:, t:t + 1] if isinstance(t, int) else y_all[:, bass.ds(t, 1)])\
                       .then_inc(S["y_done"], 1)

            def superposition(t, between=lambda k: None):
                c = Chain("phase", PHASE_STEPS, t)
                ri_all = ri_of(t)
                t0, t1 = work[:, 0:2048], work[:, 2048:4096]
                if isinstance(t, int) and t == 0:
                    dve.wait_ge(S["gathered"], 16 * NT * N)
                dve.wait_ge(S["squared"], 2 * t + 2)
                a = c.step(dve.tensor_tensor(t0, t0, t1, ALU.add))
                dve.wait_ge(S["pair_zero_made"], 3 * t)
                c.wait(a)
                dve.tensor_scalar(zero[:, :, :].rearrange("p n d -> p (n d)"), t0, 0.0, None,
                                  ALU.is_equal).then_inc(S["mask_made"], 1)
                dve.wait_ge(S["mask_made"], t + 1)
                dve.tensor_scalar(t0, t0, 1e-37, None, ALU.max).then_inc(S["n2_ready"], 1)
                c.step(dve.tensor_copy(st[:, :], strength[:, t, :, :].rearrange("p i j -> p (i j)") if isinstance(t, int)
                                       else strength[:, bass.ds(t, 1), :, :].rearrange("p a i j -> p (a i j)")))
                dve.wait_ge(S["ysq_ready"], t + 1)
                a = c.step(dve.tensor_tensor(pa[:, :], pa[:, :], t0, ALU.mult))
                c.wait(a)
                a = c.step(dve.scalar_tensor_tensor(t1, pa[:, :], 3.0, t1, ALU.subtract, ALU.mult))
                c.wait(a)
                ri = [ri_all[:, part, :, :].rearrange("p n d -> p (n d)") for part in range(2)]
                c.step(dve.scalar_tensor_tensor(t0, ri[0], -0.5, t1, ALU.mult, ALU.mult))
                a = c.step(dve.scalar_tensor_tensor(pa[:, :], ri[1], -0.5, t1, ALU.mult, ALU.mult))
                c.wait(a)
                dve.wait_ge(S["pair_zero_made"], 3 * t + 3)
                cos = t0.rearrange("p (n d) -> p n d", n=N)
                sin = pa[:, :].rearrange("p (n d) -> p n d", n=N)
                xx = t1[:, 0:6 * CH].rearrange("p (j d) -> p j d", j=6)
                yy = pb[:, :].rearrange("p (j d) -> p j d", j=6)
                w = pb[:, 0:N * CH].rearrange("p (j d) -> p j d", j=N)
                prod = t1.rearrange("p (r j d) -> p r j d", r=2, j=N)
                between(0)
                for e in range(0, D, CH):
                    cs = slice(e, e + CH)
                    for f, k, apart in PAIRS:
                        c.step(dve.tensor_tensor(xx[:, f:f + k, :], cos[:, 0:k, cs], cos[:, apart:apart + k, cs], ALU.mult))
                        a = c.step(dve.tensor_tensor(yy[:, f:f + k, :], sin[:, 0:k, cs], sin[:, apart:apart + k, cs],
                                                     ALU.mult))
                    c.wait(a)
                    a = c.step(dve.tensor_tensor(xx, xx, yy, ALU.add))
                    c.wait(a)
                    a = c.step(dve.tensor_tensor(xx, xx, pair_zero[:, :, cs], ALU.add))
                    c.wait(a)
                    last = {}
                    for step in range(3):
                        for j in range(N):
                            i = [i for i in range(N) if i != j][step]
                            f = xx[:, PAIR_AT[(min(i, j), max(i, j))], :]
                            s_ij = st[:, N * i + j:N * i + j + 1]
                            if step == 0:
                                ins = dve.tensor_scalar(w[:, j, :], f, s_ij, st[:, (N + 1) * j:(N + 1) * j + 1],
                                                        ALU.mult, ALU.add)
                            else:
                                c.wait(last[j])
                                ins = dve.scalar_tensor_tensor(w[:, j, :], f, s_ij, w[:, j, :], ALU.mult, ALU.add)
                            last[j] = c.step(ins)
                    c.wait(last[3])
                    for part in range(2):
                        a = c.step(dve.tensor_tensor(prod[:, part, :, :], ri_all[:, part, :, cs], w, ALU.mult))
                    c.wait(a)
                    a = c.step(dve.tensor_tensor(prod[:, :, 0:2, :], prod[:, :, 0:2, :], prod[:, :, 2:4, :], ALU.add))
                    c.wait(a)
                    if e == 0:
                        dve.wait_ge(S["sup_transposed"], t)
                    a = c.step(dve.tensor_tensor(sup[:, :, cs], prod[:, :, 0, :], prod[:, :, 1, :], ALU.add))
                    c.wait(a)
                    between(e // CH + 1)
                for part in range(2):
                    a = c.step(dve.scalar_tensor_tensor(t1[:, part * D:(part + 1) * D], sup[:, part, :], 1.0,
                                                        sup[:, part, :], ALU.mult, ALU.mult,
                                                        accum_out=small[:, 3 + part:4 + part]))
                c.wait(a)
                dve.scalar_tensor_tensor(small[:, 4:5], small[:, 3:4], EPS_MAG, small[:, 4:5], ALU.add,
                                         ALU.add).then_inc(S["norm_sq_ready"], 1)
                assert c.k == PHASE_STEPS, c.k
                between(3)

            def norm(t):
                dve.wait_ge(S["norm_root"], t + 1)
                dve.reciprocal(small[:, 6:7], small[:, 5:6]).then_inc(S["norm_ready"], 1)

            dve.wait_ge(early_loaded["rows"], 16)

            def body(i, att, inter, tail):
                if closing(i):
                    superposition(i - 1, lambda k: tail_stage(i - 2, k))
                    norm(i - 1)
                    return
                if att:
                    bias(i, 0)
                    bias(i, 1)
                    ch = Chain("score", SCORE_STEPS, i)
                    scores(ch, 0)
                if tail:
                    tail_stage(i - 2, 0)
                if att:
                    scores(ch, 1)
                    scores(ch, 2)
                if tail:
                    tail_stage(i - 2, 1)
                if att:
                    scores(ch, 3)
                    assert ch.k == SCORE_STEPS, ch.k
                if tail and not is_last(i):
                    tail_stage(i - 2, 2)
                if att:
                    softmax(i)
                if tail and not is_last(i):
                    tail_stage(i - 2, 3)
                if is_last(i):
                    c = Chain("pv", PV_STEPS, i)
                    attend(c, i, 0)
                    attend(c, i, 1)
                    tail_stage(i - 2, 2)
                    tail_stage(i - 2, 3)
                    superposition(i - 1)
                    norm(i - 1)
                    return
                if inter:
                    superposition(i - 1)
                if att:
                    c = Chain("pv", PV_STEPS, i)
                    attend(c, i, 0)
                if inter:
                    norm(i - 1)
                if att:
                    attend(c, i, 1)
                    assert c.k == PV_STEPS, c.k
            turns(dve, body)

        @block.tensor
        def _(pe):
            def body(i, att, inter, tail):
                at = [0]

                def next_unit():
                    slot, loaded = place(i, at[0])
                    at[0] += 1
                    pe.wait_ge(w2_loaded[slot], loaded)
                    return w2[:, slot, :].rearrange("p (k c) -> p k c", k=DT)

                def transposes(out, src, name):
                    for k in range(DT):
                        ins = pe.transpose(out[:, k * P:(k + 1) * P], src[:, k * P:(k + 1) * P], ident[:, :])
                    if name:
                        ins.then_inc(S[name], 1)

                def product_of(out, lhs, rhs, name=None, start=True, stop=True):
                    for kt in range(DT):
                        mm = pe.matmul(out, lhs(kt), rhs(kt), start=start and kt == 0, stop=stop and kt == DT - 1)
                    if name:
                        mm.then_inc(S[name], 1)

                def qkv(t, units):
                    for k in units:
                        w = next_unit()
                        if k < 2:
                            pe.wait_ge(s_loaded[k], 16 * t + 16)
                        if k == 0:
                            if not isinstance(t, int) or t:
                                pe.wait_ge(S["qkv_evacuated"], 24 * t - 4)
                        after_inter = inter and not is_last(i)
                        if k == 4 and after_inter:
                            pe.wait_ge(S["int_evacuated"], 8 * t)
                        if k == 5 and tail:
                            pe.wait_ge(S["tail"], TAIL_STEPS * (t - (1 if after_inter else 2)))
                        for n in range(N):
                            if k in (1, 2, 3) or k == 4 and not after_inter:
                                pe.wait_ge(S["qkv_evacuated"], 24 * t + (4 * (k - 1) + n + 1))
                            product_of(qkv_bank(k, n)[:, :], lambda kt: s_in[:, k % 2, DT * n + kt, :],
                                       lambda kt: w[:, kt, :], "qkv_done")

                def interference(t, n):
                    b_r, b_i = bank[2 * (n % 2)][:, :], bank[2 * (n % 2) + 1][:, :]
                    if n == 0:
                        pe.wait_ge(S["a_ready"], 8 * t + 8)
                        pe.wait_ge(S["na_ready"], 4 * t + 4)
                    if n >= 2:
                        pe.wait_ge(S["int_evacuated"], 8 * t + (2 * (n - 2) + 2))
                    rows_n = slice(n * P, (n + 1) * P)
                    w = next_unit()
                    product_of(b_r, lambda kt: a_t[:, 0, kt, rows_n], lambda kt: w[:, kt, :], None, True, False)
                    product_of(b_i, lambda kt: a_t[:, 1, kt, rows_n], lambda kt: w[:, kt, :], "int_done", True, False)
                    w = next_unit()
                    product_of(b_r, lambda kt: na_t[:, kt, rows_n], lambda kt: w[:, kt, :], None, False, True)
                    product_of(b_i, lambda kt: a_t[:, 0, kt, rows_n], lambda kt: w[:, kt, :], "int_done", False, True)

                def tail_stage(t, n):
                    if n == 0:
                        pe.wait_ge(S["sup_t_ready"], 3 * t + 3)
                        pe.wait_ge(S["tail"], TAIL_STEPS * t)
                        w = next_unit()
                        product_of(bank[4][:, :], lambda kt: sup_t[:, 0, kt, :], lambda kt: w[:, kt, :], None, True, False)
                        product_of(bank[5][:, :], lambda kt: sup_t[:, 1, kt, :], lambda kt: w[:, kt, :], "meas_done",
                                   True, False)
                        w = next_unit()
                        product_of(bank[4][:, :], lambda kt: sup_t[:, 2, kt, :], lambda kt: w[:, kt, :], None, False, True)
                        product_of(bank[5][:, :], lambda kt: sup_t[:, 0, kt, :], lambda kt: w[:, kt, :], "meas_done",
                                   False, True)
                    if n == 1:
                        pe.wait_ge(S["amp_ready"], t + 1)
                        transposes(bank[6], tb, "amp_transposed")
                        pe.wait_ge(S["amp_t_ready"], t + 1)
                        w = next_unit()
                        product_of(bank[4][:, :], lambda kt: x_t[:, kt, :], lambda kt: w[:, kt, :], "post_done")
                    if n == 2:
                        pe.wait_ge(S["z_ready"], t + 1)
                        transposes(bank[7], ta, "z_transposed")
                        pe.wait_ge(S["z_t_ready"], t + 1)
                        w = next_unit()
                        product_of(bank[5][:, :], lambda kt: x_t[:, kt, :], lambda kt: w[:, kt, :], "topz_done")
                    if n == 3:
                        pe.wait_ge(S["h1_ready"], t + 1)
                        transposes(bank[6], tb, "h1_transposed")
                        pe.wait_ge(S["h1_t_ready"], t + 1)
                        next_unit()
                        slot = place(i, at[0] - 1)[0]
                        w2t = w2[:, slot, 0:DT * TOP2].rearrange("p (k c) -> p k c", k=DT)
                        product_of(bank[4][:, 0:TOP2], lambda kt: x_t[:, kt, :], lambda kt: w2t[:, kt, :], "top2_done")

                def out_transpose(t):
                    if isinstance(t, int) and t == 0:
                        pe.wait_ge(S["ident_made"], 1)
                    pe.wait_ge(S["qkv_evacuated"], 24 * t + (48 if is_last(i) else 24))
                    if tail and not closing(i):
                        pe.wait_ge(S["sup_t_ready"], 3 * t)
                    for j in range(8):
                        r, f = j // 4, j % 4
                        if f == 0:
                            pe.wait_ge(S["out_ready"], 2 * t + (r + 1))
                        if j >= 2:
                            pe.wait_ge(S["out_t_ready"], 8 * t + (j - 1))
                        for n in range(N):
                            ins = pe.transpose(bank[6 + j % 2][:, n * P:(n + 1) * P],
                                               out_of(t, n, r)[:, f * P:(f + 1) * P], ident[:, :])
                        ins.then_inc(S["out_transposed"], 1)

                def projection(t):
                    if closing(i):
                        pe.wait_ge(S["int_evacuated"], 8 * t)
                    if att:
                        pe.wait_ge(S["qkv_evacuated"], 24 * t + (44 if is_last(i) else 40))
                    for r in range(2):
                        w = next_unit()
                        pe.wait_ge(S["out_t_ready"], 8 * t + (4 * r + 4))
                        for mt in range(DT):
                            j = 4 * r + mt
                            if j >= 4:
                                pe.wait_ge(S["a_ready"], 8 * t + (j - 3))
                            product_of(bank[j % 4][:, :], lambda kt: w[:, kt, mt * P:(mt + 1) * P],
                                       lambda kt: out_t_of(t, r)[:, kt, :], "o_done")

                def sup_transpose(t):
                    pe.wait_ge(S["sup_scaled"], 2 * t + 2)
                    pe.wait_ge(S["qkv_evacuated"], 24 * i if att and not is_last(i) else 24 * NT)
                    transposes(bank[6], sup[:, 0, :], None)
                    transposes(bank[7], sup[:, 1, :], "sup_transposed")

                if closing(i):
                    out_transpose(i - 1)
                    projection(i - 1)
                    for n in range(N):
                        interference(i - 1, n)
                    sup_transpose(i - 2)
                    for n in range(N):
                        tail_stage(i - 2, n)
                    return
                if att:
                    qkv(i, range(0, 6 if is_last(i) else 4))
                if tail:
                    sup_transpose(i - 2)
                if inter:
                    out_transpose(i - 1)
                if tail:
                    tail_stage(i - 2, 0)
                if inter:
                    projection(i - 1)
                if tail:
                    tail_stage(i - 2, 1)
                if inter:
                    interference(i - 1, 0)
                    interference(i - 1, 1)
                if tail and not is_last(i):
                    tail_stage(i - 2, 2)
                if inter:
                    interference(i - 1, 2)
                if tail and not is_last(i):
                    tail_stage(i - 2, 3)
                if inter:
                    interference(i - 1, 3)
                if is_last(i):
                    tail_stage(i - 2, 2)
                    tail_stage(i - 2, 3)
                if att and not is_last(i):
                    qkv(i, range(4, 6))
            turns(pe, body)


def kernel(**inputs):
    import numpy as np
    import concourse.bacc as bacc
    from concourse.bass_utils import run_bass_kernel_spmd

    a = {k: np.asarray(v) for k, v in inputs.items()}

    def rec(name):
        return a["L0_rec_" + name]

    def stationary_units(w):
        o, n = w.shape
        return np.ascontiguousarray(w.reshape(o // P, P, n // P, P).transpose(0, 3, 2, 1)).reshape(o // P, P, n)

    def moving_unit(w):
        n, o = w.shape
        u = np.ascontiguousarray(w.reshape(n // P, P, o).transpose(1, 0, 2)).reshape(P, n // P * o)
        return u if u.shape[1] == UNIT else np.pad(u, ((0, 0), (0, UNIT - u.shape[1])))

    units = [rec(n).T for n in ("Wq_r", "Wq_i", "Wk_r", "Wk_i", "Wv_r", "Wv_i", "Wo_r", "Wo_i")]
    for n in range(N):
        units += [rec("int_Wr")[n].T, rec("int_Wi")[n].T]
    units += [rec("meas_Mr").T, rec("meas_Mi").T, rec("post_W").T, a["W_top1"][0:D], a["W_top2"]]
    rows = np.concatenate([rec(n) for n in ("bq_r", "bq_i", "bk_r", "bk_i", "post_b", "post_g", "post_be")]
                          + [a["b_top1"], a["b_top2"], a["W_top3"][:, 0]])
    cols = np.stack([rec(n) for n in ("bv_r", "bv_i", "bo_r", "bo_i")])
    vecs = np.stack([rec(e + k) for e in ("er_", "ei_") for k in ("b1", "g1", "be1", "b2")])
    arrays = {
        "x": np.ascontiguousarray(a["r_x"].reshape(2, HALF, KT, P).transpose(0, 3, 2, 1)),
        "w1r": stationary_units(rec("er_W1")), "w1i": stationary_units(rec("ei_W1")),
        "w2r": stationary_units(rec("er_W2")), "w2i": stationary_units(rec("ei_W2")),
        "wtx": np.stack([moving_unit(a["W_top1"][D + j * D:D + (j + 1) * D]) for j in range(4)]),
        "vecs": np.ascontiguousarray(vecs.reshape(8, KT, P).transpose(2, 0, 1)),
        "ws2": np.stack([moving_unit(w) for w in units]),
        "rows": np.ascontiguousarray(np.broadcast_to(rows, (P, rows.size))),
        "cols": np.ascontiguousarray(cols.reshape(4, DT, P).transpose(2, 0, 1)),
        "ids": np.ascontiguousarray(a["ids"].reshape(NT, P, N).transpose(1, 0, 2)),
        **{f"tbl{f}": np.ascontiguousarray(a[f"tbl_{f}"]) for f in range(N)},
    }
    nc = bacc.Bacc("TRN2", target_bir_lowering=False, num_devices=1)
    dram = {k: nc.dram_tensor(k, v.shape, mybir.dt.from_np(v.dtype), kind="ExternalInput").ap()
            for k, v in arrays.items()}
    dram["s"] = nc.dram_tensor("s", (NT, P, 2, KT, P), F32, kind="Internal").ap()
    dram["t1x"] = nc.dram_tensor("t1x", (NT, P, TOP1), F32, kind="Internal").ap()
    dram["out"] = nc.dram_tensor("out", (P, NT), F32, kind="ExternalOutput").ap()
    with ExitStack() as ctx:
        early_loaded = {k: ctx.enter_context(nc.semaphore("early_" + k)) for k in ("rows", "cols", "ids")}
        early_loaded["w2"] = [ctx.enter_context(nc.semaphore(f"w2_loaded{i}")) for i in range(RING)]
        early_loaded["s"] = [ctx.enter_context(nc.semaphore(f"s_loaded{i}")) for i in range(2)]
        with ExitStack() as place:
            early = early_buffers(nc, place, "")
        encode(nc, dram, early, early_loaded)
        mix(nc, dram, early, early_loaded)
    got = run_bass_kernel_spmd(nc, [arrays], core_ids=[0])
    return np.ascontiguousarray(got.results[0]["out"].T).reshape(BATCH, 1)
```

```python
from contextlib import ExitStack

import concourse.bass as bass
from concourse import mybir

ALU = mybir.AluOpType
ACT = mybir.ActivationFunctionType
AX = mybir.AxisListType
F32 = mybir.dt.float32
F32R = mybir.dt.float32r
BF16 = mybir.dt.bfloat16
I32 = mybir.dt.int32

P = 128
BATCH = 1024
IN = 2048
HID = 2048
D = 512
N = 4
H = 8
HD = D // H
TOP1 = 512
TOP2 = 256
NT = BATCH // P
HALF = BATCH // 2
HT = HALF // P
KT = IN // P
DT = D // P
UNIT = KT * P
QC = UNIT // 4
EPS_LN = 1e-5
EPS_MAG = 1e-8

PHASES = [
    dict(kind="G1", job=0),
    dict(kind="G1", job=1, merge=0, ln=0),
    dict(kind="TX", half=0),
    dict(kind="G2", job=0, merge=1, load_x=1),
    dict(kind="G1", job=2, ln=1),
    dict(kind="G2", job=1, merge=2),
    dict(kind="G1", job=3, ln=2),
    dict(kind="G2", job=2, merge=3, normalize=3),
    dict(kind="TX", half=1, ln=3),
    dict(kind="G2", job=3),
]
_unit = _acc = _store = 0
for _p in PHASES:
    _p["units"] = 4 if _p["kind"] == "TX" else KT
    _p["unit"], _p["acc"], _p["store"] = _unit, _acc, _store
    _unit += _p["units"]
    _acc += HT if _p["kind"] == "TX" else KT
    _store += {"G1": 0, "G2": KT, "TX": HT // 2}[_p["kind"]]
UNITS = _unit
STORES = _store


def early_buffers(nc, stack, tag):
    def sb(name, shape, dt=F32):
        return stack.enter_context(nc.sbuf_tensor(name + tag, shape, dt))

    with ExitStack() as same:
        s_in = sb("s_in", [P, 2, UNIT])
        w_qkv = same.enter_context(nc.sbuf_tensor("w_qkv" + tag, [P, RING, UNIT], F32))
    return dict(
        s_in=s_in,
        w_qkv=w_qkv,
        w2=sb("w2", [P, RING, UNIT]),
        rows=sb("rows_sb", [P, 9 * D]),
        cols=sb("cols_sb", [P, 4, DT]),
        ids=sb("ids_sb", [P, NT, N], I32),
    )


def encode(nc, dram, early, early_loaded):
    with ExitStack() as ctx:
        def sb(name, shape, dt=F32):
            return ctx.enter_context(nc.sbuf_tensor(name, shape, dt))

        def sem(name):
            return ctx.enter_context(nc.semaphore(name))

        x_hi = sb("x_hi", [P, KT, HALF], F32R)
        x_lo = sb("x_lo", [P, KT, HALF], F32R)
        h_hi = sb("h_hi", [P, KT, HALF], F32R)
        h_lo = sb("h_lo", [P, KT, HALF], F32R)
        raw = sb("raw", [P, KT, HALF])
        w_raw = sb("w_raw", [P, 2, UNIT])
        w_hi = sb("w_hi", [P, 4, QC], F32R)
        w_lo = sb("w_lo", [P, 4, QC], F32R)
        lane_sum = sb("lane_sum", [P, HALF])
        lane_sq = sb("lane_sq", [P, HALF])
        rstd = sb("rstd", [P, HALF])
        dev = sb("dev", [P, HALF])
        stage = sb("stage", [P, 2, HALF])
        x_stage = sb("x_stage", [P, HALF])
        ones = sb("ones", [P, P])
        eps = sb("eps", [P, 1])
        vecs = sb("features", [P, 8, KT])

        bank = [ctx.enter_context(nc.psum_tensor(f"bank{i}", [P, 512], F32)) for i in range(8)]
        mean_bank, gelu_bank, sq_bank = bank[2], [bank[3], bank[6]], bank[7]
        tx_banks = [bank[0], bank[1], bank[4], bank[5]]

        w_loaded = [sem(f"w_loaded{i}") for i in range(2)]
        wh_ready = sem("wh_ready")
        wl_ready = sem("wl_ready")
        w_used = sem("w_used")
        x0_loaded = [sem(f"x0_loaded{i}") for i in range(4)]
        x_loaded = sem("x_loaded")
        xh_ready = sem("xh_ready")
        xl_ready = sem("xl_ready")
        consts = sem("consts")
        vecs_loaded = sem("vecs_loaded")
        acc_evacuated = sem("acc_evacuated")
        stored = [sem(f"stored{i}") for i in range(2)]
        s_hi_made = sem("s_hi_made")
        qkv_loaded = [sem(f"qkv_loaded{i}") for i in range(2)]
        qkv_stored = [sem(f"qkv_stored{i}") for i in range(2)]
        qkv_hi = sem("qkv_hi")
        qkv_lo = sem("qkv_lo")
        dev_ready = sem("dev_ready")
        sq_ready = sem("sq_ready")
        stat_done = sem("stat_done")
        merge = sem("merge")
        lane_mean_ready = sem("lane_mean_ready")
        lane_var_ready = sem("lane_var_ready")
        mean_ready = sem("mean_ready")
        var_ready = sem("var_ready")
        std_ready = sem("std_ready")
        centered = sem("centered")
        ln_scaled = sem("ln_scaled")
        ln_gelu = sem("ln_gelu")
        ln_hi = sem("ln_hi")
        ln_lo = sem("ln_lo")

        B1, G, BE, B2 = range(4)
        last_g2 = {}
        end = 0
        for ph in PHASES:
            if ph.get("ln") is not None:
                last_g2[ph["ln"]] = end
            if ph["kind"] == "G2":
                end = ph["unit"] + ph["units"]
        tx0_end = PHASES[2]["unit"] + PHASES[2]["units"]

        def steps(eng, ph, body):
            pairs = ph["units"] // 2
            if ph["kind"] == "TX":
                for i in range(pairs):
                    for e in range(2):
                        body(i, e, i == 0, False)
                return
            straight = 2 if ph is PHASES[-1] else 0
            for e in range(2):
                body(0, e, True, False)
            with eng.Fori(1, pairs - straight) as i:
                for e in range(2):
                    body(i, e, False, False)
            for i in range(pairs - straight, pairs):
                for e in range(2):
                    body(i, e, False, i == pairs - 1)

        def slab(t, i):
            return t[:, i, :] if isinstance(i, int) else t[:, bass.ds(i, 1), :].rearrange("p a c -> p (a c)")

        def col(k, enc, i):
            j = 4 * enc + k
            return vecs[:, j, i:i + 1] if isinstance(i, int) else vecs[:, j, bass.ds(i, 1)]

        def qkv_slot(e):
            at = raw[:, 8 * e:8 * e + 6, :].rearrange("p a c -> p (a c)")
            return at[:, 0:UNIT // 2], at[:, UNIT // 2:UNIT], at[:, UNIT:3 * UNIT // 2], at[:, UNIT // 2:3 * UNIT // 2]

        def splits(ph, i):
            return ph is PHASES[-1] and not (isinstance(i, int) and i >= QKV_UNITS)

        block = ctx.enter_context(nc.Block())

        @block.sync
        def _(sp):
            for c in range(4):
                sp.dma_start(raw[:, 4 * c:4 * c + 4, :], dram["x"][0, :, 4 * c:4 * c + 4, :]).then_inc(x0_loaded[c], 16)
                if c < 2:
                    sp.dma_start(w_raw[:, c, :], dram["w1r"][c, :, :]).then_inc(w_loaded[c], 16)
                if c == 2:
                    sp.dma_start(vecs[:, :, :], dram["vecs"]).then_inc(vecs_loaded, 16)
            for ph in PHASES:
                name = "wtx" if ph["kind"] == "TX" else ("w1" if ph["kind"] == "G1" else "w2") + "ri"[ph["job"] % 2]

                def load(i, e, first, last, ph=ph, name=name):
                    if ph is PHASES[0] and first:
                        return
                    sp.wait_ge(wl_ready, 8 * i + (4 * (ph["unit"] + e) - 4))
                    src = dram[name]
                    m = 2 * i + e
                    src = src[m, :, :] if isinstance(m, int) else src[bass.ds(m, 1), :, :].rearrange("a p c -> p (a c)")
                    sp.dma_start(w_raw[:, e, :], src).then_inc(w_loaded[e], 16)
                    if ph is PHASES[-1] and not (isinstance(i, int) and i in (0, QKV_UNITS + 1)):
                        sp.wait_ge(qkv_lo, 2 * i + (e - 1))
                        dst = dram["wqkv"]
                        dst = dst[i - 1, e] if isinstance(i, int) else \
                            dst[bass.ds(i - 1, 1), e].rearrange("a p c -> p (a c)")
                        sp.dma_start(dst, qkv_slot(e)[3]).then_inc(qkv_stored[e], 16)
                    if splits(ph, i):
                        if first:
                            sp.wait_ge(ln_gelu, 4 * KT)
                        half = slice(e * UNIT // 2, (e + 1) * UNIT // 2)
                        src = dram["ws2"]
                        src = src[i, :, half] if isinstance(i, int) else \
                            src[bass.ds(i, 1), :, half].rearrange("a p c -> p (a c)")
                        sp.dma_start(qkv_slot(e)[0], src).then_inc(qkv_loaded[e], 16)
                    if last and e == 1:
                        sp.wait_ge(w_used, 4 * ph["unit"])
                        for slot in range(2):
                            sp.wait_ge(stored[slot], 16 * (PHASES[5]["store"] + KT))
                            sp.wait_ge(qkv_stored[slot], 16 * QKV_UNITS)
                        for half in range(2):
                            sp.dma_start(early["s_in"][:, half, :].rearrange("p (n x) -> p n x", n=N),
                                         dram["s"][0, 0, :, half].rearrange("n p x -> p n x"))\
                              .then_inc(early_loaded["s"][half], 16)
                            for slot in ([0, 1], [2])[half]:
                                unit = TURN[0][1][slot]
                                sp.dma_start(early["w_qkv"][:, slot, :], dram["wqkv"][unit // 2, unit % 2])\
                                  .then_inc(early_loaded["w2"][slot], 16)
                        for name in ("rows", "cols", "ids"):
                            dst = early[name][:, :] if name == "rows" else early[name][:, :, :]
                            sp.dma_start(dst, dram[name]).then_inc(early_loaded[name], 16)
                    if ph.get("load_x"):
                        sp.wait_ge(xl_ready, 2 * i + (KT + e))
                        xs = dram["x"][ph["load_x"]]
                        xs = xs[:, m, :] if isinstance(m, int) else xs[:, bass.ds(m, 1), :].rearrange("p a c -> p (a c)")
                        sp.dma_start(x_stage[:, :], xs).then_inc(x_loaded, 16)
                steps(sp, ph, load)

        @block.gpsimd
        def _(pool):
            pool.memset(ones[:, :], 1.0 / P).then_inc(consts, 1)
            pool.memset(eps[:, :], EPS_LN).then_inc(consts, 1)

        @block.scalar
        def _(act):
            def split_w(slot, u_base, i, q, first_unit=False):
                if q == 0:
                    act.wait_ge(w_loaded[slot], 16 * i + 16 * (u_base // 2 + 1))
                if not first_unit:
                    act.wait_ge(w_used, 8 * i + (4 * u_base + q - 3))
                act.copy(w_hi[:, q, :], w_raw[:, slot, q * QC:(q + 1) * QC]).then_inc(wh_ready, 1)

            def gelu_tile(ln, t, c, odd):
                act.wait_ge(ln_scaled, c + 1)
                if not (isinstance(c, int) and c < 2):
                    act.wait_ge(ln_lo, c - 1)
                act.activation(gelu_bank[odd][:, :], slab(raw, t), ACT.Gelu, bias=col(BE, ln % 2, t),
                               scale=col(G, ln % 2, t)).then_inc(ln_gelu, 1)

            def hi_tile(t, c, odd):
                act.wait_ge(ln_gelu, c + 1)
                act.copy(slab(h_hi, t), gelu_bank[odd][:, :]).then_inc(ln_hi, 1)

            def std(ln):
                act.wait_ge(var_ready, ln + 1)
                act.activation(rstd[:, :], sq_bank[:, :], ACT.Sqrt, bias=eps[:, :]).then_inc(std_ready, 1)

            act.wait_ge(consts, 2)
            for kt in range(4):
                if kt % 4 == 0:
                    act.wait_ge(x0_loaded[kt // 4], 16)
                act.copy(x_hi[:, kt, :], raw[:, kt, :]).then_inc(xh_ready, 1)
            split_w(0, 0, 0, 0, True)
            for kt in range(4, KT):
                if kt % 4 == 0:
                    act.wait_ge(x0_loaded[kt // 4], 16)
                act.copy(x_hi[:, kt, :], raw[:, kt, :]).then_inc(xh_ready, 1)
                if kt % 4 == 3:
                    split_w(0, 0, 0, kt // 4, True)
            act.wait_ge(vecs_loaded, 16)
            for ph in PHASES:
                ln, merge_of = ph.get("ln"), ph.get("merge")

                def step(i, e, first, last, ph=ph, ln=ln, merge_of=merge_of):
                    u, m = ph["unit"] + e, 2 * i + e
                    more = not (last and e == 1)

                    def hi(q):
                        if more:
                            split_w((e + 1) % 2, u + 1, i, q)
                    hi(0)
                    if ln is not None and first and e == 0:
                        if merge_of is not None:
                            std(merge_of)
                        if last_g2[ln]:
                            act.wait_ge(w_used, 4 * last_g2[ln])
                    if ph["kind"] == "TX":
                        for j in range(4):
                            if ln is not None:
                                t = 4 * m + j
                                gelu_tile(ln, t, KT * ln + t, t % 2)
                                hi_tile(t, KT * ln + t, t % 2)
                            if j < 3:
                                hi(j + 1)
                    else:
                        if ln is not None:
                            gelu_tile(ln, m, m + KT * ln, e)
                        hi(1)
                        if ln is not None:
                            hi_tile(m, m + KT * ln, e)
                        hi(2)
                    if ph.get("load_x"):
                        if first and e == 0:
                            act.wait_ge(w_used, 4 * tx0_end)
                        act.wait_ge(x_loaded, 32 * i + 16 * (e + 1))
                        act.copy(slab(x_hi, m), x_stage[:, :]).then_inc(xh_ready, 1)
                    if ph["kind"] == "TX":
                        if m == 3:
                            for bt in range(HT):
                                z, slot = ph["store"] + bt // 2, bt % 2
                                if bt == 0:
                                    act.wait_ge(w_used, 4 * (ph["unit"] + 4))
                                if z:
                                    act.wait_ge(stored[slot], 16 * z)
                                act.copy(stage[:, slot, :], tx_banks[bt][:, :]).then_inc(acc_evacuated, 1)
                                act.wait_ge(acc_evacuated, ph["acc"] + bt + 1)
                                act.dma_start(dram["t1x"][HT * ph["half"] + bt], stage[:, slot, :])\
                                   .then_inc(stored[slot], 16)
                        return
                    enc, half = ph["job"] % 2, ph["job"] // 2
                    a = ph["acc"] + e
                    act.wait_ge(w_used, 8 * i + (4 * u + 4))
                    if ph["kind"] == "G1":
                        if ph is PHASES[0] and first and e == 0:
                            act.wait_ge(xl_ready, KT)
                        if first and e == 0:
                            act.wait_ge(acc_evacuated, a)
                        act.activation(slab(raw, m), bank[e][:, :], ACT.Identity,
                                       bias=col(B1, enc, m)).then_inc(acc_evacuated, 1)
                        hi(3)
                        c = KT * ph["job"] + e
                        act.wait_ge(dev_ready, 2 * i + (c + 1))
                        act.wait_ge(stat_done, 2 * i + c)
                        act.activation(sq_bank[:, :], dev[:, :], ACT.Square).then_inc(sq_ready, 1)
                    else:
                        z, g2 = ph["store"] + e, KT * ph["job"] + e
                        for slot in range(2):
                            if not (isinstance(i, int) and z + 2 * i == 0):
                                act.wait_ge(stored[slot], 32 * i + 16 * z)
                        act.activation(stage[:, 0, :].bitcast(F32R), bank[e][:, :], ACT.Identity,
                                       bias=col(B2, enc, m)).then_inc(s_hi_made, 1)
                        dst = dram["s"][HT * half:HT * half + HT, enc].rearrange("t n k p x -> t (n k) p x")
                        dst = dst[:, i] if isinstance(i, int) else \
                            dst[:, bass.ds(i, 1)].rearrange("t a p x -> t (a p) x")
                        dst = [dst[:, :, (2 * j + e) * P:(2 * j + e + 1) * P].rearrange("t p c -> p t c")
                               for j in range(2)]
                        act.wait_ge(s_hi_made, 2 * i + (g2 + 1))
                        act.dma_start(dst[0], stage[:, 0, :].rearrange("p (t c) -> p t c", t=HT)).then_inc(stored[0], 16)
                        hi(3)
                        act.wait_ge(acc_evacuated, 2 * i + (a + 1))
                        act.dma_start(dst[1], stage[:, 1, :].rearrange("p (t c) -> p t c", t=HT)).then_inc(stored[1], 16)
                        if splits(ph, i):
                            src, to_hi, _, _ = qkv_slot(e)
                            act.wait_ge(qkv_loaded[e], 16 * i + 16)
                            if not first:
                                act.wait_ge(qkv_stored[e], 16 * i)
                            act.copy(to_hi.bitcast(F32R), src).then_inc(qkv_hi, 1)
                        if merge_of is not None and first and e == 1:
                            std(merge_of)
                steps(act, ph, step)
            for z in range(2):
                act.wait_ge(stored[z], 16 * STORES)
                act.wait_ge(qkv_stored[z], 16 * QKV_UNITS)

        @block.vector
        def _(dve):
            link_count = [0]

            def link(ins):
                link_count[0] += 1
                ins.then_inc(merge, 1)
                dve.wait_ge(merge, link_count[0])

            def lo_w(slot, u_base, i, q):
                dve.wait_ge(wh_ready, 8 * i + (4 * u_base + q + 1))
                dve.tensor_tensor(w_lo[:, q, :], w_raw[:, slot, q * QC:(q + 1) * QC], w_hi[:, q, :],
                                  ALU.subtract).then_inc(wl_ready, 1)

            def lo_x(i, src, c):
                dve.wait_ge(xh_ready, c + 1)
                dve.tensor_tensor(slab(x_lo, i), src, slab(x_hi, i), ALU.subtract).then_inc(xl_ready, 1)

            def merge_lanes(job, parts=range(4)):
                if 0 in parts:
                    dve.wait_ge(stat_done, KT * (job + 1))
                    link(dve.tensor_tensor(dev[:, :], lane_sum[:, :], lane_sum[:, :], ALU.mult))
                    dve.scalar_tensor_tensor(lane_sum[:, :], lane_sum[:, :], 1.0 / KT, raw[:, 0, :], ALU.mult,
                                             ALU.add).then_inc(lane_mean_ready, 1)
                if 1 in parts:
                    link(dve.scalar_tensor_tensor(lane_sq[:, :], dev[:, :], -1.0 / KT, lane_sq[:, :], ALU.mult,
                                                  ALU.add))
                    dve.wait_ge(mean_ready, job + 1)
                    link(dve.tensor_tensor(dev[:, :], lane_sum[:, :], mean_bank[:, :], ALU.subtract))
                if 2 in parts:
                    link(dve.tensor_tensor(dev[:, :], dev[:, :], dev[:, :], ALU.mult))
                    dve.scalar_tensor_tensor(lane_sq[:, :], lane_sq[:, :], 1.0 / KT, dev[:, :], ALU.mult,
                                             ALU.add).then_inc(lane_var_ready, 1)
                if 3 in parts:
                    dve.wait_ge(std_ready, job + 1)
                    dve.memset(lane_sum[:, :], 0.0)
                    dve.memset(lane_sq[:, :], 0.0)
                    link(dve.reciprocal(rstd[:, :], rstd[:, :]))

            def normalize(t, c):
                dve.tensor_tensor(slab(raw, t), slab(raw, t), mean_bank[:, :], ALU.subtract).then_inc(centered, 1)
                dve.wait_ge(centered, c + 1)
                dve.tensor_tensor(slab(raw, t), slab(raw, t), rstd[:, :], ALU.mult).then_inc(ln_scaled, 1)

            def lo_tile(t, c, odd):
                dve.wait_ge(ln_hi, c + 1)
                dve.tensor_tensor(slab(h_lo, t), gelu_bank[odd][:, :], slab(h_hi, t), ALU.subtract).then_inc(ln_lo, 1)

            dve.memset(lane_sum[:, :], 0.0)
            link(dve.memset(lane_sq[:, :], 0.0))
            for kt in range(KT):
                lo_x(kt, raw[:, kt, :], kt)
                if kt % 4 == 3:
                    lo_w(0, 0, 0, kt // 4)
            for ph in PHASES:
                ln, merge_of = ph.get("ln"), ph.get("merge")

                def step(i, e, first, last, ph=ph, ln=ln, merge_of=merge_of):
                    u, m = ph["unit"] + e, 2 * i + e

                    def lo(q):
                        if not (last and e == 1):
                            lo_w((e + 1) % 2, u + 1, i, q)
                    lo(0)
                    if merge_of is not None and ln is not None and first and e == 0:
                        merge_lanes(merge_of)
                    spread = merge_of is not None and ln is None and first
                    if spread:
                        merge_lanes(merge_of, [0] if e == 0 else [2])
                    behind = ph.get("normalize")
                    if behind is not None and not first:
                        normalize(m - 2, m + (KT * behind - 2))
                    if ph["kind"] == "TX":
                        for j in range(4):
                            if ln is not None:
                                t = 4 * m + j
                                if t < 2:
                                    normalize(KT - 2 + t, KT * (ln + 1) - 2 + t)
                                lo_tile(t, KT * ln + t, t % 2)
                            if j < 3:
                                lo(j + 1)
                        return
                    if ln is not None:
                        normalize(m, m + KT * ln)
                    lo(1)
                    if ln is not None:
                        lo_tile(m, m + KT * ln, e)
                    lo(2)
                    if ph.get("load_x"):
                        lo_x(m, x_stage[:, :], m + KT)
                    lo(3)
                    if ph["kind"] == "G2":
                        dve.wait_ge(s_hi_made, 2 * i + (KT * ph["job"] + e + 1))
                        dve.scalar_tensor_tensor(stage[:, 1, :], bank[e][:, :], col(B2, ph["job"] % 2, m),
                                                 stage[:, 0, :], ALU.add, ALU.subtract).then_inc(acc_evacuated, 1)
                        if splits(ph, i):
                            src, to_hi, to_lo, _ = qkv_slot(e)
                            dve.wait_ge(qkv_hi, 2 * i + (e + 1))
                            dve.tensor_tensor(to_lo, src, to_hi, ALU.subtract).then_inc(qkv_lo, 1)
                    if spread:
                        merge_lanes(merge_of, [1] if e == 0 else [3])
                    if ph["kind"] == "G1":
                        c = KT * ph["job"] + e
                        dve.wait_ge(acc_evacuated, 2 * i + (ph["acc"] + e + 1))
                        dve.wait_ge(stat_done, 2 * i + c)
                        dve.tensor_tensor(dev[:, :], slab(raw, m), raw[:, 0, :], ALU.subtract).then_inc(dev_ready, 1)
                        dve.wait_ge(dev_ready, 2 * i + (c + 1))
                        dve.tensor_tensor(lane_sum[:, :], lane_sum[:, :], dev[:, :], ALU.add)
                        dve.wait_ge(sq_ready, 2 * i + (c + 1))
                        dve.tensor_tensor(lane_sq[:, :], lane_sq[:, :], sq_bank[:, :], ALU.add).then_inc(stat_done, 1)
                steps(dve, ph, step)

        @block.tensor
        def _(pe):
            pe.wait_ge(consts, 2)
            for ph in PHASES:
                ln, merge_of = ph.get("ln"), ph.get("merge")

                def step(i, e, first, last, ph=ph, ln=ln, merge_of=merge_of):
                    u, m = ph["unit"] + e, 2 * i + e
                    start = first and i == 0 and e == 0
                    if ph["kind"] == "TX":
                        if start:
                            pe.wait_ge(acc_evacuated, ph["acc"])
                    else:
                        half = ph["job"] // 2
                        a = ph["acc"] + e
                        if first and a >= 2 and PHASES[PHASES.index(ph) - 1]["kind"] == "TX":
                            pe.wait_ge(acc_evacuated, a - 3)
                        elif not (isinstance(i, int) and a + 2 * i < 2):
                            pe.wait_ge(acc_evacuated, 2 * i + (a - 1))
                        hi, lo = (x_hi, x_lo) if ph["kind"] == "G1" else (h_hi, h_lo)
                    for q in range(4):
                        pe.wait_ge(wl_ready, 8 * i + (4 * u + q + 1))
                        if start and ph["kind"] == "G1":
                            pe.wait_ge(xl_ready, KT * half + 4 * q + 4)
                        if start and ph["kind"] == "G2":
                            pe.wait_ge(ln_lo, KT * ph["job"] + 4 * q + 4)
                        for j in range(4):
                            kt = 4 * q + j
                            if ph["kind"] == "TX":
                                kt = 4 * m + q
                                out, rows = tx_banks[j][:, :], slice(j * P, (j + 1) * P)
                                args = ((x_hi[:, kt, rows], w_hi[:, q, :]), (x_lo[:, kt, rows], w_hi[:, q, :]),
                                        (x_hi[:, kt, rows], w_lo[:, q, :]))
                            else:
                                out, cols = bank[e][:, :], slice(j * P, (j + 1) * P)
                                args = ((w_hi[:, q, cols], hi[:, kt, :]), (w_hi[:, q, cols], lo[:, kt, :]),
                                        (w_lo[:, q, cols], hi[:, kt, :]))
                            for k, (a_, b_) in enumerate(args):
                                mm = pe.matmul(out, a_, b_, start=(kt == 0 and k == 0), stop=(kt == KT - 1 and k == 2))
                        mm.then_inc(w_used, 1)
                        at_once = ln is not None
                        if merge_of is not None and first and (e, q) == ((0, 0) if at_once else (0, 2)):
                            pe.wait_ge(lane_mean_ready, merge_of + 1)
                            pe.matmul(mean_bank[:, :], ones[:, :], lane_sum[:, :], start=True, stop=True)\
                              .then_inc(mean_ready, 1)
                        if merge_of is not None and first and (e, q) == ((0, 2) if at_once else (1, 2)):
                            pe.wait_ge(lane_var_ready, merge_of + 1)
                            pe.matmul(sq_bank[:, :], ones[:, :], lane_sq[:, :], start=True, stop=True)\
                              .then_inc(var_ready, 1)
                steps(pe, ph, step)


QKV_UNITS = 6
QKV, WO, INT, MEAS, POST, TOPZ, TOP2W = 0, 12, 14, 22, 24, 25, 26
UNITS2 = 27
QKV_ORDER = [(0, 0, 0), (1, 0, 4), (0, 1, 0), (1, 1, 4), (2, 1, 0), (2, 0, 0)]


def halves(pair):
    return [2 * (2 * w + part) + half for half in range(2) for w, part, _ in pair]


TURN = [
    ("att", halves(QKV_ORDER[0:2]) + halves(QKV_ORDER[2:4])),
    ("tail", [MEAS, MEAS + 1]),
    ("inter", [WO, WO + 1, INT, INT + 1]),
    ("tail", [POST]),
    ("inter", range(INT + 2, INT + 8)),
    ("tail", [TOPZ]),
    ("att", halves(QKV_ORDER[4:5])),
    ("tail", [TOP2W]),
    ("att", halves(QKV_ORDER[5:6])),
]
RING = 3
Q_I, K_R, V_R, V_I = (2 * k for k in (1, 2, 4, 5))
S_LOADS = {Q_I: (K_R, 1, 0), Q_I + 1: (K_R + 1, 1, 1), V_R: (V_I, 0, 0), V_R + 1: (V_I + 1, 0, 1)}


def turn_units(i):
    parts = dict(att=i is None or i < NT, inter=i is None or 1 <= i <= NT, tail=i is None or i >= 2)
    turn = TURN
    if i == NT - 1:
        turn = TURN[0:3] + [TURN[6], TURN[8]] + TURN[3:6] + [TURN[7]]
    elif i == NT:
        turn = [p for p in TURN if p[0] != "tail"] + [p for p in TURN if p[0] == "tail"]
    return [u for part, units in turn for u in units if parts[part]]


PAIRS = [(0, 3, 1), (3, 2, 2), (5, 1, 3)]
PAIR_AT = {}
for _f, _c, _a in PAIRS:
    for _i in range(_c):
        PAIR_AT[(_i, _i + _a)] = _f + _i
CH = 256
SCORE_STEPS, PV_STEPS, TAIL_STEPS, PHASE_STEPS = 32, 22, 7, 56


def mix(nc, dram, early, early_loaded):
    with ExitStack() as ctx:
        def sb(name, shape, dt=F32):
            return ctx.enter_context(nc.sbuf_tensor(name, shape, dt))

        def sem(name):
            return ctx.enter_context(nc.semaphore(name))

        early_buffers(nc, ctx, "_place")
        s_in, w_qkv, w2, rows, cols, ids = (early[k] for k in ("s_in", "w_qkv", "w2", "rows", "cols", "ids"))
        q_sb = sb("q_sb", [P, N, 2, D])
        k_sb = sb("k_sb", [P, N, 2, D])
        v_sb = sb("v_sb", [P, N, 2, D])
        work = sb("work", [P, 4096])
        a_t = sb("a_t", [P, 2, DT, D])
        na_t = sb("na_t", [P, DT, D])
        ri_sb = sb("ri_sb", [P, 2, N, D])
        pa = sb("pa", [P, N * D])
        pb = sb("pb", [P, 6 * CH])
        zero = sb("zero", [P, N, D], BF16)
        pair_zero = sb("pair_zero", [P, 6, D], BF16)
        sup = sb("sup", [P, 2, D])
        sup_t = sb("sup_t", [P, 3, DT, P])
        x_t = sb("x_t", [P, DT, P])
        ta = sb("ta", [P, D])
        tb = sb("tb", [P, D])
        x1 = sb("x1", [P, TOP1])
        ident = sb("ident", [P, P])
        strength = sb("strength", [P, NT, N, N])
        st = sb("st", [P, N * N])
        sc = pb[:, 0:512].rearrange("p (n k m r h) -> p n k m r h", n=N, k=2, m=N, r=2)
        ar, ai, mag = (pb[:, 512 + 128 * j:640 + 128 * j].rearrange("p (n m h) -> p n m h", n=N, m=N)
                       for j in range(3))
        w_att = sb("w_att", [P, N, N, H])
        mx = sb("mx", [P, N, H])
        small = sb("small", [P, 8])
        eps2 = sb("eps2", [P, 1])
        y_all = sb("y_all", [P, NT])
        bank = [ctx.enter_context(nc.psum_tensor(f"bank2_{i}", [P, 512], F32)) for i in range(8)]

        o_sb = a_t[:, :, :, :].rearrange("p r f c -> p (r f c)").rearrange("p (r n d) -> p n r d", n=N, r=2)
        out_t = [na_t[:, :, :], pa[:, :].rearrange("p (f c) -> p f c", f=DT)]
        bq, bk = rows[:, 0:1024], rows[:, 1024:2048]
        post_b, post_g, post_be = (rows[:, 2048 + D * j:2048 + D * (j + 1)] for j in range(3))
        b_top1, b_top2, w3 = rows[:, 3584:4096], rows[:, 4096:4352], rows[:, 4352:4608]

        w2_loaded, s_loaded = early_loaded["w2"], early_loaded["s"]
        names = """x1_loaded consts2 gathered ident_made
            qkv_front qkv_done qkv_evacuated biased biased_real score scored softmax mag_ready exp_in exp_ready pv out_ready
            out_transposed out_t_ready o_done a_ready na_ready int_done int_evacuated
            squared n2_ready mask_made pair_zero_made ln_ready y_ready ysq_ready phase norm_root norm_sq_ready
            norm_ready sup_scaled sup_transposed sup_t_ready meas_done meas_sq amp_sq_ready amp_ready
            amp_transposed amp_t_ready post_done tail mean2_ready var2_ready std2_ready pre_gelu z_ready
            z_transposed z_t_ready topz_done h1_ready h1_transposed h1_t_ready top2_done top2_ready y_done
            y_stored""".split()
        S = {n: sem("m_" + n) for n in names}

        def turns(eng, body):
            body(0, True, False, False)
            body(1, True, True, False)
            body(2, True, True, True)
            with eng.Fori(3, NT - 1) as i:
                body(i, True, True, True)
            body(NT - 1, True, True, True)
            body(NT, False, True, True)
            body(NT + 1, False, False, True)

        def first_unit(i):
            return sum(len(turn_units(j)) for j in range(i))

        def place(i, k):
            if isinstance(i, int):
                u = first_unit(i) + k
                return u % RING, 16 * (u // RING + 1)
            k += first_unit(2) - 2 * UNITS2
            return k % RING, (16 * UNITS2 // RING) * i + 16 * (k // RING + 1)

        def product(i, unit):
            if unit < WO:
                k, half = unit // 2, unit % 2
                order = [2 * w + part for w, part, _ in QKV_ORDER].index(k)
                return (S["qkv_done"], 24 * i + 4 * (order + 1)) if half else (S["qkv_front"], 6 * i + (order + 1))
            if unit < INT:
                return S["o_done"], 8 * i + (4 * (unit - WO + 1) - 8)
            if unit < MEAS:
                return S["int_done"], 8 * i + (unit - INT + 1 - 8)
            if unit < POST:
                return S["meas_done"], 2 * i + (unit - MEAS + 1 - 4)
            return S[{POST: "post_done", TOPZ: "topz_done", TOP2W: "top2_done"}[unit]], i - 1

        def units_of(i):
            return turn_units(i if isinstance(i, int) else None)

        def is_last(i):
            return isinstance(i, int) and i == NT - 1

        def closing(i):
            return isinstance(i, int) and i == NT

        def out_of(t, n, part):
            return (q_sb if is_last(t) else o_sb)[:, n, part, :]

        def out_t_of(t, part):
            if not is_last(t):
                return out_t[part]
            return k_sb[:, 2 * part:2 * part + 2, :, :].rearrange("p n r d -> p (n r) d")

        def ri_of(t):
            return v_sb[:, :, :, :].rearrange("p n r d -> p (n r d)").rearrange("p (r n d) -> p r n d", r=2, n=N) \
                if is_last(t) else ri_sb

        block = ctx.enter_context(nc.Block())

        @block.sync
        def _(sp):
            def body(i, att, inter, tail):
                units = units_of(i)
                before = [] if isinstance(i, int) and i == 0 else units_of(i - 1)

                def load_s(t, part, half, after):
                    src = dram["s"]
                    src = src[t, part, :, half] if isinstance(t, int) else \
                        src[bass.ds(t, 1), part, :, half].rearrange("t n p x -> (t n) p x")
                    sp.wait_ge(*after)
                    sp.dma_start(s_in[:, half, :].rearrange("p (n x) -> p n x", n=N),
                                 src.rearrange("n p x -> p n x")).then_inc(s_loaded[half], 16)

                for k, unit in enumerate(units):
                    if k < RING and not before:
                        continue
                    slot, _ = place(i, k)
                    if att and before and k in (1, 2):
                        load_s(i, 0, k - 1, product(i - 1, before[k - RING]))
                    if unit in S_LOADS:
                        last_use, part, half = S_LOADS[unit]
                        load_s(i, part, half, product(i, last_use))
                    if k >= RING:
                        sp.wait_ge(*product(i, units[k - RING]))
                    else:
                        sp.wait_ge(*product(i - 1, before[k - RING]))
                    if unit < WO:
                        sp.dma_start(w_qkv[:, slot, :], dram["wqkv"][unit // 2, unit % 2]).then_inc(w2_loaded[slot], 16)
                    else:
                        size = DT * TOP2 if unit == TOP2W else UNIT
                        sp.dma_start(w2[:, slot, 0:size], dram["ws2"][unit - WO + QKV_UNITS, :, 0:size])\
                          .then_inc(w2_loaded[slot], 16)
                    if unit == MEAS:
                        sp.wait_ge(S["tail"], TAIL_STEPS * (i - 2))
                        src = dram["t1x"]
                        src = src[i - 2] if isinstance(i, int) else \
                            src[bass.ds(i - 2, 1)].rearrange("a p c -> p (a c)")
                        sp.dma_start(x1[:, :], src).then_inc(S["x1_loaded"], 16)
            turns(sp, body)
            sp.wait_ge(S["y_done"], NT)
            sp.dma_start(dram["out"], y_all[:, :]).then_inc(S["y_stored"], 16)
            sp.wait_ge(S["y_stored"], 16)

        @block.gpsimd
        def _(pool):
            pool.memset(eps2[:, :], EPS_LN).then_inc(S["consts2"], 1)
            pool.memset(ident[:, :], 0.0).then_inc(S["consts2"], 1)
            pool.wait_ge(S["consts2"], 2)
            pool.affine_select(out=ident[:, :], in_=ident[:, :], compare_op=ALU.not_equal, fill=1.0, base=0,
                               pattern=[[-1, P]], channel_multiplier=1).then_inc(S["ident_made"], 1)
            pool.wait_ge(early_loaded["rows"], 16)
            pool.wait_ge(early_loaded["ids"], 16)
            for t in range(NT):
                for f in range(N):
                    pool.indirect_dma_start(strength[:, t, f, :], None, dram[f"tbl{f}"],
                                            bass.IndirectOffsetOnAxis(ap=ids[:, t, f:f + 1], axis=0))\
                        .then_inc(S["gathered"], 16)

            def body(i, att, inter, tail):
                if att:
                    for which in range(2):
                        buf, row = ((q_sb, bq), (k_sb, bk))[which]
                        pool.wait_ge(S["qkv_evacuated"], 24 * i + (4, 8)[which])
                        pool.tensor_tensor(buf[:, :, 0, :], buf[:, :, 0, :],
                                           row[:, 0:D].unsqueeze(1).broadcast_to([P, N, D]), ALU.add)\
                            .then_inc(S["biased_real"], 1)
                if not inter:
                    return
                pool.wait_ge(S["mask_made"], i)
                for f, c, apart in PAIRS:
                    last = pool.tensor_tensor(pair_zero[:, f:f + c, :], zero[:, 0:c, :],
                                              zero[:, apart:apart + c, :], ALU.add)
                    last.then_inc(S["pair_zero_made"], 1)
            turns(pool, body)

        @block.scalar
        def _(act):
            act.wait_ge(S["consts2"], 2)
            act.wait_ge(early_loaded["cols"], 16)

            def qkv(t, order):
                for k in order:
                    what, part, first_bank = QKV_ORDER[k]
                    if k == 0:
                        act.wait_ge(S["score"], SCORE_STEPS * t)
                    if k == 4:
                        act.wait_ge(S["out_ready"], 2 * t)
                    for n in range(N):
                        act.wait_ge(S["qkv_done"], 24 * t + (4 * k + n + 1))
                        act.copy((q_sb, k_sb, v_sb)[what][:, n, part, :], bank[first_bank + n][:, :])\
                           .then_inc(S["qkv_evacuated"], 1)

            def interference(t, n):
                act.wait_ge(S["int_done"], 8 * t + (2 * n + 2))
                if n == 0 and not is_last(t):
                    act.wait_ge(S["norm_ready"], t)
                for part in range(2):
                    act.copy(ri_of(t)[:, part, n, :], bank[2 * (n % 2) + part][:, :]).then_inc(S["int_evacuated"], 1)

            def sup_transpose(t):
                act.wait_ge(S["sup_transposed"], t + 1)
                act.copy(sup_t[:, 0].rearrange("p k c -> p (k c)"), bank[6][:, :]).then_inc(S["sup_t_ready"], 1)
                act.copy(sup_t[:, 1].rearrange("p k c -> p (k c)"), bank[7][:, :]).then_inc(S["sup_t_ready"], 1)
                act.mul(sup_t[:, 2].rearrange("p k c -> p (k c)"), bank[7][:, :], -1.0).then_inc(S["sup_t_ready"], 1)

            def tail_squares(t):
                act.wait_ge(S["meas_done"], 2 * t + 2)
                act.wait_ge(S["y_done"], t)
                act.activation(ta[:, :], bank[4][:, :], ACT.Square).then_inc(S["meas_sq"], 1)
                act.activation(tb[:, :], bank[5][:, :], ACT.Square).then_inc(S["meas_sq"], 1)

            def tail_amplitude(t):
                act.wait_ge(S["amp_sq_ready"], t + 1)
                act.activation(tb[:, :], ta[:, :], ACT.Sqrt).then_inc(S["amp_ready"], 1)

            def tail_amp_t(t):
                act.wait_ge(S["amp_transposed"], t + 1)
                act.copy(x_t[:, :, :].rearrange("p k c -> p (k c)"), bank[6][:, :]).then_inc(S["amp_t_ready"], 1)

            def tail_post(t):
                act.wait_ge(S["mean2_ready"], t + 1)
                act.activation(tb[:, :], ta[:, :], ACT.Square, bias=small[:, 2:3],
                               accum_out=small[:, 1:2]).then_inc(S["var2_ready"], 1)
                act.wait_ge(S["var2_ready"], t + 1)
                act.activation(small[:, 0:1], small[:, 1:2], ACT.Sqrt, bias=eps2[:, :],
                               scale=1.0 / D).then_inc(S["std2_ready"], 1)
                act.wait_ge(S["pre_gelu"], t + 1)
                act.activation(ta[:, :], tb[:, :], ACT.Gelu).then_inc(S["z_ready"], 1)

            def tail_z_t(t):
                act.wait_ge(S["z_transposed"], t + 1)
                act.copy(x_t[:, :, :].rearrange("p k c -> p (k c)"), bank[7][:, :]).then_inc(S["z_t_ready"], 1)

            def tail_h1_t(t):
                act.wait_ge(S["h1_transposed"], t + 1)
                act.copy(x_t[:, :, :].rearrange("p k c -> p (k c)"), bank[6][:, :]).then_inc(S["h1_t_ready"], 1)

            def tail_top2(t):
                act.wait_ge(S["top2_done"], t + 1)
                act.copy(ta[:, 0:TOP2], bank[4][:, 0:TOP2]).then_inc(S["top2_ready"], 1)

            def softmax(t):
                act.wait_ge(S["scored"], t + 1)
                act.activation(mag[:, :, :, :], ar[:, :, :, :], ACT.Sqrt).then_inc(S["mag_ready"], 1)
                act.wait_ge(S["exp_in"], t + 1)
                act.activation(mag[:, :, :, :], ai[:, :, :, :], ACT.Exp, scale=HD ** -0.5).then_inc(S["exp_ready"], 1)

            def out_transpose(t, parts):
                act.wait_ge(S["int_done"], 8 * t)
                for j in range(4 * parts[0], 4 * parts[-1] + 4):
                    act.wait_ge(S["out_transposed"], 8 * t + (j + 1))
                    if j == 4 and not is_last(t):
                        act.wait_ge(S["norm_ready"], t)
                    act.activation(out_t_of(t, j // 4)[:, j % 4, :], bank[6 + j % 2][:, :], ACT.Identity,
                                   bias=cols[:, j // 4, j % 4:j % 4 + 1]).then_inc(S["out_t_ready"], 1)

            def projection(t, js):
                for j in js:
                    act.wait_ge(S["o_done"], 8 * t + (j + 1))
                    act.activation(a_t[:, j // 4, j % 4, :], bank[j % 4][:, :], ACT.Identity,
                                   bias=cols[:, 2 + j // 4, j % 4:j % 4 + 1]).then_inc(S["a_ready"], 1)
                    if j >= 4:
                        act.wait_ge(S["a_ready"], 8 * t + (j + 1))
                        act.mul(na_t[:, j % 4, :], a_t[:, 1, j % 4, :], -1.0).then_inc(S["na_ready"], 1)

            def squares(t, att):
                act.wait_ge(S["norm_ready"], t)
                if att and not is_last(t + 1):
                    act.wait_ge(S["score"], SCORE_STEPS * t + 2 * SCORE_STEPS)
                else:
                    act.wait_ge(S["out_ready"], 2 * NT)
                act.wait_ge(S["int_evacuated"], 8 * t + 8)
                for part in range(2):
                    act.activation(work[:, part * 2048:(part + 1) * 2048],
                                   ri_of(t)[:, part, :, :].rearrange("p n d -> p (n d)"), ACT.Square)\
                       .then_inc(S["squared"], 1)

            def unit_vectors(t, between=lambda: None):
                act.wait_ge(S["n2_ready"], t + 1)
                act.activation(work[:, 2048:4096], work[:, 0:2048], ACT.Ln).then_inc(S["ln_ready"], 1)
                act.wait_ge(S["ln_ready"], t + 1)
                act.activation(work[:, 2048:4096], work[:, 2048:4096], ACT.Exp, scale=-0.5).then_inc(S["y_ready"], 1)
                between()
                act.wait_ge(S["y_ready"], t + 1)
                act.activation(pa[:, :], work[:, 2048:4096], ACT.Square).then_inc(S["ysq_ready"], 1)

            def norm_root(t):
                act.wait_ge(S["norm_sq_ready"], t + 1)
                act.activation(small[:, 5:6], small[:, 4:5], ACT.Sqrt).then_inc(S["norm_root"], 1)

            def scale_sup(t):
                act.wait_ge(S["norm_ready"], t + 1)
                for part in range(2):
                    act.activation(sup[:, part, :], sup[:, part, :], ACT.Copy, scale=small[:, 6:7])\
                       .then_inc(S["sup_scaled"], 1)

            def body(i, att, inter, tail):
                if closing(i):
                    projection(i - 1, range(8))
                    for n in range(N):
                        interference(i - 1, n)
                    norm_root(i - 2)
                    scale_sup(i - 2)
                    squares(i - 1, False)
                    sup_transpose(i - 2)
                    unit_vectors(i - 1)
                    for part in (tail_squares, tail_amplitude, tail_amp_t, tail_post, tail_z_t, tail_h1_t, tail_top2):
                        part(i - 2)
                    return
                if att:
                    qkv(i, range(0, 2))
                if tail:
                    norm_root(i - 2)
                if att:
                    qkv(i, [2])
                if tail:
                    scale_sup(i - 2)
                if att:
                    qkv(i, [3] if inter else [3, 4, 5])
                if tail:
                    sup_transpose(i - 2)
                if tail:
                    tail_squares(i - 2)
                if inter:
                    for part in range(2):
                        out_transpose(i - 1, [part])
                        projection(i - 1, range(4 * part, 4 * part + 4))
                if tail:
                    tail_amplitude(i - 2)
                if inter:
                    interference(i - 1, 0)
                if is_last(i):
                    qkv(i, [4, 5])
                if tail:
                    tail_amp_t(i - 2)
                    tail_post(i - 2)
                if inter:
                    interference(i - 1, 1)
                if att:
                    softmax(i)
                if inter:
                    interference(i - 1, 2)
                if tail:
                    tail_z_t(i - 2)
                if inter:
                    interference(i - 1, 3)
                if is_last(i):
                    tail_h1_t(i - 2)
                    tail_top2(i - 2)
                    squares(i - 1, att)
                    out_transpose(i, [0, 1])
                    unit_vectors(i - 1)
                    return
                if inter:
                    squares(i - 1, att)
                    unit_vectors(i - 1, (lambda: tail_h1_t(i - 2)) if tail else lambda: None)
                elif tail:
                    tail_h1_t(i - 2)
                if att and inter:
                    qkv(i, [4])
                if tail:
                    tail_top2(i - 2)
                if att and inter:
                    qkv(i, [5])
            turns(act, body)

        @block.vector
        def _(dve):
            class Chain:

                def __init__(self, name, per_tile, t):
                    self.sem, self.per, self.t, self.k = S[name], per_tile, t, 0

                def step(self, ins):
                    self.k += 1
                    ins.then_inc(self.sem, 1)
                    return self.k

                def wait(self, k):
                    dve.wait_ge(self.sem, self.t * self.per + k)

            def bias(t, which):
                buf, row = ((q_sb, bq), (k_sb, bk))[which]
                dve.wait_ge(S["qkv_evacuated"], 24 * t + (12, 16)[which])
                dve.tensor_tensor(buf[:, :, 1, :], buf[:, :, 1, :],
                                  row[:, D:2 * D].unsqueeze(1).broadcast_to([P, N, D]), ALU.add)\
                   .then_inc(S["biased"], 1)

            def scores(ch, n):
                if n == 0:
                    dve.wait_ge(S["biased"], 2 * ch.t + 2)
                    dve.wait_ge(S["biased_real"], 2 * ch.t + 2)
                    dve.wait_ge(S["out_ready"], 2 * ch.t)
                halves = [work[:, 2048 * j:2048 * (j + 1)] for j in range(2)]
                for kind in range(2):
                    made = []
                    for j in range(2):
                        if ch.k >= 2:
                            ch.wait(ch.k - 1)
                        qn = q_sb[:, n, :, :] if kind == 0 else q_sb[:, n, ::-1, :]
                        qn = qn.unsqueeze(1).broadcast_to([P, 2, 2, D])
                        km = k_sb[:, 2 * j:2 * j + 2, :, :]
                        made.append(ch.step(dve.tensor_tensor(halves[j].rearrange("p (m r d) -> p m r d", m=2, r=2),
                                                              qn, km, ALU.mult)))
                    for j in range(2):
                        ch.wait(made[j])
                        ch.step(dve.tensor_reduce(
                            sc[:, n, kind, 2 * j:2 * j + 2].rearrange("p m r h -> p (m r h)"),
                            halves[j].rearrange("p (x d) -> p x d", d=HD), AX.X, ALU.add))

            def softmax(t):
                c = Chain("softmax", 8, t)
                dve.wait_ge(S["score"], SCORE_STEPS * t + SCORE_STEPS)
                c.step(dve.tensor_tensor(ar[:, :, :, :], sc[:, :, 0, :, 0, :], sc[:, :, 0, :, 1, :], ALU.add))
                c.step(dve.tensor_tensor(ai[:, :, :, :], sc[:, :, 1, :, 0, :], sc[:, :, 1, :, 1, :], ALU.subtract))
                c.wait(1)
                c.step(dve.tensor_tensor(ar[:, :, :, :], ar[:, :, :, :], ar[:, :, :, :], ALU.mult))
                c.wait(2)
                c.step(dve.tensor_tensor(ai[:, :, :, :], ai[:, :, :, :], ai[:, :, :, :], ALU.mult))
                c.wait(4)
                dve.scalar_tensor_tensor(ar[:, :, :, :].rearrange("p n m h -> p (n m h)"),
                                         ar[:, :, :, :].rearrange("p n m h -> p (n m h)"), EPS_MAG,
                                         ai[:, :, :, :].rearrange("p n m h -> p (n m h)"), ALU.add,
                                         ALU.add).then_inc(S["scored"], 1)
                dve.wait_ge(S["mag_ready"], t + 1)
                c.step(dve.tensor_reduce(mx[:, :, :], mag[:, :, :, :].rearrange("p n m h -> p n h m"), AX.X, ALU.max))
                c.wait(5)
                dve.tensor_tensor(ai[:, :, :, :], mag[:, :, :, :],
                                  mx[:, :, :].unsqueeze(2).broadcast_to([P, N, N, H]),
                                  ALU.subtract).then_inc(S["exp_in"], 1)
                dve.wait_ge(S["exp_ready"], t + 1)
                c.step(dve.tensor_reduce(mx[:, :, :], mag[:, :, :, :].rearrange("p n m h -> p n h m"), AX.X, ALU.add))
                c.wait(6)
                c.step(dve.reciprocal(mx[:, :, :], mx[:, :, :]))
                c.wait(7)
                c.step(dve.tensor_tensor(w_att[:, :, :, :], mag[:, :, :, :],
                                         mx[:, :, :].unsqueeze(2).broadcast_to([P, N, N, H]), ALU.mult))
                c.wait(8)

            def attend(c, t, part):
                if part == 0:
                    dve.wait_ge(S["qkv_evacuated"], 24 * t + 24)
                    if not is_last(t):
                        dve.wait_ge(S["int_done"], 8 * t)
                halves = [work[:, 2048 * j:2048 * (j + 1)] for j in range(2)]
                for pair in range(2):
                    a, b = [], []
                    for j in range(2):
                        n = 2 * pair + j
                        if pair:
                            c.wait(c.k - 1)
                        elif part and j:
                            dve.wait_ge(S["out_ready"], 2 * t + 1)
                        elif part:
                            c.wait(c.k)
                        vm = v_sb[:, :, part, :].rearrange("p m (h d) -> p m h d", h=H)
                        w = w_att[:, n, :, :].unsqueeze(3).broadcast_to([P, N, H, HD])
                        a.append(c.step(dve.tensor_tensor(halves[j].rearrange("p (m h d) -> p m h d", m=N, h=H),
                                                          vm, w, ALU.mult)))
                    for j in range(2):
                        c.wait(a[j])
                        b.append(c.step(dve.tensor_tensor(halves[j][:, 0:1024], halves[j][:, 0:1024],
                                                          halves[j][:, 1024:2048], ALU.add)))
                    for j in range(2):
                        c.wait(b[j])
                        ins = dve.tensor_tensor(out_of(t, 2 * pair + j, part), halves[j][:, 0:512],
                                                halves[j][:, 512:1024], ALU.add)
                        if pair == 1 and j == 1:
                            ins.then_inc(S["out_ready"], 1)
                        else:
                            c.step(ins)

            def tail_stage(t, n):
                c = Chain("tail", TAIL_STEPS, t)
                c.k = {0: 0, 1: 1, 2: 5, 3: 6}[n]
                if n == 0:
                    dve.wait_ge(S["meas_sq"], 2 * t + 2)
                    dve.tensor_tensor(ta[:, :], ta[:, :], tb[:, :], ALU.add).then_inc(S["amp_sq_ready"], 1)
                    dve.wait_ge(S["x1_loaded"], 16 * t + 16)
                    c.step(dve.tensor_tensor(x1[:, :], x1[:, :], b_top1, ALU.add))
                if n == 1:
                    dve.wait_ge(S["post_done"], t + 1)
                    c.step(dve.scalar_tensor_tensor(ta[:, :], bank[4][:, :], 1.0, post_b, ALU.mult, ALU.add,
                                                    accum_out=small[:, 7:8]))
                    c.wait(2)
                    dve.tensor_scalar(small[:, 2:3], small[:, 7:8], -1.0 / D, None,
                                      ALU.mult).then_inc(S["mean2_ready"], 1)
                    dve.wait_ge(S["std2_ready"], t + 1)
                    c.step(dve.reciprocal(small[:, 1:2], small[:, 0:1]))
                    c.wait(3)
                    c.step(dve.tensor_scalar(tb[:, :], ta[:, :], small[:, 2:3], small[:, 1:2], ALU.add, ALU.mult))
                    c.wait(4)
                    c.step(dve.tensor_tensor(tb[:, :], tb[:, :], post_g, ALU.mult))
                    c.wait(5)
                    dve.tensor_tensor(tb[:, :], tb[:, :], post_be, ALU.add).then_inc(S["pre_gelu"], 1)
                if n == 2:
                    dve.wait_ge(S["topz_done"], t + 1)
                    c.step(dve.tensor_tensor(tb[:, :], bank[5][:, :], x1[:, :], ALU.add))
                    c.wait(6)
                    dve.tensor_scalar(tb[:, :], tb[:, :], 0.0, None, ALU.max).then_inc(S["h1_ready"], 1)
                if n == 3:
                    dve.wait_ge(S["top2_ready"], t + 1)
                    c.step(dve.tensor_tensor(ta[:, 0:TOP2], ta[:, 0:TOP2], b_top2, ALU.add))
                    c.wait(7)
                    dve.scalar_tensor_tensor(ta[:, TOP2:2 * TOP2], ta[:, 0:TOP2], 0.0, w3, ALU.max, ALU.mult,
                                             accum_out=y_all[:, t:t + 1] if isinstance(t, int) else y_all[:, bass.ds(t, 1)])\
                       .then_inc(S["y_done"], 1)

            def superposition(t, between=lambda k: None):
                c = Chain("phase", PHASE_STEPS, t)
                ri_all = ri_of(t)
                t0, t1 = work[:, 0:2048], work[:, 2048:4096]
                if isinstance(t, int) and t == 0:
                    dve.wait_ge(S["gathered"], 16 * NT * N)
                dve.wait_ge(S["squared"], 2 * t + 2)
                a = c.step(dve.tensor_tensor(t0, t0, t1, ALU.add))
                dve.wait_ge(S["pair_zero_made"], 3 * t)
                c.wait(a)
                dve.tensor_scalar(zero[:, :, :].rearrange("p n d -> p (n d)"), t0, 0.0, None,
                                  ALU.is_equal).then_inc(S["mask_made"], 1)
                dve.wait_ge(S["mask_made"], t + 1)
                dve.tensor_scalar(t0, t0, 1e-37, None, ALU.max).then_inc(S["n2_ready"], 1)
                c.step(dve.tensor_copy(st[:, :], strength[:, t, :, :].rearrange("p i j -> p (i j)") if isinstance(t, int)
                                       else strength[:, bass.ds(t, 1), :, :].rearrange("p a i j -> p (a i j)")))
                between(-1)
                dve.wait_ge(S["ysq_ready"], t + 1)
                a = c.step(dve.tensor_tensor(pa[:, :], pa[:, :], t0, ALU.mult))
                c.wait(a)
                a = c.step(dve.scalar_tensor_tensor(t1, pa[:, :], 3.0, t1, ALU.subtract, ALU.mult))
                c.wait(a)
                ri = [ri_all[:, part, :, :].rearrange("p n d -> p (n d)") for part in range(2)]
                c.step(dve.scalar_tensor_tensor(t0, ri[0], -0.5, t1, ALU.mult, ALU.mult))
                a = c.step(dve.scalar_tensor_tensor(pa[:, :], ri[1], -0.5, t1, ALU.mult, ALU.mult))
                c.wait(a)
                dve.wait_ge(S["pair_zero_made"], 3 * t + 3)
                cos = t0.rearrange("p (n d) -> p n d", n=N)
                sin = pa[:, :].rearrange("p (n d) -> p n d", n=N)
                xx = t1[:, 0:6 * CH].rearrange("p (j d) -> p j d", j=6)
                yy = pb[:, :].rearrange("p (j d) -> p j d", j=6)
                w = pb[:, 0:N * CH].rearrange("p (j d) -> p j d", j=N)
                prod = t1.rearrange("p (r j d) -> p r j d", r=2, j=N)
                between(0)
                for e in range(0, D, CH):
                    cs = slice(e, e + CH)
                    for f, k, apart in PAIRS:
                        c.step(dve.tensor_tensor(xx[:, f:f + k, :], cos[:, 0:k, cs], cos[:, apart:apart + k, cs], ALU.mult))
                        a = c.step(dve.tensor_tensor(yy[:, f:f + k, :], sin[:, 0:k, cs], sin[:, apart:apart + k, cs],
                                                     ALU.mult))
                    c.wait(a)
                    a = c.step(dve.tensor_tensor(xx, xx, yy, ALU.add))
                    c.wait(a)
                    a = c.step(dve.tensor_tensor(xx, xx, pair_zero[:, :, cs], ALU.add))
                    c.wait(a)
                    last = {}
                    for step in range(3):
                        for j in range(N):
                            i = [i for i in range(N) if i != j][step]
                            f = xx[:, PAIR_AT[(min(i, j), max(i, j))], :]
                            s_ij = st[:, N * i + j:N * i + j + 1]
                            if step == 0:
                                ins = dve.tensor_scalar(w[:, j, :], f, s_ij, st[:, (N + 1) * j:(N + 1) * j + 1],
                                                        ALU.mult, ALU.add)
                            else:
                                c.wait(last[j])
                                ins = dve.scalar_tensor_tensor(w[:, j, :], f, s_ij, w[:, j, :], ALU.mult, ALU.add)
                            last[j] = c.step(ins)
                    c.wait(last[3])
                    for part in range(2):
                        a = c.step(dve.tensor_tensor(prod[:, part, :, :], ri_all[:, part, :, cs], w, ALU.mult))
                    c.wait(a)
                    a = c.step(dve.tensor_tensor(prod[:, :, 0:2, :], prod[:, :, 0:2, :], prod[:, :, 2:4, :], ALU.add))
                    c.wait(a)
                    if e == 0:
                        dve.wait_ge(S["sup_transposed"], t)
                    a = c.step(dve.tensor_tensor(sup[:, :, cs], prod[:, :, 0, :], prod[:, :, 1, :], ALU.add))
                    c.wait(a)
                    between(e // CH + 1)
                for part in range(2):
                    a = c.step(dve.scalar_tensor_tensor(t1[:, part * D:(part + 1) * D], sup[:, part, :], 1.0,
                                                        sup[:, part, :], ALU.mult, ALU.mult,
                                                        accum_out=small[:, 3 + part:4 + part]))
                c.wait(a)
                dve.scalar_tensor_tensor(small[:, 4:5], small[:, 3:4], EPS_MAG, small[:, 4:5], ALU.add,
                                         ALU.add).then_inc(S["norm_sq_ready"], 1)
                assert c.k == PHASE_STEPS, c.k
                between(3)

            def norm(t):
                dve.wait_ge(S["norm_root"], t + 1)
                dve.reciprocal(small[:, 6:7], small[:, 5:6]).then_inc(S["norm_ready"], 1)

            dve.wait_ge(early_loaded["rows"], 16)

            def body(i, att, inter, tail):
                if closing(i):
                    superposition(i - 1, lambda k: tail_stage(i - 2, k) if k >= 0 else None)
                    norm(i - 1)
                    return
                if att:
                    bias(i, 0)
                    bias(i, 1)
                    ch = Chain("score", SCORE_STEPS, i)
                    scores(ch, 0)
                if tail:
                    tail_stage(i - 2, 0)
                if att:
                    scores(ch, 1)
                    scores(ch, 2)
                    if is_last(i):
                        scores(ch, 3)
                if tail:
                    tail_stage(i - 2, 1)
                if att:
                    if not is_last(i):
                        scores(ch, 3)
                    assert ch.k == SCORE_STEPS, ch.k
                if att:
                    softmax(i)
                if is_last(i):
                    c = Chain("pv", PV_STEPS, i)
                    attend(c, i, 0)
                    attend(c, i, 1)
                    tail_stage(i - 2, 2)
                    tail_stage(i - 2, 3)
                    superposition(i - 1)
                    norm(i - 1)
                    return

                def late_tail(k):
                    if tail and k in (-1, 1):
                        tail_stage(i - 2, 2 if k == -1 else 3)
                if inter:
                    superposition(i - 1, late_tail)
                else:
                    late_tail(-1)
                    late_tail(1)
                if inter:
                    norm(i - 1)
                if att:
                    c = Chain("pv", PV_STEPS, i)
                    attend(c, i, 0)
                    attend(c, i, 1)
                    assert c.k == PV_STEPS, c.k
            turns(dve, body)

        @block.tensor
        def _(pe):
            def body(i, att, inter, tail):
                at = [0]

                def next_unit():
                    slot, loaded = place(i, at[0])
                    at[0] += 1
                    pe.wait_ge(w2_loaded[slot], loaded)
                    return w2[:, slot, :].rearrange("p (k c) -> p k c", k=DT)

                def transposes(out, src, name):
                    for k in range(DT):
                        ins = pe.transpose(out[:, k * P:(k + 1) * P], src[:, k * P:(k + 1) * P], ident[:, :])
                    if name:
                        ins.then_inc(S[name], 1)

                def product_of(out, lhs, rhs, name=None, start=True, stop=True):
                    for kt in range(DT):
                        mm = pe.matmul(out, lhs(kt), rhs(kt), start=start and kt == 0, stop=stop and kt == DT - 1)
                    if name:
                        mm.then_inc(S[name], 1)

                def qkv(t, pairs):
                    for group in pairs:
                        for half in range(2):
                            for k in group:
                                what, part, first_bank = QKV_ORDER[k]
                                next_unit()
                                slot = place(i, at[0] - 1)[0]
                                w = w_qkv[:, slot, :].rearrange("p (j k c) -> p j k c", j=2, k=2).bitcast(F32R)
                                s_half = s_in[:, half, :].rearrange("p (n j k c) -> p n j k c", n=N, j=2, k=2)\
                                    .bitcast(F32R)
                                pe.wait_ge(s_loaded[half], 48 * t + 16 * (1, 1, 2, 2, 2, 3)[k])
                                if half == 0:
                                    if k == 1 and tail:
                                        pe.wait_ge(S["top2_ready"], t - 2)
                                    if k in (2, 3):
                                        pe.wait_ge(S["qkv_evacuated"], 24 * t + 4 * (k - 1))
                                    if k == 4 and not inter:
                                        pe.wait_ge(S["qkv_evacuated"], 24 * t + 12)
                                    if k == 4 and inter:
                                        pe.wait_ge(S["int_evacuated"], 8 * t - (6 if is_last(t) else 0))
                                for n in range(N):
                                    if half == 0 and (k == 5 or k == 0 and not (isinstance(t, int) and t == 0)):
                                        pe.wait_ge(S["qkv_evacuated"], 24 * t + (n + 17 if k else n - 3))
                                    for kt in range(2):
                                        for j, (a_, b_) in enumerate(((0, 0), (0, 1), (1, 0))):
                                            mm = pe.matmul(bank[first_bank + n][:, :], s_half[:, n, a_, kt, :],
                                                           w[:, b_, kt, :], start=half + kt + j == 0,
                                                           stop=half + kt == 2 and j == 2)
                                    if half == 1:
                                        mm.then_inc(S["qkv_done"], 1)
                                if half == 0:
                                    mm.then_inc(S["qkv_front"], 1)

                def interference(t, n):
                    b_r, b_i = bank[2 * (n % 2)][:, :], bank[2 * (n % 2) + 1][:, :]
                    if n == 0:
                        pe.wait_ge(S["a_ready"], 8 * t + 8)
                        pe.wait_ge(S["na_ready"], 4 * t + 4)
                    if n == 1 and is_last(i):
                        pe.wait_ge(S["qkv_evacuated"], 24 * NT)
                    if n >= 2:
                        pe.wait_ge(S["int_evacuated"], 8 * t + (2 * (n - 2) + 2))
                    rows_n = slice(n * P, (n + 1) * P)
                    w = next_unit()
                    product_of(b_r, lambda kt: a_t[:, 0, kt, rows_n], lambda kt: w[:, kt, :], None, True, False)
                    product_of(b_i, lambda kt: a_t[:, 1, kt, rows_n], lambda kt: w[:, kt, :], "int_done", True, False)
                    w = next_unit()
                    product_of(b_r, lambda kt: na_t[:, kt, rows_n], lambda kt: w[:, kt, :], None, False, True)
                    product_of(b_i, lambda kt: a_t[:, 0, kt, rows_n], lambda kt: w[:, kt, :], "int_done", False, True)

                def tail_stage(t, n):
                    if n == 0:
                        pe.wait_ge(S["sup_t_ready"], 3 * t + 1)
                        pe.wait_ge(S["tail"], TAIL_STEPS * t)
                        w = next_unit()
                        product_of(bank[4][:, :], lambda kt: sup_t[:, 0, kt, :], lambda kt: w[:, kt, :], None, True, False)
                        pe.wait_ge(S["sup_t_ready"], 3 * t + 2)
                        product_of(bank[5][:, :], lambda kt: sup_t[:, 1, kt, :], lambda kt: w[:, kt, :], "meas_done",
                                   True, False)
                        w = next_unit()
                        pe.wait_ge(S["sup_t_ready"], 3 * t + 3)
                        product_of(bank[4][:, :], lambda kt: sup_t[:, 2, kt, :], lambda kt: w[:, kt, :], None, False, True)
                        product_of(bank[5][:, :], lambda kt: sup_t[:, 0, kt, :], lambda kt: w[:, kt, :], "meas_done",
                                   False, True)
                    if n == 1:
                        pe.wait_ge(S["amp_ready"], t + 1)
                        transposes(bank[6], tb, "amp_transposed")
                        pe.wait_ge(S["amp_t_ready"], t + 1)
                        w = next_unit()
                        product_of(bank[4][:, :], lambda kt: x_t[:, kt, :], lambda kt: w[:, kt, :], "post_done")
                    if n == 2:
                        pe.wait_ge(S["z_t_ready"], t + 1)
                        w = next_unit()
                        product_of(bank[5][:, :], lambda kt: x_t[:, kt, :], lambda kt: w[:, kt, :], "topz_done")
                    if n == 3:
                        pe.wait_ge(S["h1_ready"], t + 1)
                        transposes(bank[6], tb, "h1_transposed")
                        pe.wait_ge(S["h1_t_ready"], t + 1)
                        next_unit()
                        slot = place(i, at[0] - 1)[0]
                        w2t = w2[:, slot, 0:DT * TOP2].rearrange("p (k c) -> p k c", k=DT)
                        product_of(bank[4][:, 0:TOP2], lambda kt: x_t[:, kt, :], lambda kt: w2t[:, kt, :], "top2_done")

                def z_transpose(t):
                    pe.wait_ge(S["z_ready"], t + 1)
                    transposes(bank[7], ta, "z_transposed")

                def out_transpose(t, parts):
                    if isinstance(t, int) and t == 0:
                        pe.wait_ge(S["ident_made"], 1)
                    pe.wait_ge(S["qkv_evacuated"], 24 * t + (40 if att else 24))
                    if tail and not closing(i):
                        pe.wait_ge(S["sup_t_ready"], 3 * t)
                    for j in range(4 * parts[0], 4 * parts[-1] + 4):
                        r, f = j // 4, j % 4
                        if f == 0:
                            pe.wait_ge(S["out_ready"], 2 * t + (r + 1))
                        if j >= 2:
                            pe.wait_ge(S["out_t_ready"], 8 * t + (j - 1))
                        for n in range(N):
                            ins = pe.transpose(bank[6 + j % 2][:, n * P:(n + 1) * P],
                                               out_of(t, n, r)[:, f * P:(f + 1) * P], ident[:, :])
                        ins.then_inc(S["out_transposed"], 1)

                def projection(t, parts):
                    if closing(i):
                        pe.wait_ge(S["int_evacuated"], 8 * t)
                    if att:
                        pe.wait_ge(S["qkv_evacuated"], 24 * t + 40)
                    for r in parts:
                        w = next_unit()
                        pe.wait_ge(S["out_t_ready"], 8 * t + (4 * r + 4))
                        for mt in range(DT):
                            j = 4 * r + mt
                            if j >= 4:
                                pe.wait_ge(S["a_ready"], 8 * t + (j - 3))
                            product_of(bank[j % 4][:, :], lambda kt: w[:, kt, mt * P:(mt + 1) * P],
                                       lambda kt: out_t_of(t, r)[:, kt, :], "o_done")

                def sup_transpose(t):
                    pe.wait_ge(S["sup_scaled"], 2 * t + 2)
                    pe.wait_ge(S["qkv_evacuated"], 24 * i + 16 if att else 24 * NT)
                    transposes(bank[6], sup[:, 0, :], None)
                    transposes(bank[7], sup[:, 1, :], "sup_transposed")

                if closing(i):
                    out_transpose(i - 1, [0, 1])
                    projection(i - 1, [0, 1])
                    for n in range(N):
                        interference(i - 1, n)
                    sup_transpose(i - 2)
                    for n in range(N):
                        if n == 2:
                            z_transpose(i - 2)
                        tail_stage(i - 2, n)
                    return
                if att:
                    qkv(i, [[0, 1], [2, 3]])
                if tail:
                    sup_transpose(i - 2)
                if tail:
                    tail_stage(i - 2, 0)
                if inter:
                    for part in range(2):
                        out_transpose(i - 1, [part])
                        projection(i - 1, [part])
                    interference(i - 1, 0)
                if is_last(i):
                    qkv(i, [[4], [5]])
                if tail:
                    tail_stage(i - 2, 1)
                if inter:
                    interference(i - 1, 1)
                    interference(i - 1, 2)
                if tail:
                    z_transpose(i - 2)
                if inter:
                    interference(i - 1, N - 1)
                if tail:
                    tail_stage(i - 2, 2)
                if att and not is_last(i):
                    qkv(i, [[4]])
                if tail:
                    tail_stage(i - 2, 3)
                if att and not is_last(i):
                    qkv(i, [[5]])
            turns(pe, body)


def kernel(**inputs):
    import numpy as np
    import concourse.bacc as bacc
    from concourse.bass_utils import run_bass_kernel_spmd

    a = {k: np.asarray(v) for k, v in inputs.items()}

    def rec(name):
        return a["L0_rec_" + name]

    def stationary_units(w):
        o, n = w.shape
        return np.ascontiguousarray(w.reshape(o // P, P, n // P, P).transpose(0, 3, 2, 1)).reshape(o // P, P, n)

    def moving_unit(w):
        n, o = w.shape
        u = np.ascontiguousarray(w.reshape(n // P, P, o).transpose(1, 0, 2)).reshape(P, n // P * o)
        return u if u.shape[1] == UNIT else np.pad(u, ((0, 0), (0, UNIT - u.shape[1])))

    units = [rec(n).T for n in ("Wq_r", "Wq_i", "Wk_r", "Wk_i", "Wv_r", "Wv_i", "Wo_r", "Wo_i")]
    for n in range(N):
        units += [rec("int_Wr")[n].T, rec("int_Wi")[n].T]
    units += [rec("meas_Mr").T, rec("meas_Mi").T, rec("post_W").T, a["W_top1"][0:D], a["W_top2"]]
    rows = np.concatenate([rec(n) for n in ("bq_r", "bq_i", "bk_r", "bk_i", "post_b", "post_g", "post_be")]
                          + [a["b_top1"], a["b_top2"], a["W_top3"][:, 0]])
    cols = np.stack([rec(n) for n in ("bv_r", "bv_i", "bo_r", "bo_i")])
    vecs = np.stack([rec(e + k) for e in ("er_", "ei_") for k in ("b1", "g1", "be1", "b2")])
    arrays = {
        "x": np.ascontiguousarray(a["r_x"].reshape(2, HALF, KT, P).transpose(0, 3, 2, 1)),
        "w1r": stationary_units(rec("er_W1")), "w1i": stationary_units(rec("ei_W1")),
        "w2r": stationary_units(rec("er_W2")), "w2i": stationary_units(rec("ei_W2")),
        "wtx": np.stack([moving_unit(a["W_top1"][D + j * D:D + (j + 1) * D]) for j in range(4)]),
        "vecs": np.ascontiguousarray(vecs.reshape(8, KT, P).transpose(2, 0, 1)),
        "ws2": np.stack([moving_unit(w) for w in units]),
        "rows": np.ascontiguousarray(np.broadcast_to(rows, (P, rows.size))),
        "cols": np.ascontiguousarray(cols.reshape(4, DT, P).transpose(2, 0, 1)),
        "ids": np.ascontiguousarray(a["ids"].reshape(NT, P, N).transpose(1, 0, 2)),
        **{f"tbl{f}": np.ascontiguousarray(a[f"tbl_{f}"]) for f in range(N)},
    }
    nc = bacc.Bacc("TRN2", target_bir_lowering=False, num_devices=1)
    dram = {k: nc.dram_tensor(k, v.shape, mybir.dt.from_np(v.dtype), kind="ExternalInput").ap()
            for k, v in arrays.items()}
    dram["s"] = nc.dram_tensor("s", (NT, 2, N, 2, P, 2 * 2 * P), F32, kind="Internal").ap()
    dram["wqkv"] = nc.dram_tensor("wqkv", (QKV_UNITS, 2, P, UNIT), F32, kind="Internal").ap()
    dram["t1x"] = nc.dram_tensor("t1x", (NT, P, TOP1), F32, kind="Internal").ap()
    dram["out"] = nc.dram_tensor("out", (P, NT), F32, kind="ExternalOutput").ap()
    with ExitStack() as ctx:
        early_loaded = {k: ctx.enter_context(nc.semaphore("early_" + k)) for k in ("rows", "cols", "ids")}
        early_loaded["w2"] = [ctx.enter_context(nc.semaphore(f"w2_loaded{i}")) for i in range(RING)]
        early_loaded["s"] = [ctx.enter_context(nc.semaphore(f"s_loaded{i}")) for i in range(2)]
        with ExitStack() as place:
            early = early_buffers(nc, place, "")
        encode(nc, dram, early, early_loaded)
        mix(nc, dram, early, early_loaded)
    got = run_bass_kernel_spmd(nc, [arrays], core_ids=[0])
    return np.ascontiguousarray(got.results[0]["out"].T).reshape(BATCH, 1)
```
